# Optimizing a Trainium2 kernel written in Bass

```python
import numpy as np
import jax
import jax.numpy as jnp

def _softmax(x, axis=-1):
    return jax.nn.softmax(x, axis=axis)
def _gelu(x):
    return jax.nn.gelu(x, approximate=True)
def _silu(x):
    return jax.nn.silu(x)
def _sigmoid(x):
    return jax.nn.sigmoid(x)
def _layernorm(x, axis=-1, eps=1e-5):
    m = jnp.mean(x, axis=axis, keepdims=True)
    v = jnp.var(x, axis=axis, keepdims=True)
    return (x - m) / jnp.sqrt(v + eps)
def _scatter_add(tgt, idx, src, axis=0):
    return tgt.at[idx].add(src)
def _segment_sum(src, seg, n):
    return jax.ops.segment_sum(src, seg, n)

kernel_name = 'mk_conv_attn_hybrid_d2_conv_nhwc128_e3ae3c'

def setup_inputs(seed: int = 0):
    np.random.seed(seed)
    _w = jnp.asarray
    def _rec_inputs():
        import jax
        import jax.numpy as jnp
        _gk = jax.random.key(seed)
        x = -0.0005207 + 1.001 * jax.random.normal(jax.random.fold_in(_gk, 1), (4, 64, 64, 128), jnp.float32)
        return x
    x = _rec_inputs()
    def _L0_conv_setup():
        import jax, jax.numpy as jnp
        import numpy as np
        B, H, W, C = (4, 64, 64, 128)
        G = 4
        HC = C // G
        K = 3
        K2 = K * K
        PAD = K // 2
        SCALE = HC ** (-0.5)

        def conv2d(x, w, padding=1, dilation=1, groups=1):
            return jax.lax.conv_general_dilated(x, w, (1, 1), [(padding, padding), (padding, padding)], rhs_dilation=(dilation, dilation), dimension_numbers=('NCHW', 'OIHW', 'NCHW'), feature_group_count=groups)

        def pconv(x, w):
            c4 = w.shape[0]
            return jnp.concatenate([conv2d(x[:, :c4], w, padding=1), x[:, c4:]], axis=1)

        def conv1x1(x, w, b):
            return jnp.einsum('bchw,oc->bohw', x, w) + b[None, :, None, None]

        def deform_sample(img, offset, mask, dilation, pad):
            b, cg, h, w = img.shape
            ky, kx = jnp.meshgrid(jnp.arange(K), jnp.arange(K), indexing='ij')
            base_y = (ky.reshape(-1) * dilation - pad).astype(img.dtype)
            base_x = (kx.reshape(-1) * dilation - pad).astype(img.dtype)
            off = offset.reshape(b, K2, 2, h, w)
            py = jnp.arange(h, dtype=img.dtype)[None, None, :, None] + base_y[None, :, None, None] + off[:, :, 0]
            px = jnp.arange(w, dtype=img.dtype)[None, None, None, :] + base_x[None, :, None, None] + off[:, :, 1]
            y0 = jnp.floor(py)
            x0 = jnp.floor(px)
            wy = py - y0
            wx = px - x0
            flat = img.reshape(b, cg, h * w)

            def gather(iy, ix):
                valid = ((iy >= 0) & (iy < h) & (ix >= 0) & (ix < w)).astype(img.dtype)
                idx = (jnp.clip(iy, 0, h - 1) * w + jnp.clip(ix, 0, w - 1)).astype(jnp.int32)
                g = jax.vmap(lambda f, i: jnp.take(f, i, axis=1))(flat, idx.reshape(b, -1))
                return g.reshape(b, cg, K2, h, w) * valid[:, None]
            wy_ = wy[:, None]
            wx_ = wx[:, None]
            out = gather(y0, x0) * (1 - wy_) * (1 - wx_) + gather(y0, x0 + 1) * (1 - wy_) * wx_ + gather(y0 + 1, x0) * wy_ * (1 - wx_) + gather(y0 + 1, x0 + 1) * wy_ * wx_
            return out * mask[:, None]
        key = jax.random.key(seed)
        ks = jax.random.split(key, 14)
        d = {}
        d['x'] = jax.random.normal(ks[0], (B, H, W, C), jnp.float32)
        d['w_qkv'] = jax.random.normal(ks[1], (C, 3 * C), jnp.float32) * C ** (-0.5)
        d['b_qkv'] = jax.random.normal(ks[2], (3 * C,), jnp.float32) * 0.02
        d['w_dw'] = jax.random.normal(ks[3], (3 * C, 1, 3, 3), jnp.float32) * 0.2
        d['b_dw'] = jax.random.normal(ks[4], (3 * C,), jnp.float32) * 0.02
        d['pconv_off_w'] = jax.random.normal(ks[5], (G, C // 4, C // 4, 3, 3), jnp.float32) * 0.05
        d['w_off'] = jax.random.normal(ks[6], (G, 2 * K2, C), jnp.float32) * 0.01
        d['b_off'] = jax.random.normal(ks[7], (G, 2 * K2), jnp.float32) * 0.01
        d['pconv_mask_w'] = jax.random.normal(ks[8], (C // 4, C // 4, 3, 3), jnp.float32) * 0.05
        d['w_mask'] = jax.random.normal(ks[9], (K2, C), jnp.float32) * 0.01
        d['b_mask'] = jax.random.normal(ks[10], (K2,), jnp.float32) * 0.01
        d['w_proj'] = jax.random.normal(ks[11], (C, C), jnp.float32) * C ** (-0.5)
        d['b_proj'] = jax.random.normal(ks[12], (C,), jnp.float32) * 0.02
        return d
    _L0_conv_all = _L0_conv_setup()
    _L0_conv_in = {k: v for k, v in _L0_conv_all.items() if k in ('w_qkv', 'b_qkv', 'w_dw', 'b_dw', 'pconv_off_w', 'w_off', 'b_off', 'pconv_mask_w', 'w_mask', 'b_mask', 'w_proj', 'b_proj', )}
    del _L0_conv_all

    def _L1_attn_setup():
        import jax, jax.numpy as jnp
        import numpy as np
        B, T, D = (4, 2048, 128)
        key = jax.random.key(seed)
        k1, k2, k3 = jax.random.split(key, 3)
        x = jax.random.normal(k1, (B, T, D), dtype=jnp.float32)
        lim = 1.0 / np.sqrt(D)
        W = jax.random.uniform(k2, (3 * D, D), dtype=jnp.float32, minval=-lim, maxval=lim)
        b = jax.random.uniform(k3, (3 * D,), dtype=jnp.float32, minval=-lim, maxval=lim)
        return {'x': x, 'W': W, 'b': b}
    _L1_attn_all = _L1_attn_setup()
    _L1_attn_in = {k: v for k, v in _L1_attn_all.items() if k in ('W', 'b', )}
    del _L1_attn_all

    def _L1_ffn_setup():
        import jax, jax.numpy as jnp
        import numpy as np
        B, N, D, C, E, K = (8, 8192, 128, 128, 8, 2)
        key = jax.random.key(seed)
        k0, k1, k2 = jax.random.split(key, 3)
        x = jax.random.normal(k0, (B, N, D), dtype=jnp.float32)
        router_w = jax.random.normal(k1, (D, E), dtype=jnp.float32) * 0.05
        router_b = jnp.zeros((E,), dtype=jnp.float32)
        expert_w = jax.random.normal(k2, (E, D, C), dtype=jnp.float32) * (1.0 / np.sqrt(D))
        expert_b = jnp.zeros((E, C), dtype=jnp.float32)
        return {'x': x, 'router_w': router_w, 'router_b': router_b, 'expert_w': expert_w, 'expert_b': expert_b}
    _L1_ffn_all = _L1_ffn_setup()
    _L1_ffn_in = {k: v for k, v in _L1_ffn_all.items() if k in ('router_w', 'router_b', 'expert_w', 'expert_b', )}
    del _L1_ffn_all

    return {
        "x": x,
        "L0_conv_w_qkv": _L0_conv_in["w_qkv"],
        "L0_conv_b_qkv": _L0_conv_in["b_qkv"],
        "L0_conv_w_dw": _L0_conv_in["w_dw"],
        "L0_conv_b_dw": _L0_conv_in["b_dw"],
        "L0_conv_pconv_off_w": _L0_conv_in["pconv_off_w"],
        "L0_conv_w_off": _L0_conv_in["w_off"],
        "L0_conv_b_off": _L0_conv_in["b_off"],
        "L0_conv_pconv_mask_w": _L0_conv_in["pconv_mask_w"],
        "L0_conv_w_mask": _L0_conv_in["w_mask"],
        "L0_conv_b_mask": _L0_conv_in["b_mask"],
        "L0_conv_w_proj": _L0_conv_in["w_proj"],
        "L0_conv_b_proj": _L0_conv_in["b_proj"],
        "L1_attn_W": _L1_attn_in["W"],
        "L1_attn_b": _L1_attn_in["b"],
        "L1_ffn_router_w": _L1_ffn_in["router_w"],
        "L1_ffn_router_b": _L1_ffn_in["router_b"],
        "L1_ffn_expert_w": _L1_ffn_in["expert_w"],
        "L1_ffn_expert_b": _L1_ffn_in["expert_b"],
    }

def reference(x, L0_conv_w_qkv, L0_conv_b_qkv, L0_conv_w_dw, L0_conv_b_dw, L0_conv_pconv_off_w, L0_conv_w_off, L0_conv_b_off, L0_conv_pconv_mask_w, L0_conv_w_mask, L0_conv_b_mask, L0_conv_w_proj, L0_conv_b_proj, L1_attn_W, L1_attn_b, L1_ffn_router_w, L1_ffn_router_b, L1_ffn_expert_w, L1_ffn_expert_b):
    import jax
    import jax.numpy as jnp
    def _L0_conv_ref(x, w_qkv, b_qkv, w_dw, b_dw, pconv_off_w, w_off, b_off, pconv_mask_w, w_mask, b_mask, w_proj, b_proj):
        import jax, jax.numpy as jnp
        import numpy as np
        B, H, W, C = (4, 64, 64, 128)
        G = 4
        HC = C // G
        K = 3
        K2 = K * K
        PAD = K // 2
        SCALE = HC ** (-0.5)

        def conv2d(x, w, padding=1, dilation=1, groups=1):
            return jax.lax.conv_general_dilated(x, w, (1, 1), [(padding, padding), (padding, padding)], rhs_dilation=(dilation, dilation), dimension_numbers=('NCHW', 'OIHW', 'NCHW'), feature_group_count=groups)

        def pconv(x, w):
            c4 = w.shape[0]
            return jnp.concatenate([conv2d(x[:, :c4], w, padding=1), x[:, c4:]], axis=1)

        def conv1x1(x, w, b):
            return jnp.einsum('bchw,oc->bohw', x, w) + b[None, :, None, None]

        def deform_sample(img, offset, mask, dilation, pad):
            b, cg, h, w = img.shape
            ky, kx = jnp.meshgrid(jnp.arange(K), jnp.arange(K), indexing='ij')
            base_y = (ky.reshape(-1) * dilation - pad).astype(img.dtype)
            base_x = (kx.reshape(-1) * dilation - pad).astype(img.dtype)
            off = offset.reshape(b, K2, 2, h, w)
            py = jnp.arange(h, dtype=img.dtype)[None, None, :, None] + base_y[None, :, None, None] + off[:, :, 0]
            px = jnp.arange(w, dtype=img.dtype)[None, None, None, :] + base_x[None, :, None, None] + off[:, :, 1]
            y0 = jnp.floor(py)
            x0 = jnp.floor(px)
            wy = py - y0
            wx = px - x0
            flat = img.reshape(b, cg, h * w)

            def gather(iy, ix):
                valid = ((iy >= 0) & (iy < h) & (ix >= 0) & (ix < w)).astype(img.dtype)
                idx = (jnp.clip(iy, 0, h - 1) * w + jnp.clip(ix, 0, w - 1)).astype(jnp.int32)
                g = jax.vmap(lambda f, i: jnp.take(f, i, axis=1))(flat, idx.reshape(b, -1))
                return g.reshape(b, cg, K2, h, w) * valid[:, None]
            wy_ = wy[:, None]
            wx_ = wx[:, None]
            out = gather(y0, x0) * (1 - wy_) * (1 - wx_) + gather(y0, x0 + 1) * (1 - wy_) * wx_ + gather(y0 + 1, x0) * wy_ * (1 - wx_) + gather(y0 + 1, x0 + 1) * wy_ * wx_
            return out * mask[:, None]
        b, h, w, c = x.shape
        n = h * w
        qkv = x @ w_qkv + b_qkv
        qkv = conv2d(qkv.transpose(0, 3, 1, 2), w_dw, padding=1, groups=3 * c) + b_dw[None, :, None, None]
        qkv = qkv.transpose(0, 2, 3, 1)
        q = qkv[..., :c]
        kv = qkv[..., c:].reshape(b, h, w, 2, G, HC).transpose(3, 0, 4, 5, 1, 2)
        q_img = q.transpose(0, 3, 1, 2)
        mask = jax.nn.sigmoid(conv1x1(pconv(q_img, pconv_mask_w), w_mask, b_mask))
        k_list, v_list = ([], [])
        for i in range(G):
            off = conv1x1(pconv(q_img, pconv_off_w[i]), w_off[i], b_off[i])
            dil = 2 * i + 1
            k_list.append(deform_sample(kv[0, :, i], off, mask, dil, dil * PAD))
            v_list.append(deform_sample(kv[1, :, i], off, mask, dil, dil * PAD))
        ks_ = jnp.stack(k_list, 1).reshape(b, G, HC, K2, n)
        vs_ = jnp.stack(v_list, 1).reshape(b, G, HC, K2, n)
        qf = (q.reshape(b, n, G, HC) * SCALE).transpose(0, 2, 1, 3)
        attn = jax.nn.softmax(jnp.einsum('bgnc,bgckn->bgnk', qf, ks_), axis=-1)
        out = jnp.einsum('bgnk,bgckn->bgnc', attn, vs_)
        out = out.transpose(0, 2, 1, 3).reshape(b, h, w, c)
        return out @ w_proj + b_proj

    def _L1_attn_ref(x, W, b):
        import jax, jax.numpy as jnp
        import numpy as np
        B, T, D = (4, 2048, 128)
        Bx, Tx, Dx = x.shape
        qkv = (x @ W.T + b).reshape(Bx, Tx, 3, Dx)
        q, k, v = (qkv[:, :, 0], qkv[:, :, 1], qkv[:, :, 2])
        q = jax.nn.elu(q) + 1.0
        k = jax.nn.elu(k) + 1.0
        kv = jnp.einsum('bti,btj->btij', k, v)
        kv_cum = jnp.cumsum(kv, axis=1)
        k_cum = jnp.cumsum(k, axis=1)
        num = jnp.einsum('bti,btij->btj', q, kv_cum)
        den = jnp.einsum('bti,bti->bt', q, k_cum)[..., None] + 1e-06
        return num / den

    def _L1_ffn_ref(x, router_w, router_b, expert_w, expert_b):
        import jax, jax.numpy as jnp
        import numpy as np
        B, N, D, C, E, K = (8, 8192, 128, 128, 8, 2)
        router_probs = jax.nn.softmax(x @ router_w + router_b, axis=-1)
        top_p, top_i = jax.lax.top_k(router_probs, K)
        top_p = top_p / jnp.sum(top_p, axis=-1, keepdims=True)
        expert_out = jnp.einsum('bnd,edc->bnec', x, expert_w) + expert_b
        gathered = jnp.take_along_axis(expert_out, top_i[..., None], axis=2)
        return jnp.einsum('bnk,bnkc->bnc', top_p, gathered)

    def _gn(v, G=32, eps=1e-5):
        B_, H_, W_, C_ = v.shape
        g = v.reshape(B_, H_, W_, G, C_ // G)
        m = jnp.mean(g, axis=(1, 2, 4), keepdims=True)
        s = jnp.var(g, axis=(1, 2, 4), keepdims=True)
        return ((g - m) / jnp.sqrt(s + eps)).reshape(v.shape)

    def _ln_c(v, eps=1e-6):
        m = jnp.mean(v, axis=-1, keepdims=True)
        s = jnp.var(v, axis=-1, keepdims=True)
        return (v - m) / jnp.sqrt(s + eps)

    def _ln_t(v, eps=1e-5):
        m = jnp.mean(v, axis=-1, keepdims=True)
        s = jnp.var(v, axis=-1, keepdims=True)
        return (v - m) / jnp.sqrt(s + eps)

    def _to_tokens(v):
        B_, H_, W_, C_ = v.shape
        return v.reshape(B_, H_ * W_, C_)
    def _from_tokens(t, like):
        return t.reshape(like.shape)

    x = x + _L0_conv_ref(_gn(x), L0_conv_w_qkv, L0_conv_b_qkv, L0_conv_w_dw, L0_conv_b_dw, L0_conv_pconv_off_w, L0_conv_w_off, L0_conv_b_off, L0_conv_pconv_mask_w, L0_conv_w_mask, L0_conv_b_mask, L0_conv_w_proj, L0_conv_b_proj)
    t = _to_tokens(x)
    t = t + _L1_attn_ref(_ln_t(t), L1_attn_W, L1_attn_b)
    t = t + _L1_ffn_ref(_ln_t(t), L1_ffn_router_w, L1_ffn_router_b, L1_ffn_expert_w, L1_ffn_expert_b)
    x = _from_tokens(t, x)
    return x


_drawn_inputs = setup_inputs


def setup_inputs(seed=0):
    import zlib

    import numpy as np

    out = dict(_drawn_inputs(seed))
    spreads = {'L1_ffn_router_b': (0.0, 0.1), 'L1_ffn_expert_b': (0.0, 0.1)}
    factors = {'L0_conv_b_off': 3.062, 'L0_conv_pconv_mask_w': 3.964}
    for name, (base, spread) in spreads.items():
        noise = np.random.default_rng([zlib.crc32(name.encode()), seed]).standard_normal(out[name].shape)
        drawn = base * np.exp(spread * noise) if base else spread * noise
        out[name] = jnp.asarray(drawn.astype(out[name].dtype))
    for name, factor in factors.items():
        out[name] = (out[name] * factor).astype(out[name].dtype)
    return out
```

```python
import concourse.bass as bass
from concourse import mybir
from contextlib import ExitStack

FP32 = mybir.dt.float32
INT32 = mybir.dt.int32
ALU = mybir.AluOpType
ACT = mybir.ActivationFunctionType
AX = mybir.AxisListType

B, H, W, C = 4, 64, 64, 128
N = H * W
G, HC, TAPS = 4, 32, 9
E = 8
SCALE = HC ** -0.5
TILE = 128
TILES = N // TILE

ROWS, PCOLS = 8, 4
BANDS = H // ROWS
PATCHES = W // PCOLS
PIX = ROWS * PCOLS
WR, WC = ROWS + 2, PCOLS + 2
WIN = WR * WC
KEYS = TAPS * WIN // 5
BPX = ROWS * W

RP = W + 2
RAW = (H + 2) * RP
FAR = 8
WP = W + FAR
WIDE = (H + 2 * FAR) * WP + 16
BAND = WR * WP


CHAIN_A, CHAIN_B, CHAIN_C = 73, 30, 68


ONE_PIXEL = 1.0


def view(ap, dims):
    return bass.AP(tensor=ap.tensor, offset=ap.offset, ap=[ap.ap[0]] + dims)


class Chain:

    def __init__(self, eng, sem, turn, per_turn):
        self.eng, self.sem, self.base, self.per_turn, self.n = eng, sem, turn * per_turn, per_turn, 0

    def did(self, ins):
        ins.then_inc(self.sem, 1)
        self.n += 1
        return self.n

    def after(self, n):
        self.eng.wait_ge(self.sem, self.base + n)

    def link(self, ins):
        self.after(self.did(ins))

    def close(self):
        assert self.n == self.per_turn, (self.n, self.per_turn)


def hybrid_kernel(nc, x, w_qkv, b_qkv, w_dw, b_dw, wp_off, w_off, b_off, wp_mask, w_mask, b_mask, w_proj, b_proj,
                  wa, ba, wr, br, we, be, c_ident, c_gavg, c_causal, c_grid, c_before, c_place, table, offs, out):
    ctx = ExitStack()
    with ctx:
        def sb(name, shape, dt=FP32):
            return ctx.enter_context(nc.sbuf_tensor(name, shape, dt))

        def sem(name):
            return ctx.enter_context(nc.semaphore(name))

        ident = sb("ident", [128, 128])
        gavg = sb("gavg", [128, 128])
        causal = sb("causal", [128, 128])
        grid = sb("grid", [128, WC + WR])
        before = sb("before", [128, E * E])
        place = sb("place", [128, 2 * TAPS + 1])
        wq_sb = sb("wq_sb", [128, 3 * C])
        wn_sb = sb("wn_sb", [128, 3 * C])
        bq_sb = sb("bq_sb", [128, 3])
        bn_sb = sb("bn_sb", [128, 3])
        dw_sb = sb("dw_sb", [128, 3, TAPS])
        db_sb = sb("db_sb", [128, 3])
        conv_w = sb("conv_w", [96, 3, 128])
        pass_w = sb("pass_w", [128, 128])
        ob_sb = sb("ob_sb", [128, 1])
        wproj_sb = sb("wproj_sb", [128, C])
        rows = sb("rows", [128, 2 * C + E])
        wa_sb = sb("wa_sb", [128, 3 * C])
        ba_sb = sb("ba_sb", [128, 2])
        wr_sb = sb("wr_sb", [128, E])
        we_sb = sb("we_sb", [128, E * C])
        be_sb = sb("be_sb", [E, C])
        xtok = sb("xtok", [128, TILES * C])
        xch = sb("xch", [128, N])
        qpad = sb("qpad", [128, RAW])
        kwide = sb("kwide", [128, WIDE])
        vwide = sb("vwide", [128, WIDE])
        kband = sb("kband", [128, TAPS * BAND])
        vwin = sb("vwin", [128, (W + 2) * TAPS * WR])
        vstage = sb("vstage", [128, 3 * BAND])
        raw = [kband[:, 0:RAW], vwin[:, 0:RAW]]
        qstack = sb("qstack", [96, WR * RP])
        offc = sb("offc", [128, BPX])
        offt = sb("offt", [128, BPX])
        HN = PATCHES * TAPS
        hat = xtok[:, 0:HN * (WC + WR)]
        hx, hy = hat[:, 0:HN * WC], hat[:, HN * WC:]
        rsum = xtok[:, HN * 16:HN * 26]
        qbd = sb("qbd", [128, PATCHES * 128])
        gx = sb("gx", [128, HN * WC])
        prod = sb("prod", [128, 2, TAPS * WIN])
        attbuf = sb("attbuf", [128, TAPS * 128])
        att = attbuf[:, 0:2 * TAPS * WIN].rearrange("p (a n) -> p a n", a=2)
        diag = attbuf[:, :].rearrange("p (t n) -> p t n", t=TAPS)
        keysT = sb("keysT", [128, 2, 10 * 128])
        half = sb("half", [128, 4])
        msk = sb("msk", [128, HN])
        lg = sb("lg", [128, HN])
        small = sb("small", [128, 3 * PATCHES])
        offmax = sb("offmax", [128, 1 + BANDS])
        stats = sb("stats", [128, 8, 6])
        mom = sb("mom", [128, 12])
        cbuf = [kwide[:, 0:5760], vwide[:, 0:5760], qpad[:, 0:4352]]
        x1, ln, lnT = cbuf[0][:, 0:512], cbuf[0][:, 512:1024], cbuf[0][:, 1024:1536]
        qk_raw, qk_exp, qk = cbuf[0][:, 1536:2560], cbuf[0][:, 2560:3584], cbuf[0][:, 3584:4608]
        ktok, pmask = cbuf[0][:, 4608:5120], cbuf[0][:, 5120:5632]
        vone, state = cbuf[1][:, 0:516], cbuf[1][:, 516:516 + 645]
        t1, acc, accb = cbuf[1][:, 1280:1792], cbuf[1][:, 1792:2304], cbuf[1][:, 2304:2816]
        ao = cbuf[1][:, 2816:3328]
        wT = cbuf[1][0:E, 3328:3840]
        lstat, lmom, lrs = cbuf[1][:, 3840:3864], cbuf[1][:, 3864:3872], cbuf[1][:, 3872:3880]
        den = cbuf[1][:, 3880:3884]
        rl, re_, rsel, rw = (cbuf[1][:, 3900 + 32 * i:3932 + 32 * i] for i in range(4))
        rsm = cbuf[1][:, 4032:4040]
        gt, eq = cbuf[1][:, 4096:4352], cbuf[1][:, 4352:4608]

        f_corner, f_part, f_sample = kband[:, 0:2304], kband[:, 2304:4608], kband[:, 4608:5184]
        f_off, f_q, f_qT = vstage[:, 0:512], vstage[:, 512:544], vstage[:, 544:576]
        f_in, f_out = vstage[:, 576:704], vstage[:, 704:832]
        f_o, f_oT = vstage[:, 832:864], vstage[:, 864:896]
        f_pos, f_low, f_frac, f_tmp = (vstage[:, 900 + 18 * n:918 + 18 * n] for n in range(4))
        f_edge, f_wt = vstage[:, 1000:1036], vstage[:, 1040:1076]
        f_int, f_idx = vstage[:, 1080:1098].bitcast(INT32), vstage[:, 1100:1136].bitcast(INT32)
        f_flat, f_cw = vstage[:, 1140:1176], vstage[:, 1180:1216]
        f_mask, f_lg, f_s = vstage[:, 1220:1229], vstage[:, 1230:1239], vstage[:, 1240:1244]
        f_at = vstage[:, 1250:1252]
        flag = sb("flag", [1, 2], INT32)

        P = [ctx.enter_context(nc.psum_tensor(f"P{i}", [128, 512], FP32)) for i in range(8)]

        s_hold = sem("s_hold")
        w_in = sem("w_in")
        s_zero, s_setup_pe, s_setup_cp, s_ready = sem("s_zero"), sem("s_setup_pe"), sem("s_setup_cp"), sem("s_ready")
        done_a, done_b, done_c = sem("done_a"), sem("done_b"), sem("done_c")
        x_in = [sem(f"x_in{j}") for j in range(4)]
        xT_ready, xT_copied, xT_stated = sem("xT_ready"), sem("xT_copied"), sem("xT_stated")
        moments, groups, norm, wnorm, biasmm, bias_ok = (sem(n) for n in
            ("moments", "groups", "norm", "wnorm", "biasmm", "bias_ok"))
        raw_zero, qkv_ready, raw_ready, q_conv = sem("raw_zero"), sem("qkv_ready"), sem("raw_ready"), sem("q_conv")
        vconv_ready, v_ready = sem("vconv_ready"), sem("v_ready")
        diag_ready = sem("diag_ready")
        gvar_ready, gstd_ready, var_ready, std_ready = sem("gvar_ready"), sem("gstd_ready"), sem("var_ready"), sem("std_ready")
        dve_a, dve_b, dve_c = sem("dve_a"), sem("dve_b"), sem("dve_c")
        q_in, k_in, v_in = sem("q_in"), sem("k_in"), sem("v_in")
        v_packed = sem("v_packed")
        off_mm, offc_ready, offt_ready, diff_ready, hat_ready = (sem(n) for n in
            ("off_mm", "offc_ready", "offt_ready", "diff_ready", "hat_ready"))
        absd, mexp, mask_ready, qbd_ready = sem("absd"), sem("mexp"), sem("mask_ready"), sem("qbd_ready")
        s_mm, s_used = sem("s_mm"), sem("s_used")
        lg_ready, p_ready, gx_ready, a_dve, a_pool = (sem(n) for n in ("lg_ready", "p_ready", "gx_ready", "a_dve", "a_pool"))
        t_ready, t_copied, o_ready, o_copied = sem("t_ready"), sem("t_copied"), sem("o_ready"), sem("o_copied")
        xr_in, ao_ready, st_out = sem("xr_in"), sem("ao_ready"), sem("st_out")
        peak_ok = sem("peak_ok")
        off_kept, peak_ready, peak_row, flag_ready, done_f = (sem(n) for n in
            ("off_kept", "peak_ready", "peak_row", "flag_ready", "done_f"))
        (f_chain, f_turned, f_stored, f_table, f_off_in, f_mexp, f_masked, f_ready, f_gather, f_gathered, f_lgr, f_exp,
         f_used) = (sem(n) for n in ("f_chain f_turned f_stored f_table f_off_in f_mexp f_masked f_ready f_gather "
                                     "f_gathered f_lgr f_exp f_used").split())
        turn_done = sem("turn_done")
        (proj_ready, ln_ready, lnT_ready, lnT_copied, qkv_c, qk_biased, clip_ready, exp_ready, qk_ready, v_c, kt_ready,
         kt_copied, st_ready, pm_ready, delta_ready, state_ready, num_ready, ln2_ready, ln2T_ready, ln2T_copied,
         route_ready, logit_ready, rexp_ready, gate_ready, gateT_ready, gateT_copied, bias_c, ex_ready, ex_used) = (
            sem(n) for n in ("proj_ready ln_ready lnT_ready lnT_copied qkv_c qk_biased clip_ready exp_ready qk_ready "
                             "v_c kt_ready kt_copied st_ready pm_ready delta_ready state_ready num_ready ln2_ready "
                             "ln2T_ready ln2T_copied route_ready logit_ready rexp_ready gate_ready gateT_ready "
                             "gateT_copied bias_c ex_ready ex_used").split())

        block = ctx.enter_context(nc.Block())

        def hold(eng):
            eng.sem_inc(s_hold, 1)

        x_tok = x.rearrange("b h w c -> (b h w) c")
        out_tok = out.rearrange("b h w c -> (b h w) c")
        wide_at = lambda y, xx: (y + FAR) * WP + xx + FAR

        loads = [
            (ident[:, :], c_ident), (gavg[:, :], c_gavg), (causal[:, :], c_causal), (grid[:, :], c_grid),
            (before[:, :], c_before), (place[:, :], c_place),
            (wq_sb[:, :], w_qkv), (bq_sb[:, :], b_qkv.rearrange("(c p) -> p c", p=128)),
            (dw_sb[:, :, :], w_dw.rearrange("(c p) i a b -> p c (i a b)", p=128)),
            (db_sb[:, :], b_dw.rearrange("(c p) -> p c", p=128)),
            (wproj_sb[:, :], w_proj), (ba_sb[:, :], ba[0:2 * C].rearrange("(c p) -> p c", p=128)),
            (wr_sb[:, :], wr), (we_sb[:, :].rearrange("p (e c) -> p e c", e=E), we.rearrange("e d c -> d e c")),
            (be_sb[:, :], be),
        ]
        s_wpo = kband[0:32, 0:G * 32 * TAPS].rearrange("o (g i t) -> o g i t", g=G, t=TAPS)
        s_wpm = kband[0:32, 1152:1152 + 288].rearrange("o (i t) -> o i t", t=TAPS)
        s_w1 = kband[:, 1536:1664]
        s_wa = kband[:, 1664:2048].rearrange("p (c i) -> p c i", c=3)
        s_row = kband[0:1, 2048:2048 + 2 * C + E]
        s_one = kband[0:1, 2432:2560]
        s_w1T = kband[:, 2560:2688]
        loads += [(s_wpo, wp_off.rearrange("g o i a b -> o g i (a b)")),
                  (s_wpm, wp_mask.rearrange("o i a b -> o i (a b)")),
                  (s_wa, wa.rearrange("(c p) i -> p c i", p=128)),
                  (s_row[:, 0:C], b_proj.rearrange("(a n) -> a n", a=1)),
                  (s_row[:, C:2 * C], ba[2 * C:3 * C].rearrange("(a n) -> a n", a=1)),
                  (s_row[:, 2 * C:], br.rearrange("(a n) -> a n", a=1))]
        late = []
        for g in range(G):
            late += [(s_w1[32 * g:32 * g + 18, :], w_off[g]), (s_w1[32 * g + 18:32 * g + 27, :], w_mask),
                     (ob_sb[32 * g:32 * g + 18, :], b_off[g].rearrange("(n a) -> n a", a=1)),
                     (ob_sb[32 * g + 18:32 * g + 27, :], b_mask.rearrange("(n a) -> n a", a=1))]
        BAND_IN = 16 * 3 * G
        ALL_IN = 16 * (len(loads) + len(late))

        def weigh(eng, s):
            return eng.tensor_tensor(
                view(att[:, s % 2, 0:1], [[TAPS * WR, WC], [WR, TAPS], [1, WR]]),
                view(gx[:, s * TAPS * WC:s * TAPS * WC + 1], [[1, WC], [WC, TAPS], [0, WR]]),
                view(hy[:, s * TAPS * WR:s * TAPS * WR + 1], [[0, WC], [WR, TAPS], [1, WR]]), ALU.mult)

        def shifted(eng, i, ky, wide, dst, load):
            for g in range(G):
                d = 2 * g + 1
                start = wide_at(-1 + d * (ky - 1), -1 - d)
                eng.dma_start(dst[32 * g:32 * g + 32, :].rearrange("p (c n) -> p c n", c=3),
                              view(wide[32 * g:32 * g + 32, bass.ds(i * (ROWS * WP) + start, 1)],
                                   [[d, 3], [1, BAND]])).then_inc(load, 16)

        @block.sync
        def _(sp):
            sp.sem_inc(st_out, 16)
            sp.sem_inc(off_kept, 16)
            for dst, src in loads:
                sp.dma_start(dst, src, allow_slow_non_contiguous=True).then_inc(w_in, 16)
            sp.wait_ge(s_zero, 1)
            for dst, src in late:
                sp.dma_start(dst, src, allow_slow_non_contiguous=True).then_inc(w_in, 16)
            sp.wait_ge(s_ready, 1)
            with sp.Fori(0, B) as b:
                for j in range(4):
                    src = x_tok[bass.ds(b * N + j * N // 4, N // 4), :].rearrange("(t p) c -> p t c", p=128)
                    dst = xtok[:, j * 1024:(j + 1) * 1024].rearrange("p (t c) -> p t c", c=C)
                    sp.dma_start(dst, src).then_inc(x_in[j], 16)
                sp.sem_inc(done_a, 1)
                sp.wait_ge(done_a, b * 5 + 5)
                hold(sp)
                with sp.Fori(0, BANDS) as i:
                    t = b * BANDS + i
                    sp.wait_ge(off_mm, t + 1)
                    hold(sp)
                    for kx in range(3):
                        sp.dma_start(qstack[32 * kx:32 * kx + 32, 0:WR * RP - 2],
                                     qpad[0:32, bass.ds(i * (ROWS * RP) + kx, WR * RP - 2)]).then_inc(q_in, 16)
                    sp.wait_ge(offt_ready, t + 1)
                    hold(sp)
                    sp.dma_start(offs[bass.ds(i * 128, 128), :], offt[:, :]).then_inc(off_kept, 16)
                    sp.wait_ge(s_used, t * PATCHES + 1)
                    hold(sp)
                    for ky in range(3):
                        shifted(sp, i, ky, kwide, kband[:, 3 * ky * BAND:3 * (ky + 1) * BAND], k_in)
                    for ky in range(3):
                        sp.wait_ge(v_packed, t * 3 + ky + 1)
                        hold(sp)
                        shifted(sp, i, ky, vwide, vstage[:, :], v_in)
                sp.wait_ge(off_kept, b * (16 * BANDS) + 16 * BANDS + 16)
                hold(sp)
                sp.sem_inc(done_b, 1)
                sp.wait_ge(done_b, b * 5 + 5)
                hold(sp)
                sp.sem_inc(done_f, 1)
                sp.wait_ge(done_f, b * 5 + 5)
                hold(sp)
                with sp.Fori(0, BANDS) as u:
                    t = b * BANDS + u
                    sp.wait_ge(turn_done, t + 1)
                    hold(sp)
                    src = x_tok[bass.ds(b * N + u * 512, 512), :].rearrange("(t p) c -> p t c", p=128)
                    sp.dma_start(x1.rearrange("p (t c) -> p t c", c=C), src).then_inc(xr_in, 16)
                    sp.wait_ge(turn_done, t + 2)
                    hold(sp)
                    dst = out_tok[bass.ds(b * N + u * 512, 512), :].rearrange("(t p) c -> p t c", p=128)
                    sp.dma_start(dst, acc.rearrange("p (t c) -> p t c", c=C)).then_inc(st_out, 16)
                sp.wait_ge(st_out, b * (16 * BANDS) + 16 * BANDS + 16)
                hold(sp)
                sp.sem_inc(done_c, 1)
                sp.wait_ge(done_c, b * 5 + 5)
                hold(sp)

        @block.gpsimd
        def _(pool):
            nc.gpsimd.memset(s_w1, 0.0)
            nc.gpsimd.memset(s_one, 1.0)
            nc.gpsimd.memset(half[:, :], -0.5)
            nc.gpsimd.memset(ob_sb[:, :], 0.0)
            nc.gpsimd.memset(qpad[:, :], 0.0)
            nc.gpsimd.memset(kwide[:, :], 0.0)
            nc.gpsimd.memset(vwide[:, :], 0.0)
            nc.gpsimd.memset(qbd[:, :], 0.0)
            pool.drain().then_inc(s_zero, 1)
            pool.sem_inc(v_packed, 1)
            pool.wait_ge(s_ready, 1)
            with pool.Fori(0, B) as b:
                for r in (*raw, kwide[:, :], vwide[:, :]):
                    nc.gpsimd.memset(r, 0.0).then_inc(raw_zero, 1)
                pool.wait_ge(gvar_ready, b + 1)
                nc.gpsimd.tensor_tensor(mom[:, 6:7], mom[:, 6:7], half[:, 0:1], ALU.pow).then_inc(gstd_ready, 1)
                pool.drain().then_inc(done_a, 1)
                pool.wait_ge(done_a, b * 5 + 5)
                hold(pool)
                with pool.Fori(0, BANDS) as i:
                    t = b * BANDS + i
                    off = offt[:, :]
                    pool.wait_ge(offt_ready, t + 1)
                    for dst, n, at, axis in ((hx, WC, 0, 1), (hy, WR, WC, 0)):
                        nc.gpsimd.tensor_tensor(
                            view(dst, [[TAPS * n, PATCHES], [n, TAPS], [1, n]]),
                            view(grid[:, at:at + 1], [[0, PATCHES], [0, TAPS], [1, n]]),
                            view(off[:, axis:axis + 1], [[32, PATCHES], [2, TAPS], [0, n]]),
                            ALU.subtract).then_inc(diff_ready, 1)
                    for ky in range(3):
                        pool.wait_ge(v_in, t * BAND_IN + (ky + 1) * 16 * G)
                        hold(pool)
                        for kx in range(3):
                            ins = nc.gpsimd.tensor_copy(
                                view(vwin[:, (3 * ky + kx) * WR:(3 * ky + kx) * WR + 1], [[TAPS * WR, W + 2], [1, WR]]),
                                view(vstage[:, kx * BAND:kx * BAND + 1], [[1, W + 2], [WP, WR]]))
                        ins.then_inc(v_packed, 1)
                    pool.wait_ge(gx_ready, t + 1)
                    for s in range(1, PATCHES, 2):
                        if s > 1:
                            pool.wait_ge(t_ready, t * (3 * PATCHES) + 3 * (s - 1))
                        weigh(nc.gpsimd, s).then_inc(a_pool, 1)
                pool.drain().then_inc(done_b, 1)
                pool.wait_ge(done_b, b * 5 + 5)
                pool.wait_ge(flag_ready, b + 1)
                hold(pool)
                with pool.If(pool.value_load(flag[0:1, 0:1], min_val=0, max_val=1) != 0):
                    with pool.Fori(0, H) as y:
                        pool.wait_ge(f_turned, 1)
                        pool.sem_clear(f_turned)
                        for g in range(G):
                            dst = table.rearrange("(n g) e -> g n e", g=G)[g, bass.ds(y * W, W), :]
                            pool.dma_start(dst.rearrange("(j p) e -> p j e", p=32),
                                           f_out[32 * g:32 * g + 32, :].rearrange("p (j e) -> p j e", j=2)).then_inc(f_stored, 16)
                        pool.wait_ge(f_stored, 16 * G)
                        pool.dma_reset(range(f_stored.num, f_stored.num + 1))
                        pool.sem_clear(f_stored)
                        pool.sem_inc(f_table, 1)
                    with pool.Fori(0, BANDS) as i:
                        pool.dma_start(f_off, offs[bass.ds(i * 128, 128), :]).then_inc(f_stored, 16)
                        pool.wait_ge(f_stored, 16)
                        pool.dma_reset(range(f_stored.num, f_stored.num + 1))
                        pool.sem_clear(f_stored)
                        pool.sem_inc(f_off_in, 1)
                        with pool.Fori(0, PATCHES):
                            pool.wait_ge(f_ready, 1)
                            pool.sem_clear(f_ready)
                            for k in range(4 * TAPS):
                                pool.indirect_dma_start(
                                    out=f_corner[:, 64 * k:64 * k + 64], out_offset=None, in_=table,
                                    in_offset=bass.IndirectOffsetOnAxis(ap=f_idx[:, k:k + 1], axis=0)).then_inc(f_gather, 16)
                            pool.wait_ge(f_gather, 16 * 4 * TAPS)
                            pool.dma_reset(range(f_gather.num, f_gather.num + 1))
                            pool.sem_clear(f_gather)
                            pool.sem_inc(f_gathered, 1)
                        pool.wait_ge(f_used, 1)
                        pool.sem_clear(f_used)
                pool.drain().then_inc(done_f, 1)
                pool.wait_ge(done_f, b * 5 + 5)
                hold(pool)
                with pool.Fori(0, BANDS) as u:
                    t = b * BANDS + u
                    pool.wait_ge(turn_done, t + 1)
                    hold(pool)
                    nc.gpsimd.tensor_copy(ao, xch[:, bass.ds(u * 512, 512)]).then_inc(ao_ready, 1)
                    for k in range(2):
                        pool.wait_ge(var_ready, t * 2 + k + 1)
                        nc.gpsimd.tensor_tensor(lrs[:, 0:4], lrs[:, 0:4], half[:, :], ALU.pow).then_inc(std_ready, 1)
                pool.drain().then_inc(done_c, 1)
                pool.wait_ge(done_c, b * 5 + 5)
                hold(pool)

        @block.tensor
        def _(pe):
            mm = nc.tensor.matmul

            pe.wait_ge(w_in, ALL_IN)
            nc.tensor.transpose(P[0][:, 0:128], s_w1, ident[:, :])
            for c in range(3):
                nc.tensor.transpose(P[1][:, 128 * c:128 * c + 128], s_wa[:, c, :], ident[:, :])
            mm(P[2][:, 0:2 * C + E], s_one, s_row, start=True, stop=True)
            pe.drain().then_inc(s_setup_pe, 1)
            pe.wait_ge(s_setup_cp, 2)
            for t in range(TAPS):
                ky, kx = divmod(t, 3)
                for g in range(G):
                    o = P[3][32 * kx:32 * kx + 32, ky * 128 + 32 * g:ky * 128 + 32 * g + 32]
                    mm(o[:, 0:18], s_wpo[:, g, :, t], s_w1T[0:32, 32 * g:32 * g + 18], start=True, stop=True)
                    mm(o[:, 18:32], s_wpm[:, :, t], s_w1T[0:32, 32 * g + 18:32 * g + 32], start=True, stop=True)
            pe.drain().then_inc(s_setup_pe, 1)
            pe.sem_inc(off_mm, 1)
            pe.wait_ge(s_ready, 1)

            with pe.Fori(0, B) as b:
                for m in range(8):
                    if m % 2 == 0:
                        pe.wait_ge(x_in[m // 2], b * 16 + 16)
                    if m >= 2:
                        pe.wait_ge(xT_copied, b * 8 + m - 1)
                    for j in range(4):
                        ins = nc.tensor.transpose(P[m % 2][:, 128 * j:128 * j + 128],
                                                  xtok[:, (4 * m + j) * C:(4 * m + j + 1) * C], ident[:, :])
                    ins.then_inc(xT_ready, 1)
                pe.wait_ge(moments, b + 1)
                mm(P[7][:, 0:2], gavg[:, :], mom[:, 2:4], start=True, stop=True).then_inc(groups, 1)
                pe.wait_ge(norm, b + 1)
                for c in range(3):
                    ins = mm(P[6][:, c:c + 1], wq_sb[:, c * C:c * C + C], mom[:, 7:8], start=True, stop=True)
                ins.then_inc(biasmm, 1)
                pe.wait_ge(wnorm, b + 1)
                pe.wait_ge(xT_copied, b * 8 + 8)
                for c in range(3):
                    for n in range(8):
                        k = c * 8 + n
                        if k >= 2:
                            pe.wait_ge(raw_ready, b * 24 + k - 1)
                        mm(P[2 + k % 2][:, :], wn_sb[:, c * C:c * C + C], xch[:, 512 * n:512 * n + 512],
                           start=True, stop=True).then_inc(qkv_ready, 1)
                r3 = raw[0].rearrange("p (y x) -> p y x", x=RP)
                pe.wait_ge(diag_ready, b + 1)
                pe.wait_ge(raw_ready, b * 24 + 24)
                for n in range(8):
                    if n >= 2:
                        pe.wait_ge(v_ready, b * 8 + n - 1)
                    for t in range(TAPS):
                        ky, kx = divmod(t, 3)
                        ins = mm(P[4 + n % 2][:, :], diag[:, t, :], r3[:, 8 * n + ky:8 * n + ky + 8, kx:kx + W],
                                 start=t == 0, stop=t == TAPS - 1)
                    ins.then_inc(vconv_ready, 1)
                pe.drain().then_inc(done_a, 1)
                pe.wait_ge(done_a, b * 5 + 5)
                hold(pe)

                with pe.Fori(0, BANDS) as i:
                    t = b * BANDS + i
                    pe.wait_ge(q_in, t * 48 + 48)
                    hold(pe)
                    for ky in range(3):
                        mm(P[6][:, :], conv_w[:, ky, :], view(qstack[:, ky * RP:ky * RP + 1],
                           [[PCOLS, PATCHES], [RP, ROWS], [1, PCOLS]]), start=ky == 0, stop=False)
                    mm(P[6][:, :], pass_w[:, :], view(qpad[:, bass.ds(i * (ROWS * RP) + RP + 1, 1)],
                       [[PCOLS, PATCHES], [RP, ROWS], [1, PCOLS]]), start=False, stop=True).then_inc(off_mm, 1)
                    pe.wait_ge(qbd_ready, t * 4 + 4)
                    pe.wait_ge(k_in, t * BAND_IN + BAND_IN)
                    for s in range(PATCHES):
                        pe.wait_ge(s_used, t * PATCHES + (s if s >= 2 else 1))
                        for h, (t0, nt) in enumerate(((0, 5), (5, 4))):
                            keys = view(kband[:, t0 * BAND + PCOLS * s:t0 * BAND + PCOLS * s + 1],
                                        [[BAND, nt], [WP, WR], [1, WC]])
                            ins = mm(P[2 * (s % 2) + h][:, 0:nt * WIN], qbd[:, 128 * s:128 * s + 128], keys,
                                     start=True, stop=True)
                        ins.then_inc(s_mm, 1)
                    pe.wait_ge(v_packed, t * 3 + 4)

                    def turn(s):
                        if s % 2 == 0:
                            pe.wait_ge(a_dve, t * 8 + s // 2 + 1)
                        else:
                            pe.wait_ge(a_pool, t * 8 + s // 2 + 1)
                        jobs = [[("a", k) for k in range(4)], [("v", k) for k in range(4)], [("a", 4), ("v", 4)]]
                        for k, job in enumerate(jobs):
                            if s > 0:
                                pe.wait_ge(t_copied, t * (3 * PATCHES) + 3 * s + k - 1)
                            for c, (what, part) in enumerate(job):
                                if what == "a":
                                    src = att[:, s % 2, KEYS * part:KEYS * (part + 1)]
                                else:
                                    at = PCOLS * s * TAPS * WR + KEYS * part
                                    src = vwin[:, at:at + KEYS]
                                ins = nc.tensor.transpose(P[4 + k][0:KEYS, 128 * c:128 * c + 128], src, ident[:, :])
                            ins.then_inc(t_ready, 1)

                    def mix(s):
                        pe.wait_ge(t_copied, t * (3 * PATCHES) + 3 * s + 4)
                        if s % 4 == 0 and s:
                            pe.wait_ge(o_copied, t * 4 + s // 4)
                        for pair in range(5):
                            ins = mm(P[7][:, 128 * (s % 4):128 * (s % 4) + 128],
                                     keysT[0:KEYS, s % 2, 128 * (5 + pair):128 * (6 + pair)],
                                     keysT[0:KEYS, s % 2, 128 * pair:128 * pair + 128], start=pair == 0, stop=pair == 4)
                        ins.then_inc(o_ready, 1)

                    for s in range(PATCHES):
                        turn(s)
                        if s:
                            mix(s - 1)
                    mix(PATCHES - 1)
                pe.drain().then_inc(done_b, 1)
                pe.wait_ge(done_b, b * 5 + 5)
                hold(pe)
                pe.wait_ge(peak_ready, b + 1)
                mm(P[0][0:1, 0:128], offmax[:, 0:1], ident[:, :], start=True, stop=True).then_inc(peak_row, 1)
                pe.drain().then_inc(done_f, 1)
                pe.wait_ge(done_f, b * 5 + 5)
                hold(pe)

                with pe.Fori(0, BANDS) as u:
                    t = b * BANDS + u
                    q4 = lambda a, j: a[:, 128 * j:128 * j + 128]
                    pe.wait_ge(ao_ready, t + 1)
                    for j in range(4):
                        ins = mm(q4(P[0], j), q4(ao, j), wproj_sb[:, :], start=True, stop=True)
                    ins.then_inc(proj_ready, 1)
                    pe.wait_ge(ln_ready, t + 1)
                    for j in range(4):
                        ins = nc.tensor.transpose(q4(P[1], j), q4(ln, j), ident[:, :])
                    ins.then_inc(lnT_ready, 1)
                    pe.wait_ge(lnT_copied, t + 1)
                    mm(P[2][:, :], wa_sb[:, 0:C], lnT, start=True, stop=True)
                    mm(P[3][:, :], wa_sb[:, C:2 * C], lnT, start=True, stop=True).then_inc(qkv_c, 1)
                    for j in range(4):
                        ins = mm(q4(P[4], j), q4(lnT, j), wa_sb[:, 2 * C:3 * C], start=True, stop=True)
                    ins.then_inc(qkv_c, 1)
                    pe.wait_ge(qk_ready, t + 1)
                    for j in range(4):
                        ins = nc.tensor.transpose(q4(P[5], j), q4(qk[:, 512:1024], j), ident[:, :])
                    ins.then_inc(kt_ready, 1)
                    for j in range(4):
                        ins = mm(q4(P[6], j), q4(qk[:, 512:1024], j), q4(qk[:, 0:512], j), start=True, stop=True)
                    ins.then_inc(st_ready, 1)
                    pe.wait_ge(kt_copied, t + 1)
                    pe.wait_ge(v_c, t + 1)
                    vj = lambda j: vone[:, 129 * j:129 * j + 129]
                    sj = lambda j: state[:, 129 * j:129 * j + 129]
                    for j in range(4):
                        ins = mm(P[j // 2][:, 256 * (j % 2):256 * (j % 2) + 129], q4(ktok, j), vj(j), start=True, stop=True)
                    ins.then_inc(delta_ready, 1)
                    pe.wait_ge(pm_ready, t + 1)
                    pe.wait_ge(state_ready, t + 1)
                    for j in range(4):
                        o = P[2 + j // 2][:, 256 * (j % 2):256 * (j % 2) + 129]
                        mm(o, q4(pmask, j), vj(j), start=True, stop=False)
                        ins = mm(o, q4(qk[:, 0:512], j), sj(j), start=False, stop=True)
                    ins.then_inc(num_ready, 1)
                    pe.wait_ge(ln2_ready, t + 1)
                    for j in range(4):
                        ins = nc.tensor.transpose(q4(P[4], j), q4(ln, j), ident[:, :])
                    ins.then_inc(ln2T_ready, 1)
                    pe.wait_ge(ln2T_copied, t + 1)
                    for j in range(4):
                        ins = mm(P[5][:, E * j:E * j + E], q4(lnT, j), wr_sb[:, :], start=True, stop=True)
                    ins.then_inc(route_ready, 1)

                    def experts(j):
                        for h in range(2):
                            ins = mm(P[2 * (j % 2) + h][:, :], q4(lnT, j), we_sb[:, 512 * h:512 * h + 512], start=True, stop=True)
                        ins.then_inc(ex_ready, 1)

                    experts(0)
                    experts(1)
                    pe.wait_ge(gate_ready, t + 1)
                    for j in range(4):
                        ins = mm(P[6][0:E, 128 * j:128 * j + 128], rw[:, E * j:E * j + E], ident[:, :], start=True, stop=True)
                    ins.then_inc(gateT_ready, 1)
                    pe.wait_ge(gateT_copied, t + 1)
                    for j in range(4):
                        ins = mm(q4(P[7], j), wT[:, 128 * j:128 * j + 128], be_sb[:, :], start=True, stop=True)
                    ins.then_inc(bias_c, 1)
                    for j in range(2, 4):
                        pe.wait_ge(ex_used, t * 4 + j - 1)
                        experts(j)
                pe.drain().then_inc(done_c, 1)
                pe.wait_ge(done_c, b * 5 + 5)
                hold(pe)

        @block.scalar
        def _(act):
            A = nc.scalar.activation
            act.wait_ge(s_setup_pe, 1)
            A(rows[:, :], P[2][:, 0:2 * C + E], ACT.Copy)
            A(wa_sb[:, :], P[1][:, 0:3 * C], ACT.Copy)
            act.wait_ge(s_zero, 1)
            act.drain().then_inc(s_setup_cp, 1)
            act.sem_inc(t_copied, 1)
            act.wait_ge(s_ready, 1)
            with act.Fori(0, B) as b:
                for m in range(8):
                    act.wait_ge(xT_ready, b * 8 + m + 1)
                    A(xch[:, 512 * m:512 * m + 512], P[m % 2][:, :], ACT.Copy).then_inc(xT_copied, 1)
                act.wait_ge(raw_zero, b * 4 + 4)
                act.wait_ge(bias_ok, b + 1)
                for c in range(3):
                    r3 = raw[c % 2].rearrange("p (y x) -> p y x", x=RP)
                    if c == 2:
                        act.wait_ge(q_conv, b * 4 + 4)
                    for n in range(8):
                        act.wait_ge(qkv_ready, b * 24 + c * 8 + n + 1)
                        A(r3[:, 8 * n + 1:8 * n + 9, 1:W + 1], P[2 + n % 2][:, :].rearrange("p (y x) -> p y x", x=W),
                          ACT.Identity, bias=bn_sb[:, c:c + 1]).then_inc(raw_ready, 1)
                for n in range(8):
                    act.wait_ge(vconv_ready, b * 8 + n + 1)
                    A(view(vwide[:, wide_at(8 * n, 0):wide_at(8 * n, 0) + 1], [[WP, 8], [1, W]]),
                      P[4 + n % 2][:, :].rearrange("p (y x) -> p y x", x=W),
                      ACT.Identity, bias=db_sb[:, 2:3]).then_inc(v_ready, 1)
                act.drain().then_inc(done_a, 1)
                act.wait_ge(done_a, b * 5 + 5)
                hold(act)

                with act.Fori(0, BANDS) as i:
                    t = b * BANDS + i
                    act.wait_ge(off_mm, t + 2)
                    A(offc[:, :], P[6][:, :], ACT.Identity, bias=ob_sb[:, 0:1]).then_inc(offc_ready, 1)
                    for g in range(G):
                        q = slice(32 * g, 32 * g + 32)
                        A(view(qbd[q, 32 * g:32 * g + 1], [[128, PATCHES], [PCOLS, ROWS], [1, PCOLS]]),
                          view(qpad[q, bass.ds(i * (ROWS * RP) + RP + 1, 1)], [[PCOLS, PATCHES], [RP, ROWS], [1, PCOLS]]),
                          ACT.Copy, scale=SCALE).then_inc(qbd_ready, 1)
                    act.wait_ge(offt_ready, t + 1)
                    A(msk[:, :].rearrange("p (s k) -> p s k", k=TAPS),
                      offt[:, :].rearrange("p (s j) -> p s j", j=32)[:, :, 18:27], ACT.Exp, scale=-1.0).then_inc(mexp, 1)
                    act.wait_ge(diff_ready, t * 2 + 2)
                    A(hat, hat, ACT.Abs).then_inc(absd, 1)
                    act.wait_ge(absd, t + 1)
                    A(hat, hat, ACT.Relu, bias=1.0, scale=-1.0).then_inc(hat_ready, 1)
                    act.wait_ge(lg_ready, t + 1)
                    A(lg[:, :], lg[:, :], ACT.Exp).then_inc(p_ready, 1)
                    for s in range(PATCHES):
                        for k in range(3):
                            act.wait_ge(t_ready, t * (3 * PATCHES) + 3 * s + k + 1)
                            if k == 0 and s >= 2:
                                act.wait_ge(o_ready, t * PATCHES + s - 1)
                            if k < 2:
                                A(keysT[0:KEYS, s % 2, 640 * k:640 * k + 512], P[4 + k][0:KEYS, :], ACT.Copy).then_inc(t_copied, 1)
                            else:
                                A(view(keysT[0:KEYS, s % 2, 512:513], [[640, 2], [1, 128]]),
                                  P[6][0:KEYS, 0:256].rearrange("p (a n) -> p a n", a=2), ACT.Copy).then_inc(t_copied, 1)
                act.drain().then_inc(done_b, 1)
                act.wait_ge(done_b, b * 5 + 5)
                act.wait_ge(flag_ready, b + 1)
                hold(act)
                with act.If(act.value_load(flag[0:1, 0:1], min_val=0, max_val=1) != 0):
                    with act.Fori(0, BANDS):
                        with act.Fori(0, PATCHES):
                            act.wait_ge(f_masked, 1)
                            act.sem_clear(f_masked)
                            A(f_mask, f_mask, ACT.Exp, scale=-1.0).then_inc(f_mexp, 1)
                            act.wait_ge(f_lgr, 1)
                            act.sem_clear(f_lgr)
                            A(f_lg, f_lg, ACT.Exp).then_inc(f_exp, 1)
                act.drain().then_inc(done_f, 1)
                act.wait_ge(done_f, b * 5 + 5)
                hold(act)

                with act.Fori(0, BANDS) as u:
                    t = b * BANDS + u
                    act.wait_ge(lnT_ready, t + 1)
                    A(lnT, P[1][:, :], ACT.Copy).then_inc(lnT_copied, 1)
                    act.wait_ge(qkv_c, t * 2 + 1)
                    A(qk_raw[:, 0:512], P[2][:, :], ACT.Identity, bias=ba_sb[:, 0:1])
                    A(qk_raw[:, 512:1024], P[3][:, :], ACT.Identity, bias=ba_sb[:, 1:2]).then_inc(qk_biased, 1)
                    act.wait_ge(clip_ready, t + 1)
                    A(qk_exp, qk_exp, ACT.Exp).then_inc(exp_ready, 1)
                    act.wait_ge(kt_ready, t + 1)
                    A(ktok, P[5][:, :], ACT.Copy).then_inc(kt_copied, 1)
                    act.wait_ge(ln2T_ready, t + 1)
                    A(lnT, P[4][:, :], ACT.Copy).then_inc(ln2T_copied, 1)
                    act.wait_ge(logit_ready, t + 1)
                    A(re_, rl, ACT.Exp).then_inc(rexp_ready, 1)
                    act.wait_ge(gateT_ready, t + 1)
                    A(wT, P[6][0:E, :], ACT.Copy).then_inc(gateT_copied, 1)
                act.drain().then_inc(done_c, 1)
                act.wait_ge(done_c, b * 5 + 5)
                hold(act)

        @block.vector
        def _(dve):
            V = nc.vector

            def general_path(dve):
                count = [0]

                def link(ins):
                    ins.then_inc(f_chain, 1)
                    count[0] += 1
                    dve.wait_ge(f_chain, count[0])

                def unchain():
                    dve.sem_clear(f_chain)
                    count[0] = 0

                with dve.Fori(0, H) as y:
                    link(V.tensor_copy(f_in[:, 0:64], kwide[:, bass.ds(y * WP + wide_at(0, 0), W)]))
                    link(V.tensor_copy(f_in[:, 64:128], vwide[:, bass.ds(y * WP + wide_at(0, 0), W)]))
                    for n in range(2):
                        for j in range(2):
                            link(V.transpose(f_out[:, 64 * j + 32 * n:64 * j + 32 * n + 32],
                                             f_in[:, 64 * n + 32 * j:64 * n + 32 * j + 32]))
                    unchain()
                    dve.sem_inc(f_turned, 1)
                    dve.wait_ge(f_table, 1)
                    dve.sem_clear(f_table)
                two = lambda a, n: view(a[:, n:n + 1], [[18, 2], [1, TAPS]])
                link(V.memset(f_at, 0.0))
                unchain()
                with dve.Fori(0, BANDS) as i:
                    dve.wait_ge(f_off_in, 1)
                    dve.sem_clear(f_off_in)
                    with dve.Fori(0, PATCHES) as s:
                        link(V.tensor_copy(f_q.rearrange("p (r c) -> p r c", c=PCOLS),
                                           view(qpad[:, bass.ds(i * (ROWS * RP) + s * PCOLS + RP + 1, 1)],
                                                [[RP, ROWS], [1, PCOLS]])))
                        link(V.transpose(f_qT, f_q))
                        link(V.tensor_scalar(f_qT, f_qT, SCALE, None, ALU.mult))
                        link(V.tensor_copy(f_mask, f_off[:, bass.ds(s * 32 + 18, TAPS)]))
                        dve.sem_inc(f_masked, 1)
                        for n in range(2):
                            link(V.tensor_scalar(f_pos[:, TAPS * n:TAPS * n + TAPS], place[:, TAPS * n:TAPS * n + TAPS],
                                                 f_at[:, n:n + 1], None, ALU.add))
                            link(V.tensor_copy(f_tmp[:, TAPS * n:TAPS * n + TAPS],
                                               view(f_off[:, bass.ds(s * 32 + n, 1)], [[2, TAPS]])))
                        link(V.tensor_tensor(f_pos, f_pos, f_tmp, ALU.add))
                        link(V.tensor_scalar(f_pos, f_pos, -3.0, W + 3.0, ALU.max, ALU.min))
                        link(V.tensor_copy(f_int, f_pos))
                        link(V.tensor_copy(f_low, f_int))
                        link(V.tensor_tensor(f_tmp, f_low, f_pos, ALU.is_gt))
                        link(V.tensor_tensor(f_low, f_low, f_tmp, ALU.subtract))
                        link(V.tensor_tensor(f_frac, f_pos, f_low, ALU.subtract))
                        link(V.tensor_scalar(f_wt[:, 0:18], f_frac, -1.0, 1.0, ALU.mult, ALU.add))
                        link(V.tensor_copy(f_wt[:, 18:36], f_frac))
                        link(V.tensor_copy(f_edge[:, 0:18], f_low))
                        link(V.tensor_scalar(f_edge[:, 18:36], f_low, 1.0, None, ALU.add))
                        link(V.scalar_tensor_tensor(f_wt, f_edge, 0.0, f_wt, ALU.is_ge, ALU.mult))
                        link(V.scalar_tensor_tensor(f_wt, f_edge, W - 1.0, f_wt, ALU.is_le, ALU.mult))
                        link(V.tensor_scalar(f_edge, f_edge, 0.0, W - 1.0, ALU.max, ALU.min))
                        link(V.tensor_scalar(two(f_edge, 0), two(f_edge, 0), float(W), None, ALU.mult))
                        corner = lambda a, at: view(a[:, at:at + 1], [[4, TAPS], [1, 2]])
                        for sy in range(2):
                            ys = lambda a: view(a[:, 18 * sy:18 * sy + 1], [[1, TAPS], [0, 2]])
                            xs = lambda a: view(a[:, TAPS:TAPS + 1], [[1, TAPS], [18, 2]])
                            link(V.tensor_tensor(corner(f_cw, 2 * sy), ys(f_wt), xs(f_wt), ALU.mult))
                            link(V.tensor_tensor(corner(f_flat, 2 * sy), ys(f_edge), xs(f_edge), ALU.add))
                        link(V.tensor_scalar(f_flat, f_flat, float(G), place[:, 2 * TAPS:2 * TAPS + 1], ALU.mult, ALU.add))
                        link(V.tensor_copy(f_idx, f_flat))
                        dve.sem_inc(f_ready, 1)
                        dve.wait_ge(f_mexp, 1)
                        dve.sem_clear(f_mexp)
                        link(V.tensor_scalar(f_mask, f_mask, 1.0, None, ALU.add))
                        link(V.reciprocal(f_mask, f_mask))
                        dve.wait_ge(f_gathered, 1)
                        dve.sem_clear(f_gathered)
                        link(V.tensor_tensor(f_part.rearrange("p (k e) -> p k e", e=64),
                                             f_corner.rearrange("p (k e) -> p k e", e=64),
                                             view(f_cw[:, 0:1], [[1, 4 * TAPS], [0, 64]]), ALU.mult))
                        link(V.tensor_reduce(f_sample.rearrange("p (k e) -> p k e", e=64),
                                             view(f_part[:, 0:1], [[256, TAPS], [1, 64], [64, 4]]), AX.X, ALU.add))
                        link(V.tensor_tensor(f_sample.rearrange("p (k e) -> p k e", e=64),
                                             f_sample.rearrange("p (k e) -> p k e", e=64),
                                             view(f_mask[:, 0:1], [[1, TAPS], [0, 64]]), ALU.mult))
                        products = view(f_part[:, 0:1], [[32, TAPS], [1, 32]])
                        link(V.tensor_tensor(products, view(f_sample[:, 0:1], [[64, TAPS], [1, 32]]),
                                             view(f_qT[:, 0:1], [[0, TAPS], [1, 32]]), ALU.mult))
                        link(V.tensor_reduce(f_lg, products, AX.X, ALU.add))
                        link(V.tensor_reduce(f_s[:, 0:1], f_lg, AX.X, ALU.max))
                        link(V.tensor_scalar(f_lg, f_lg, f_s[:, 0:1], None, ALU.subtract))
                        dve.sem_inc(f_lgr, 1)
                        dve.wait_ge(f_exp, 1)
                        dve.sem_clear(f_exp)
                        link(V.tensor_reduce(f_s[:, 1:2], f_lg, AX.X, ALU.add))
                        link(V.reciprocal(f_s[:, 2:3], f_s[:, 1:2]))
                        link(V.tensor_scalar(f_lg, f_lg, f_s[:, 2:3], None, ALU.mult))
                        link(V.tensor_tensor(products, view(f_sample[:, 32:33], [[64, TAPS], [1, 32]]),
                                             view(f_lg[:, 0:1], [[1, TAPS], [0, 32]]), ALU.mult))
                        link(V.tensor_reduce(f_o, view(f_part[:, 0:1], [[1, 32], [32, TAPS]]), AX.X, ALU.add))
                        link(V.transpose(f_oT, f_o))
                        link(V.tensor_copy(view(xch[:, bass.ds(i * BPX + s * PCOLS, 1)], [[W, ROWS], [1, PCOLS]]),
                                           f_oT.rearrange("p (r c) -> p r c", c=PCOLS)))
                        link(V.tensor_scalar(f_at[:, 1:2], f_at[:, 1:2], float(PCOLS), None, ALU.add))
                        unchain()
                    link(V.tensor_scalar(f_at[:, 0:1], f_at[:, 0:1], float(ROWS), None, ALU.add))
                    link(V.memset(f_at[:, 1:2], 0.0))
                    unchain()
                    dve.sem_inc(f_used, 1)

            dve.wait_ge(w_in, ALL_IN)
            dve.wait_ge(s_setup_pe, 1)
            V.tensor_copy(s_w1T, P[0][:, 0:128])
            V.memset(pass_w[0:32, :], 0.0)
            for g in range(1, 4):
                V.tensor_copy(pass_w[32 * g:32 * g + 32, :], P[0][32 * g:32 * g + 32, 0:128])
            V.memset(offmax[:, :], 0.0)
            dve.drain().then_inc(s_setup_cp, 1)
            dve.wait_ge(s_setup_cp, 2)
            dve.wait_ge(s_setup_pe, 2)
            V.tensor_copy(conv_w[:, :, :], P[3][0:96, 0:384].rearrange("p (a n) -> p a n", a=3))
            dve.sem_inc(s_used, 1)
            dve.sem_inc(turn_done, 1)
            dve.drain().then_inc(s_ready, 1)
            with dve.Fori(0, B) as b:
                for t in range(TAPS):
                    ins = V.tensor_scalar(diag[:, t, :], ident[:, :], dw_sb[:, 2, t:t + 1], None, ALU.mult)
                ins.then_inc(diag_ready, 1)
                for m in range(8):
                    dve.wait_ge(xT_copied, b * 8 + m + 1)
                    V.bn_stats(stats[:, m, :], xch[:, 512 * m:512 * m + 512]).then_inc(xT_stated, 1)
                dve.wait_ge(xT_stated, b * 8 + 8)
                hold(dve)
                ch = Chain(dve, dve_a, b, CHAIN_A)
                ch.link(V.bn_aggr(mom[:, 0:2], stats[:, :, :].rearrange("p a c -> p (a c)")))
                V.tensor_copy(mom[:, 2:3], mom[:, 0:1])
                V.scalar_tensor_tensor(mom[:, 3:4], mom[:, 0:1], mom[:, 0:1], mom[:, 1:2], ALU.mult, ALU.add).then_inc(moments, 1)
                dve.wait_ge(groups, b + 1)
                ch.link(V.tensor_copy(mom[:, 4:6], P[7][:, 0:2]))
                ch.link(V.tensor_tensor(mom[:, 6:7], mom[:, 4:5], mom[:, 4:5], ALU.mult))
                ch.link(V.tensor_tensor(mom[:, 6:7], mom[:, 5:6], mom[:, 6:7], ALU.subtract))
                V.tensor_scalar(mom[:, 6:7], mom[:, 6:7], 1e-5, None, ALU.add).then_inc(gvar_ready, 1)
                dve.wait_ge(gstd_ready, b + 1)
                ch.link(V.tensor_scalar(mom[:, 8:9], mom[:, 4:5], -1.0, None, ALU.mult))
                V.tensor_tensor(mom[:, 7:8], mom[:, 8:9], mom[:, 6:7], ALU.mult).then_inc(norm, 1)
                V.tensor_scalar(wn_sb[:, :], wq_sb[:, :], mom[:, 6:7], None, ALU.mult).then_inc(wnorm, 1)
                dve.wait_ge(biasmm, b + 1)
                V.tensor_tensor(bn_sb[:, :], P[6][:, 0:3], bq_sb[:, :], ALU.add).then_inc(bias_ok, 1)
                for c, (dst, pitch, at) in enumerate(((qpad, RP, RP + 1), (kwide, WP, wide_at(0, 0)))):
                    r3 = raw[c].rearrange("p (y x) -> p y x", x=RP)
                    dve.wait_ge(raw_ready, b * 24 + 8 * c + 8)
                    if c == 1:
                        dve.wait_ge(raw_zero, b * 4 + 4)
                    first = ch.n
                    for t in range(TAPS):
                        ky, kx = divmod(t, 3)
                        for h in range(4):
                            o = view(dst[:, at + 16 * h * pitch:at + 16 * h * pitch + 1], [[pitch, 16], [1, W]])
                            src = r3[:, 16 * h + ky:16 * h + ky + 16, kx:kx + W]
                            if t == 0:
                                ins = V.tensor_scalar(o, src, dw_sb[:, c, 0:1], db_sb[:, c:c + 1], ALU.mult, ALU.add)
                            else:
                                ch.after(first + 4 * (t - 1) + h + 1)
                                ins = V.scalar_tensor_tensor(o, src, dw_sb[:, c, t:t + 1], o, ALU.mult, ALU.add)
                            if t == TAPS - 1 and c == 0:
                                ins.then_inc(q_conv, 1)
                            else:
                                ch.did(ins)
                ch.close()
                dve.drain().then_inc(done_a, 1)
                dve.wait_ge(done_a, b * 5 + 5)
                hold(dve)

                with dve.Fori(0, BANDS) as i:
                    t = b * BANDS + i
                    ch = Chain(dve, dve_b, t, CHAIN_B)
                    per_patch = lambda a, n: a.rearrange("p (s n) -> p s n", n=n)
                    dve.wait_ge(offc_ready, t + 1)
                    dve.wait_ge(off_kept, t * 16 + 16)
                    hold(dve)
                    V.transpose(offt[:, :], offc[:, :]).then_inc(offt_ready, 1)
                    dve.wait_ge(offt_ready, t + 1)
                    ch.did(V.tensor_reduce(offmax[:, 1:2], per_patch(offt[:, :], 32)[:, :, 0:18], AX.XY, ALU.max))
                    ch.link(V.tensor_reduce(offmax[:, 2:3], per_patch(offt[:, :], 32)[:, :, 0:18], AX.XY, ALU.min))
                    ch.link(V.scalar_tensor_tensor(offmax[:, 0:1], offmax[:, 2:3], -1.0, offmax[:, 0:1], ALU.mult, ALU.max))
                    ch.link(V.tensor_tensor(offmax[:, 0:1], offmax[:, 0:1], offmax[:, 1:2], ALU.max))
                    dve.wait_ge(mexp, t + 1)
                    ch.link(V.tensor_scalar(msk[:, :], msk[:, :], 1.0, None, ALU.add))
                    ch.link(V.reciprocal(msk[:, :], msk[:, :]))
                    dve.wait_ge(hat_ready, t + 1)
                    reduced = {}

                    def reduce_columns(s):
                        dve.wait_ge(s_used, t * PATCHES + s + 2)
                        reduced[s] = ch.did(V.tensor_reduce(
                            rsum[:, s * TAPS * WR:(s + 1) * TAPS * WR],
                            prod[:, s % 2, :].rearrange("p (n w) -> p n w", w=WC), AX.X, ALU.add))

                    for s in range(PATCHES):
                        dve.wait_ge(s_mm, t * PATCHES + s + 1)
                        if s >= 2:
                            ch.after(reduced[s - 2])
                        for h, (t0, nt) in enumerate(((0, 5), (5, 4))):
                            at = (s * TAPS + t0) * WC
                            ins = V.tensor_tensor(
                                view(prod[:, s % 2, t0 * WIN:t0 * WIN + 1], [[WIN, nt], [WC, WR], [1, WC]]),
                                P[2 * (s % 2) + h][:, 0:nt * WIN].rearrange("p (k v w) -> p k v w", v=WR, w=WC),
                                view(hx[:, at:at + 1], [[WC, nt], [0, WR], [1, WC]]), ALU.mult)
                        ins.then_inc(s_used, 1)
                        if s:
                            reduce_columns(s - 1)
                    reduce_columns(PATCHES - 1)
                    ch.after(reduced[PATCHES - 1])
                    ch.link(V.tensor_tensor(rsum, rsum, hy, ALU.mult))
                    ch.link(V.tensor_reduce(lg[:, :], rsum.rearrange("p (n v) -> p n v", v=WR), AX.X, ALU.add))
                    ch.link(V.tensor_tensor(lg[:, :], lg[:, :], msk[:, :], ALU.mult))
                    mx, tot, inv = (small[:, n * PATCHES:(n + 1) * PATCHES] for n in range(3))
                    spread = lambda a: view(a, [[1, PATCHES], [0, TAPS]])
                    ch.link(V.tensor_reduce(mx, per_patch(lg[:, :], TAPS), AX.X, ALU.max))
                    V.tensor_tensor(per_patch(lg[:, :], TAPS), per_patch(lg[:, :], TAPS), spread(mx),
                                    ALU.subtract).then_inc(lg_ready, 1)
                    dve.wait_ge(p_ready, t + 1)
                    ch.link(V.tensor_reduce(tot, per_patch(lg[:, :], TAPS), AX.X, ALU.add))
                    ch.link(V.reciprocal(inv, tot))
                    ch.link(V.tensor_tensor(lg[:, :], lg[:, :], msk[:, :], ALU.mult))
                    ch.link(V.tensor_tensor(per_patch(lg[:, :], TAPS), per_patch(lg[:, :], TAPS), spread(inv), ALU.mult))
                    V.tensor_tensor(gx[:, :].rearrange("p (n w) -> p n w", w=WC), hx.rearrange("p (n w) -> p n w", w=WC),
                                    view(lg[:, 0:1], [[1, HN], [0, WC]]), ALU.mult).then_inc(gx_ready, 1)
                    dve.wait_ge(gx_ready, t + 1)

                    def own_blocks(q):
                        dve.wait_ge(o_ready, t * PATCHES + 4 * q + 4)
                        hold(dve)
                        for g in range(G):
                            r = slice(32 * g, 32 * g + 32)
                            ins = V.tensor_copy(
                                view(xch[r, bass.ds(i * BPX + 4 * q * PCOLS, 1)], [[PCOLS, 4], [W, ROWS], [1, PCOLS]]),
                                view(P[7][r, 32 * g:32 * g + 1], [[128, 4], [PCOLS, ROWS], [1, PCOLS]]))
                        ins.then_inc(o_copied, 1)

                    for s in range(0, PATCHES, 2):
                        if s:
                            dve.wait_ge(t_ready, t * (3 * PATCHES) + 3 * (s - 1))
                        weigh(V, s).then_inc(a_dve, 1)
                        if s % 4 == 0 and s:
                            own_blocks(s // 4 - 1)
                    own_blocks(3)
                    ch.close()
                dve.drain().then_inc(done_b, 1)
                dve.wait_ge(done_b, b * 5 + 5)
                hold(dve)
                V.tensor_scalar(offmax[:, 0:1], offmax[:, 0:1], 2.0, None, ALU.min).then_inc(peak_ready, 1)
                dve.wait_ge(peak_row, b + 1)
                V.tensor_reduce(offmax[0:1, 3:4], P[0][0:1, 0:128], AX.X, ALU.max).then_inc(peak_ok, 1)
                V.memset(offmax[:, 0:1], 0.0)
                dve.wait_ge(peak_ok, b + 1)
                V.tensor_scalar(flag[0:1, 0:1], offmax[0:1, 3:4], ONE_PIXEL, None, ALU.is_gt).then_inc(flag_ready, 1)
                dve.wait_ge(flag_ready, b + 1)
                hold(dve)
                with dve.If(dve.value_load(flag[0:1, 0:1], min_val=0, max_val=1) != 0):
                    general_path(dve)
                dve.drain().then_inc(done_f, 1)
                dve.wait_ge(done_f, b * 5 + 5)
                hold(dve)

                V.memset(state[:, 0:129], 0.0)
                V.memset(view(vone[:, 128:129], [[129, 4], [1, 1]]), 1.0)
                dve.drain()
                with dve.Fori(0, BANDS) as u:
                    t = b * BANDS + u
                    ch = Chain(dve, dve_c, t, CHAIN_C)
                    q4 = lambda a, j: a[:, 128 * j:128 * j + 128]
                    tiles = lambda a: a.rearrange("p (j n) -> p j n", j=4)
                    row = lambda at, n: view(rows[:, at:at + 1], [[0, 4], [1, n]])

                    def layernorm(src, signal):
                        for j in range(4):
                            ch.did(V.bn_stats(lstat[:, 6 * j:6 * j + 6], q4(src, j)))
                        ch.after(ch.n)
                        hold(dve)
                        for j in range(4):
                            ch.did(V.bn_aggr(lmom[:, 2 * j:2 * j + 2], lstat[:, 6 * j:6 * j + 6]))
                        ch.after(ch.n)
                        V.tensor_scalar(lrs[:, 0:4], view(lmom[:, 1:2], [[2, 4]]), 1e-5, None, ALU.add).then_inc(var_ready, 1)
                        dve.wait_ge(std_ready, t * 2 + (1 if signal is ln_ready else 2))
                        for j in range(4):
                            ins = V.tensor_scalar(q4(ln, j), q4(src, j), lmom[:, 2 * j:2 * j + 1], lrs[:, j:j + 1],
                                                  ALU.subtract, ALU.mult)
                        ins.then_inc(signal, 1)

                    dve.wait_ge(xr_in, t * 16 + 16)
                    ch.link(V.tensor_tensor(tiles(x1), tiles(x1), row(0, C), ALU.add))
                    dve.wait_ge(proj_ready, t + 1)
                    ch.link(V.tensor_tensor(x1, x1, P[0][:, :], ALU.add))
                    layernorm(x1, ln_ready)
                    dve.wait_ge(qk_biased, t + 1)
                    V.tensor_scalar(qk_exp, qk_raw, 0.0, None, ALU.min).then_inc(clip_ready, 1)
                    dve.wait_ge(qkv_c, t * 2 + 2)
                    V.tensor_tensor(view(vone[:, 0:1], [[129, 4], [1, C]]), tiles(P[4][:, :]), row(C, C),
                                    ALU.add).then_inc(v_c, 1)
                    dve.wait_ge(exp_ready, t + 1)
                    V.scalar_tensor_tensor(qk, qk_raw, 0.0, qk_exp, ALU.max, ALU.add).then_inc(qk_ready, 1)
                    dve.wait_ge(st_ready, t + 1)
                    V.tensor_tensor(tiles(pmask), tiles(P[6][:, :]), view(causal[:, 0:1], [[0, 4], [1, 128]]),
                                    ALU.mult).then_inc(pm_ready, 1)
                    dve.wait_ge(delta_ready, t + 1)
                    part = lambda p, j: P[p + j // 2][:, 256 * (j % 2):256 * (j % 2) + 129]
                    for j in range(4):
                        ins = V.tensor_tensor(state[:, 129 * (j + 1):129 * (j + 2)], state[:, 129 * j:129 * (j + 1)],
                                              part(0, j), ALU.add)
                        if j < 3:
                            ch.link(ins)
                    ins.then_inc(state_ready, 1)
                    dve.wait_ge(num_ready, t + 1)
                    for h in range(2):
                        ch.did(V.tensor_scalar(den[:, 2 * h:2 * h + 2], view(P[2 + h][:, 128:129], [[256, 2]]),
                                               1e-6, None, ALU.add))
                    ch.did(V.tensor_copy(state[:, 0:129], state[:, 516:645]))
                    ch.after(ch.n)
                    ch.link(V.reciprocal(den[:, :], den[:, :]))
                    for j in range(4):
                        ch.did(V.scalar_tensor_tensor(q4(t1, j), part(2, j)[:, 0:C], den[:, j:j + 1], q4(x1, j),
                                                      ALU.mult, ALU.add))
                    ch.after(ch.n)
                    layernorm(t1, ln2_ready)
                    dve.wait_ge(route_ready, t + 1)
                    le = lambda a: a.rearrange("p (j e) -> p j e", e=E)
                    ch.link(V.tensor_tensor(le(rl), le(P[5][:, 0:4 * E]), row(2 * C, E), ALU.add))
                    ch.link(V.tensor_reduce(rsm[:, 0:4], le(rl), AX.X, ALU.max))
                    V.tensor_tensor(le(rl), le(rl), view(rsm[:, 0:1], [[1, 4], [0, E]]), ALU.subtract).then_inc(logit_ready, 1)
                    dve.wait_ge(rexp_ready, t + 1)
                    pair = lambda a: a.rearrange("p (j i k) -> p j i k", j=4, i=E)
                    other, own = view(re_[:, 0:1], [[E, 4], [0, E], [1, E]]), view(re_[:, 0:1], [[E, 4], [1, E], [0, E]])
                    ch.did(V.tensor_tensor(pair(gt), other, own, ALU.is_gt))
                    ch.link(V.tensor_tensor(pair(eq), other, own, ALU.is_equal))
                    ch.link(V.tensor_tensor(pair(eq), pair(eq), view(before[:, 0:1], [[0, 4], [E, E], [1, E]]), ALU.mult))
                    ch.link(V.tensor_tensor(gt, gt, eq, ALU.add))
                    ch.link(V.tensor_reduce(rsel, gt.rearrange("p (n k) -> p n k", k=E), AX.X, ALU.add))
                    ch.link(V.scalar_tensor_tensor(rsel, rsel, 2.0, re_, ALU.is_lt, ALU.mult))
                    ch.link(V.tensor_reduce(rsm[:, 0:4], le(rsel), AX.X, ALU.add))
                    ch.link(V.reciprocal(rsm[:, 4:8], rsm[:, 0:4]))
                    V.tensor_tensor(le(rw), le(rsel), view(rsm[:, 4:5], [[1, 4], [0, E]]), ALU.mult).then_inc(gate_ready, 1)
                    dve.wait_ge(gate_ready, t + 1)
                    dve.wait_ge(bias_c, t + 1)
                    dve.wait_ge(st_out, t * 16 + 16)
                    ch.link(V.tensor_tensor(acc, t1, P[7][:, :], ALU.add))
                    for j in range(4):
                        dve.wait_ge(ex_ready, t * 4 + j + 1)
                        for e in range(E):
                            src = P[2 * (j % 2) + e // 4][:, 128 * (e % 4):128 * (e % 4) + 128]
                            w = rw[:, E * j + e:E * j + e + 1]
                            dst = q4((acc, accb)[e % 2], j)
                            if e == 1:
                                ins = V.tensor_scalar(dst, src, w, None, ALU.mult)
                            else:
                                if e > 1:
                                    ch.after(ch.n - 1)
                                ins = V.scalar_tensor_tensor(dst, src, w, dst, ALU.mult, ALU.add)
                            if e < E - 1:
                                ch.did(ins)
                        ins.then_inc(ex_used, 1)
                    ch.after(ch.n)
                    dve.wait_ge(ex_used, t * 4 + 4)
                    V.tensor_tensor(acc, acc, accb, ALU.add).then_inc(turn_done, 1)
                    ch.close()
                dve.drain().then_inc(done_c, 1)
                dve.wait_ge(done_c, b * 5 + 5)
                hold(dve)


_INS = ["x", "L0_conv_w_qkv", "L0_conv_b_qkv", "L0_conv_w_dw", "L0_conv_b_dw", "L0_conv_pconv_off_w", "L0_conv_w_off",
        "L0_conv_b_off", "L0_conv_pconv_mask_w", "L0_conv_w_mask", "L0_conv_b_mask", "L0_conv_w_proj",
        "L0_conv_b_proj", "L1_attn_W", "L1_attn_b", "L1_ffn_router_w", "L1_ffn_router_b", "L1_ffn_expert_w",
        "L1_ffn_expert_b"]


def _constants():
    import numpy as np
    p = np.arange(128)
    f32 = np.float32
    place_c, place_r = p % PCOLS, (p // PCOLS) % ROWS
    grid = np.concatenate([np.arange(WC)[None, :] - 1 - place_c[:, None],
                           np.arange(WR)[None, :] - 1 - place_r[:, None]], axis=1)
    e = np.arange(E)
    tap, group = np.arange(TAPS)[None, :], p // 32
    dilation = (2 * group + 1)[:, None]
    before = np.broadcast_to((e[None, :] < e[:, None]).reshape(1, E * E), (128, E * E))
    return [("ident", np.eye(128, dtype=f32)),
            ("gavg", ((p[:, None] // 4 == p[None, :] // 4) * 0.25).astype(f32)),
            ("causal", (p[:, None] <= p[None, :]).astype(f32)),
            ("grid", np.ascontiguousarray(grid.astype(f32))),
            ("before", np.ascontiguousarray(before.astype(f32))),
            ("place", np.ascontiguousarray(np.concatenate([
                place_r[:, None] + dilation * (tap // 3 - 1), place_c[:, None] + dilation * (tap % 3 - 1),
                group[:, None]], axis=1).astype(f32)))]


def kernel(**inputs):
    import numpy as _np
    import concourse.bacc as _bacc
    from concourse import mybir as _mybir
    from concourse.bass_utils import run_bass_kernel_spmd as _run

    nc = _bacc.Bacc("TRN2", target_bir_lowering=False, num_devices=1)
    arrays, args = {}, []
    for name, a in [(n, inputs[n]) for n in _INS] + _constants():
        a = _np.ascontiguousarray(a)
        arrays[f"in_{name}_dram"] = a
        args.append(nc.dram_tensor(f"in_{name}_dram", a.shape, _mybir.dt.from_np(a.dtype), kind="ExternalInput").ap())
    args.append(nc.dram_tensor("table_dram", (N * G, 2 * HC), FP32, kind="Internal").ap())
    args.append(nc.dram_tensor("offs_dram", (BANDS * 128, BPX), FP32, kind="Internal").ap())
    args.append(nc.dram_tensor("out_0_dram", (B, H, W, C), FP32, kind="ExternalOutput").ap())
    hybrid_kernel(nc, *args)
    r = _run(nc, [arrays], core_ids=[0])
    return r.results[0]["out_0_dram"]
```

```python
import concourse.bass as bass
from concourse import mybir
from contextlib import ExitStack

FP32 = mybir.dt.float32
INT32 = mybir.dt.int32
ALU = mybir.AluOpType
ACT = mybir.ActivationFunctionType
AX = mybir.AxisListType

B, H, W, C = 4, 64, 64, 128
N = H * W
G, HC, TAPS = 4, 32, 9
E = 8
SCALE = HC ** -0.5
TILE = 128
TILES = N // TILE

ROWS, PCOLS = 8, 4
BANDS = H // ROWS
PATCHES = W // PCOLS
PIX = ROWS * PCOLS
WR, WC = ROWS + 2, PCOLS + 2
WIN = WR * WC
KEYS = TAPS * WIN // 5
BPX = ROWS * W

RP = W + 2
RAW = (H + 2) * RP
FAR = 8
WP = W + FAR
WIDE = (H + 2 * FAR) * WP + 16
BAND = WR * WP


CHAIN_A, CHAIN_B, CHAIN_O, CHAIN_C = 73, 34, 4, 68


ONE_PIXEL = 1.0


def view(ap, dims):
    return bass.AP(tensor=ap.tensor, offset=ap.offset, ap=[ap.ap[0]] + dims)


class Chain:

    def __init__(self, eng, sem, turn, per_turn):
        self.eng, self.sem, self.base, self.per_turn, self.n = eng, sem, turn * per_turn, per_turn, 0

    def did(self, ins):
        ins.then_inc(self.sem, 1)
        self.n += 1
        return self.n

    def after(self, n):
        self.eng.wait_ge(self.sem, self.base + n)

    def link(self, ins):
        self.after(self.did(ins))

    def close(self):
        assert self.n == self.per_turn, (self.n, self.per_turn)


def hybrid_kernel(nc, x, w_qkv, b_qkv, w_dw, b_dw, wp_off, w_off, b_off, wp_mask, w_mask, b_mask, w_proj, b_proj,
                  wa, ba, wr, br, we, be, c_ident, c_gavg, c_causal, c_grid, c_before, c_place, table, offs, attn, out):
    ctx = ExitStack()
    with ctx:
        def sb(name, shape, dt=FP32):
            return ctx.enter_context(nc.sbuf_tensor(name, shape, dt))

        def sem(name):
            return ctx.enter_context(nc.semaphore(name))

        ident = sb("ident", [128, 128])
        gavg = sb("gavg", [128, 128])
        grid = sb("grid", [128, WC + WR])
        before = sb("before", [128, E * E])
        place = sb("place", [128, 2 * TAPS + 1])
        wq_sb = sb("wq_sb", [128, 3 * C])
        bq_sb = sb("bq_sb", [128, 3])
        bn_sb = sb("bn_sb", [128, 3])
        dw_sb = sb("dw_sb", [128, 3, TAPS])
        db_sb = sb("db_sb", [128, 3])
        conv_w = sb("conv_w", [96, 3, 128])
        pass_w = sb("pass_w", [128, 128])
        ob_sb = sb("ob_sb", [128, 1])
        wproj_sb = sb("wproj_sb", [128, C])
        rows = sb("rows", [128, 2 * C + E])
        wa_sb = sb("wa_sb", [128, 3 * C])
        ba_sb = sb("ba_sb", [128, 2])
        wr_sb = sb("wr_sb", [128, E])
        we_sb = sb("we_sb", [128, E * C])
        be_sb = sb("be_sb", [E, C])
        big = sb("big", [128, 2 * N])
        xtok, xch = big[:, 0:N], big[:, N:2 * N]
        qpad = sb("qpad", [128, RAW])
        kwide = sb("kwide", [128, WIDE])
        vwide = sb("vwide", [128, WIDE])
        kband = sb("kband", [128, TAPS * BAND])
        vwin = sb("vwin", [128, (W + 2) * TAPS * WR])
        vband = sb("vband", [128, TAPS * BAND])
        diag = vband[:, 0:TAPS * 128].rearrange("p (t n) -> p t n", t=TAPS)
        wn_sb = vband[:, TAPS * 128:TAPS * 128 + 3 * C]
        raw = [kband[:, 0:RAW], vwin[:, 0:RAW]]
        qstack = sb("qstack", [96, WR * RP])
        offt = sb("offt", [128, BPX])
        HN = PATCHES * TAPS
        parts, at = {}, 0
        for name, n in (("hx", HN * WC), ("hy", HN * WR), ("rsum", HN * WR), ("hyw", HN * WR), ("gx", HN * WC),
                        ("prod", 2 * 6 * WIN), ("aband", BPX), ("offc", BPX), ("msk", HN), ("lg", HN),
                        ("small", 3 * PATCHES)):
            parts[name] = big[:, at:at + n]
            at += n
        assert at <= 2 * N
        hx, hy, rsum = parts["hx"], parts["hy"], parts["rsum"]
        hyw, gx = parts["hyw"], parts["gx"]
        prod = parts["prod"].rearrange("p (a n) -> p a n", a=2)
        aband, offc, msk, lg, small = (parts[n] for n in ("aband", "offc", "msk", "lg", "small"))
        qbd = sb("qbd", [128, PATCHES * 128])
        attbuf = sb("attbuf", [128, 2 * TAPS * WIN])
        att = attbuf[:, :].rearrange("p (a n) -> p a n", a=2)
        keysT = sb("keysT", [128, 2, 10 * 128])
        half = sb("half", [128, 4])
        offmax = sb("offmax", [128, 1 + BANDS])
        stats, mom = keysT[:, 0, 0:48].rearrange("p (m s) -> p m s", s=6), keysT[:, 0, 48:60]
        cbuf = [kwide[:, 0:5760], vwide[:, 0:5760], qpad[:, 0:4352]]
        x1, ln, lnT = cbuf[0][:, 0:512], cbuf[0][:, 512:1024], cbuf[0][:, 1024:1536]
        qk_raw, qk_exp, qk = cbuf[0][:, 1536:2560], cbuf[0][:, 2560:3584], cbuf[0][:, 3584:4608]
        ktok, pmask = cbuf[0][:, 4608:5120], cbuf[0][:, 5120:5632]
        vone, state = cbuf[1][:, 0:516], cbuf[1][:, 516:516 + 645]
        t1, acc, accb = cbuf[1][:, 1280:1792], cbuf[1][:, 1792:2304], cbuf[1][:, 2304:2816]
        ao = cbuf[1][:, 2816:3328]
        causal = cbuf[0][:, 5632:5760]
        wT = cbuf[1][0:E, 3328:3840]
        lstat, lmom, lrs = cbuf[1][:, 3840:3864], cbuf[1][:, 3864:3872], cbuf[1][:, 3872:3880]
        den = cbuf[1][:, 3880:3884]
        rl, re_, rsel, rw = (cbuf[1][:, 3900 + 32 * i:3932 + 32 * i] for i in range(4))
        rsm = cbuf[1][:, 4032:4040]
        gt, eq = cbuf[1][:, 4096:4352], cbuf[1][:, 4352:4608]

        f_corner, f_part, f_sample = kband[:, 0:2304], kband[:, 2304:4608], kband[:, 4608:5184]
        f_off, f_q, f_qT = vband[:, 0:512], vband[:, 512:544], vband[:, 544:576]
        f_in, f_out = vband[:, 576:704], vband[:, 704:832]
        f_o, f_oT = vband[:, 832:864], vband[:, 864:896]
        f_pos, f_low, f_frac, f_tmp = (vband[:, 900 + 18 * n:918 + 18 * n] for n in range(4))
        f_edge, f_wt = vband[:, 1000:1036], vband[:, 1040:1076]
        f_int, f_idx = vband[:, 1080:1098].bitcast(INT32), vband[:, 1100:1136].bitcast(INT32)
        f_flat, f_cw = vband[:, 1140:1176], vband[:, 1180:1216]
        f_mask, f_lg, f_s = vband[:, 1220:1229], vband[:, 1230:1239], vband[:, 1240:1244]
        f_at = vband[:, 1250:1252]
        flag = sb("flag", [1, 2], INT32)

        P = [ctx.enter_context(nc.psum_tensor(f"P{i}", [128, 512], FP32)) for i in range(8)]

        s_hold = sem("s_hold")
        w_in = sem("w_in")
        s_zero, s_setup_pe, s_setup_cp, s_ready = sem("s_zero"), sem("s_setup_pe"), sem("s_setup_cp"), sem("s_ready")
        done_a, done_b, done_c = sem("done_a"), sem("done_b"), sem("done_c")
        x_in = [sem(f"x_in{j}") for j in range(4)]
        xT_ready, xT_copied, xT_stated = sem("xT_ready"), sem("xT_copied"), sem("xT_stated")
        moments, groups, norm, wnorm, biasmm, bias_ok = (sem(n) for n in
            ("moments", "groups", "norm", "wnorm", "biasmm", "bias_ok"))
        raw_zero, qkv_ready, raw_ready, q_conv = sem("raw_zero"), sem("qkv_ready"), sem("raw_ready"), sem("q_conv")
        vconv_ready, v_ready = sem("vconv_ready"), sem("v_ready")
        diag_ready = sem("diag_ready")
        gvar_ready, gstd_ready, var_ready, std_ready = sem("gvar_ready"), sem("gstd_ready"), sem("var_ready"), sem("std_ready")
        dve_o = sem("dve_o")
        dve_a, dve_b, dve_c = sem("dve_a"), sem("dve_b"), sem("dve_c")
        q_in, k_in, v_in = sem("q_in"), [sem(f"k_in{ky}") for ky in range(3)], sem("v_in")
        v_packed = sem("v_packed")
        off_mm, offc_ready, offt_ready, diff_ready, hat_ready = (sem(n) for n in
            ("off_mm", "offc_ready", "offt_ready", "diff_ready", "hat_ready"))
        absd, mexp, mask_ready, qbd_ready = sem("absd"), sem("mexp"), sem("mask_ready"), sem("qbd_ready")
        s_mm, s_used = sem("s_mm"), sem("s_used")
        lg_ready, p_ready, gx_ready, a_dve, a_pool = (sem(n) for n in ("lg_ready", "p_ready", "gx_ready", "a_dve", "a_pool"))
        t_ready, t_copied, o_ready, o_copied = sem("t_ready"), sem("t_copied"), sem("o_ready"), sem("o_copied")
        xr_in, causal_in, ao_in, st_out = sem("xr_in"), sem("causal_in"), sem("ao_in"), sem("st_out")
        a_kept, hyw_ready, hx_ready = sem("a_kept"), sem("hyw_ready"), sem("hx_ready")
        peak_ok = sem("peak_ok")
        off_kept, peak_ready, peak_row, flag_ready, done_f = (sem(n) for n in
            ("off_kept", "peak_ready", "peak_row", "flag_ready", "done_f"))
        (f_chain, f_turned, f_stored, f_table, f_off_in, f_mexp, f_masked, f_ready, f_gather, f_gathered, f_lgr, f_exp,
         f_used) = (sem(n) for n in ("f_chain f_turned f_stored f_table f_off_in f_mexp f_masked f_ready f_gather "
                                     "f_gathered f_lgr f_exp f_used").split())
        turn_done = sem("turn_done")
        (proj_ready, ln_ready, lnT_ready, lnT_copied, qkv_c, qk_biased, clip_ready, exp_ready, qk_ready, v_c, kt_ready,
         kt_copied, st_ready, pm_ready, delta_ready, state_ready, num_ready, ln2_ready, ln2T_ready, ln2T_copied,
         route_ready, logit_ready, rexp_ready, gate_ready, gateT_ready, gateT_copied, bias_c, ex_ready, ex_used) = (
            sem(n) for n in ("proj_ready ln_ready lnT_ready lnT_copied qkv_c qk_biased clip_ready exp_ready qk_ready "
                             "v_c kt_ready kt_copied st_ready pm_ready delta_ready state_ready num_ready ln2_ready "
                             "ln2T_ready ln2T_copied route_ready logit_ready rexp_ready gate_ready gateT_ready "
                             "gateT_copied bias_c ex_ready ex_used").split())

        block = ctx.enter_context(nc.Block())

        def hold(eng):
            eng.sem_inc(s_hold, 1)

        x_tok = x.rearrange("b h w c -> (b h w) c")
        out_tok = out.rearrange("b h w c -> (b h w) c")
        wide_at = lambda y, xx: (y + FAR) * WP + xx + FAR

        loads = [
            (ident[:, :], c_ident), (gavg[:, :], c_gavg), (grid[:, :], c_grid),
            (before[:, :], c_before), (place[:, :], c_place),
            (wq_sb[:, :], w_qkv), (bq_sb[:, :], b_qkv.rearrange("(c p) -> p c", p=128)),
            (dw_sb[:, :, :], w_dw.rearrange("(c p) i a b -> p c (i a b)", p=128)),
            (db_sb[:, :], b_dw.rearrange("(c p) -> p c", p=128)),
            (wproj_sb[:, :], w_proj), (ba_sb[:, :], ba[0:2 * C].rearrange("(c p) -> p c", p=128)),
            (wr_sb[:, :], wr), (we_sb[:, :].rearrange("p (e c) -> p e c", e=E), we.rearrange("e d c -> d e c")),
            (be_sb[:, :], be),
        ]
        s_wpo = kband[0:32, 0:G * 32 * TAPS].rearrange("o (g i t) -> o g i t", g=G, t=TAPS)
        s_wpm = kband[0:32, 1152:1152 + 288].rearrange("o (i t) -> o i t", t=TAPS)
        s_w1 = kband[:, 1536:1664]
        s_wa = kband[:, 1664:2048].rearrange("p (c i) -> p c i", c=3)
        s_row = kband[0:1, 2048:2048 + 2 * C + E]
        s_one = kband[0:1, 2432:2560]
        s_w1T = kband[:, 2560:2688]
        loads += [(s_wpo, wp_off.rearrange("g o i a b -> o g i (a b)")),
                  (s_wpm, wp_mask.rearrange("o i a b -> o i (a b)")),
                  (s_wa, wa.rearrange("(c p) i -> p c i", p=128)),
                  (s_row[:, 0:C], b_proj.rearrange("(a n) -> a n", a=1)),
                  (s_row[:, C:2 * C], ba[2 * C:3 * C].rearrange("(a n) -> a n", a=1)),
                  (s_row[:, 2 * C:], br.rearrange("(a n) -> a n", a=1))]
        late = []
        for g in range(G):
            late += [(s_w1[32 * g:32 * g + 18, :], w_off[g]), (s_w1[32 * g + 18:32 * g + 27, :], w_mask),
                     (ob_sb[32 * g:32 * g + 18, :], b_off[g].rearrange("(n a) -> n a", a=1)),
                     (ob_sb[32 * g + 18:32 * g + 27, :], b_mask.rearrange("(n a) -> n a", a=1))]
        UNITS = 24
        OFFSETS_AT, SOFTMAX_AT = 5, 13
        BAND_IN = 16 * 3 * G
        ALL_IN = 16 * (len(loads) + len(late))

        def pipeline(eng, body):
            body(None, None, 0)
            body(None, 0, 1)
            with eng.Fori(0, BANDS - 2) as i:
                body(i, i + 1, i + 2)
            body(BANDS - 2, BANDS - 1, None)
            body(BANDS - 1, None, None)

        def weigh(eng, s):
            return eng.tensor_tensor(
                view(att[:, s % 2, 0:1], [[TAPS * WR, WC], [WR, TAPS], [1, WR]]),
                view(gx[:, s * TAPS * WC:s * TAPS * WC + 1], [[1, WC], [WC, TAPS], [0, WR]]),
                view(hyw[:, s * TAPS * WR:s * TAPS * WR + 1], [[0, WC], [WR, TAPS], [1, WR]]), ALU.mult)

        def shifted(eng, i, ky, wide, dst, load):
            for g in range(G):
                d = 2 * g + 1
                start = wide_at(-1 + d * (ky - 1), -1 - d)
                eng.dma_start(dst[32 * g:32 * g + 32, :].rearrange("p (c n) -> p c n", c=3),
                              view(wide[32 * g:32 * g + 32, bass.ds(i * (ROWS * WP) + start, 1)],
                                   [[d, 3], [1, BAND]])).then_inc(load, 16)

        @block.sync
        def _(sp):
            sp.sem_inc(st_out, 16)
            sp.sem_inc(off_kept, 16)
            sp.sem_inc(a_kept, 16)
            for dst, src in loads:
                sp.dma_start(dst, src, allow_slow_non_contiguous=True).then_inc(w_in, 16)
            sp.wait_ge(s_zero, 1)
            for dst, src in late:
                sp.dma_start(dst, src, allow_slow_non_contiguous=True).then_inc(w_in, 16)
            sp.wait_ge(s_ready, 1)
            with sp.Fori(0, B) as b:
                for j in range(4):
                    src = x_tok[bass.ds(b * N + j * N // 4, N // 4), :].rearrange("(t p) c -> p t c", p=128)
                    dst = xtok[:, j * 1024:(j + 1) * 1024].rearrange("p (t c) -> p t c", c=C)
                    sp.dma_start(dst, src).then_inc(x_in[j], 16)
                sp.sem_inc(done_a, 1)
                sp.wait_ge(done_a, b * 5 + 5)
                hold(sp)
                def sp_body(v, s, o):
                    def keys(ky):
                        sp.wait_ge(s_used, t * UNITS + 8 * (ky + 1))
                        hold(sp)
                        shifted(sp, o, ky, kwide, kband[:, 3 * ky * BAND:3 * (ky + 1) * BAND], k_in[ky])

                    if o is not None:
                        t = b * BANDS + o
                        sp.wait_ge(off_mm, t + 1)
                        hold(sp)
                        for kx in range(3):
                            sp.dma_start(qstack[32 * kx:32 * kx + 32, 0:WR * RP - 2],
                                         qpad[0:32, bass.ds(o * (ROWS * RP) + kx, WR * RP - 2)]).then_inc(q_in, 16)
                        keys(0)
                        sp.wait_ge(offt_ready, t + 1)
                        hold(sp)
                        sp.dma_start(offs[bass.ds(o * 128, 128), :], offt[:, :]).then_inc(off_kept, 16)
                        keys(1)
                        keys(2)
                        sp.wait_ge(v_packed, t * 8 + 1)
                        hold(sp)
                        for ky in range(3):
                            shifted(sp, o, ky, vwide, vband[:, 3 * ky * BAND:3 * (ky + 1) * BAND], v_in)
                    if v is not None:
                        t = b * BANDS + v
                        sp.wait_ge(o_copied, t * 4 + 4)
                        hold(sp)
                        sp.dma_start(attn[:, bass.ds(v * BPX, BPX)], aband).then_inc(a_kept, 16)

                pipeline(sp, sp_body)
                sp.wait_ge(a_kept, b * (16 * BANDS) + 16 * BANDS + 16)
                hold(sp)
                sp.wait_ge(off_kept, b * (16 * BANDS) + 16 * BANDS + 16)
                hold(sp)
                sp.sem_inc(done_b, 1)
                sp.wait_ge(done_b, b * 5 + 5)
                hold(sp)
                sp.sem_inc(done_f, 1)
                sp.wait_ge(done_f, b * 5 + 5)
                hold(sp)
                sp.dma_start(causal, c_causal).then_inc(causal_in, 16)
                with sp.Fori(0, BANDS) as u:
                    t = b * BANDS + u
                    sp.wait_ge(turn_done, t + 1)
                    hold(sp)
                    sp.dma_start(ao, attn[:, bass.ds(u * 512, 512)]).then_inc(ao_in, 16)
                    src = x_tok[bass.ds(b * N + u * 512, 512), :].rearrange("(t p) c -> p t c", p=128)
                    sp.dma_start(x1.rearrange("p (t c) -> p t c", c=C), src).then_inc(xr_in, 16)
                    sp.wait_ge(turn_done, t + 2)
                    hold(sp)
                    dst = out_tok[bass.ds(b * N + u * 512, 512), :].rearrange("(t p) c -> p t c", p=128)
                    sp.dma_start(dst, acc.rearrange("p (t c) -> p t c", c=C)).then_inc(st_out, 16)
                sp.wait_ge(st_out, b * (16 * BANDS) + 16 * BANDS + 16)
                hold(sp)
                sp.sem_inc(done_c, 1)
                sp.wait_ge(done_c, b * 5 + 5)
                hold(sp)

        @block.gpsimd
        def _(pool):
            nc.gpsimd.memset(s_w1, 0.0)
            nc.gpsimd.memset(s_one, 1.0)
            nc.gpsimd.memset(half[:, :], -0.5)
            nc.gpsimd.memset(ob_sb[:, :], 0.0)
            nc.gpsimd.memset(qpad[:, :], 0.0)
            nc.gpsimd.memset(kwide[:, :], 0.0)
            nc.gpsimd.memset(vwide[:, :], 0.0)
            nc.gpsimd.memset(qbd[:, :], 0.0)
            pool.drain().then_inc(s_zero, 1)
            pool.sem_inc(v_packed, 1)
            pool.wait_ge(s_ready, 1)
            with pool.Fori(0, B) as b:
                for r in (*raw, kwide[:, :], vwide[:, :]):
                    nc.gpsimd.memset(r, 0.0).then_inc(raw_zero, 1)
                pool.wait_ge(gvar_ready, b + 1)
                nc.gpsimd.tensor_tensor(mom[:, 6:7], mom[:, 6:7], half[:, 0:1], ALU.pow).then_inc(gstd_ready, 1)
                pool.drain().then_inc(done_a, 1)
                pool.wait_ge(done_a, b * 5 + 5)
                hold(pool)
                def distances(s, dst, n, at, axis):
                    for ky in range(3):
                        ins = nc.gpsimd.tensor_tensor(
                            view(dst[:, ky * 48 * n:ky * 48 * n + 1], [[3 * n, PATCHES], [n, 3], [1, n]]),
                            view(grid[:, at:at + 1], [[0, PATCHES], [0, 3], [1, n]]),
                            view(offt[:, 6 * ky + axis:6 * ky + axis + 1], [[32, PATCHES], [2, 3], [0, n]]),
                            ALU.subtract)
                    ins.then_inc(diff_ready, 1)

                def pool_body(v, s, o):
                    if s is not None:
                        pool.wait_ge(offt_ready, b * BANDS + s + 1)
                        if v is not None:
                            pool.wait_ge(gx_ready, b * BANDS + s)
                        distances(s, hx, WC, 0, 1)
                    for m in range(8):
                        if v is not None:
                            t = b * BANDS + v
                            if m == 0:
                                pool.wait_ge(gx_ready, t + 1)
                                pool.wait_ge(hyw_ready, t + 2)
                            else:
                                pool.wait_ge(t_ready, t * (3 * PATCHES) + 6 * m)
                            weigh(nc.gpsimd, 2 * m + 1).then_inc(a_pool, 1)
                        if s is not None and m == 0:
                            pool.wait_ge(hyw_ready, b * BANDS + s + 1)
                            distances(s, hy, WR, WC, 0)
                        if s is not None and m:
                            pack(s, m - 1)
                    if s is not None:
                        if v is not None:
                            pool.wait_ge(t_ready, (b * BANDS + v) * (3 * PATCHES) + 3 * PATCHES)
                            hold(pool)
                        pack(s, 7)

                def pack(s, c):
                    if c == 0:
                        pool.wait_ge(v_in, (b * BANDS + s) * BAND_IN + BAND_IN)
                        hold(pool)
                    n = 8 if c < 7 else 10
                    nc.gpsimd.tensor_copy(
                        view(vwin[:, 8 * c * TAPS * WR:8 * c * TAPS * WR + 1], [[TAPS * WR, n], [WR, TAPS], [1, WR]]),
                        view(vband[:, 8 * c:8 * c + 1], [[1, n], [BAND, TAPS], [WP, WR]])).then_inc(v_packed, 1)

                pipeline(pool, pool_body)
                pool.drain().then_inc(done_b, 1)
                pool.wait_ge(done_b, b * 5 + 5)
                pool.wait_ge(flag_ready, b + 1)
                hold(pool)
                with pool.If(pool.value_load(flag[0:1, 0:1], min_val=0, max_val=1) != 0):
                    with pool.Fori(0, H) as y:
                        pool.wait_ge(f_turned, 1)
                        pool.sem_clear(f_turned)
                        for g in range(G):
                            dst = table.rearrange("(n g) e -> g n e", g=G)[g, bass.ds(y * W, W), :]
                            pool.dma_start(dst.rearrange("(j p) e -> p j e", p=32),
                                           f_out[32 * g:32 * g + 32, :].rearrange("p (j e) -> p j e", j=2)).then_inc(f_stored, 16)
                        pool.wait_ge(f_stored, 16 * G)
                        pool.dma_reset(range(f_stored.num, f_stored.num + 1))
                        pool.sem_clear(f_stored)
                        pool.sem_inc(f_table, 1)
                    with pool.Fori(0, BANDS) as i:
                        pool.dma_start(f_off, offs[bass.ds(i * 128, 128), :]).then_inc(f_stored, 16)
                        pool.wait_ge(f_stored, 16)
                        pool.dma_reset(range(f_stored.num, f_stored.num + 1))
                        pool.sem_clear(f_stored)
                        pool.sem_inc(f_off_in, 1)
                        with pool.Fori(0, PATCHES):
                            pool.wait_ge(f_ready, 1)
                            pool.sem_clear(f_ready)
                            for k in range(4 * TAPS):
                                pool.indirect_dma_start(
                                    out=f_corner[:, 64 * k:64 * k + 64], out_offset=None, in_=table,
                                    in_offset=bass.IndirectOffsetOnAxis(ap=f_idx[:, k:k + 1], axis=0)).then_inc(f_gather, 16)
                            pool.wait_ge(f_gather, 16 * 4 * TAPS)
                            pool.dma_reset(range(f_gather.num, f_gather.num + 1))
                            pool.sem_clear(f_gather)
                            pool.sem_inc(f_gathered, 1)
                        pool.wait_ge(f_used, 1)
                        pool.sem_clear(f_used)
                        pool.dma_start(attn[:, bass.ds(i * BPX, BPX)], aband).then_inc(f_stored, 16)
                        pool.wait_ge(f_stored, 16)
                        pool.dma_reset(range(f_stored.num, f_stored.num + 1))
                        pool.sem_clear(f_stored)
                pool.drain().then_inc(done_f, 1)
                pool.wait_ge(done_f, b * 5 + 5)
                hold(pool)
                with pool.Fori(0, BANDS) as u:
                    t = b * BANDS + u
                    for k in range(2):
                        pool.wait_ge(var_ready, t * 2 + k + 1)
                        nc.gpsimd.tensor_tensor(lrs[:, 0:4], lrs[:, 0:4], half[:, :], ALU.pow).then_inc(std_ready, 1)
                pool.drain().then_inc(done_c, 1)
                pool.wait_ge(done_c, b * 5 + 5)
                hold(pool)

        @block.tensor
        def _(pe):
            mm = nc.tensor.matmul

            pe.wait_ge(w_in, ALL_IN)
            nc.tensor.transpose(P[0][:, 0:128], s_w1, ident[:, :])
            for c in range(3):
                nc.tensor.transpose(P[1][:, 128 * c:128 * c + 128], s_wa[:, c, :], ident[:, :])
            mm(P[2][:, 0:2 * C + E], s_one, s_row, start=True, stop=True)
            pe.drain().then_inc(s_setup_pe, 1)
            pe.wait_ge(s_setup_cp, 2)
            for t in range(TAPS):
                ky, kx = divmod(t, 3)
                for g in range(G):
                    o = P[3][32 * kx:32 * kx + 32, ky * 128 + 32 * g:ky * 128 + 32 * g + 32]
                    mm(o[:, 0:18], s_wpo[:, g, :, t], s_w1T[0:32, 32 * g:32 * g + 18], start=True, stop=True)
                    mm(o[:, 18:32], s_wpm[:, :, t], s_w1T[0:32, 32 * g + 18:32 * g + 32], start=True, stop=True)
            pe.drain().then_inc(s_setup_pe, 1)
            pe.sem_inc(off_mm, 1)
            pe.wait_ge(s_ready, 1)

            with pe.Fori(0, B) as b:
                for m in range(8):
                    if m % 2 == 0:
                        pe.wait_ge(x_in[m // 2], b * 16 + 16)
                    if m >= 2:
                        pe.wait_ge(xT_copied, b * 8 + m - 1)
                    for j in range(4):
                        ins = nc.tensor.transpose(P[m % 2][:, 128 * j:128 * j + 128],
                                                  xtok[:, (4 * m + j) * C:(4 * m + j + 1) * C], ident[:, :])
                    ins.then_inc(xT_ready, 1)
                pe.wait_ge(moments, b + 1)
                mm(P[7][:, 0:2], gavg[:, :], mom[:, 2:4], start=True, stop=True).then_inc(groups, 1)
                pe.wait_ge(norm, b + 1)
                for c in range(3):
                    ins = mm(P[6][:, c:c + 1], wq_sb[:, c * C:c * C + C], mom[:, 7:8], start=True, stop=True)
                ins.then_inc(biasmm, 1)
                pe.wait_ge(wnorm, b + 1)
                pe.wait_ge(xT_copied, b * 8 + 8)
                for c in range(3):
                    for n in range(8):
                        k = c * 8 + n
                        if k >= 2:
                            pe.wait_ge(raw_ready, b * 24 + k - 1)
                        mm(P[2 + k % 2][:, :], wn_sb[:, c * C:c * C + C], xch[:, 512 * n:512 * n + 512],
                           start=True, stop=True).then_inc(qkv_ready, 1)
                r3 = raw[0].rearrange("p (y x) -> p y x", x=RP)
                pe.wait_ge(diag_ready, b + 1)
                pe.wait_ge(raw_ready, b * 24 + 24)
                for n in range(8):
                    if n >= 2:
                        pe.wait_ge(v_ready, b * 8 + n - 1)
                    for t in range(TAPS):
                        ky, kx = divmod(t, 3)
                        ins = mm(P[4 + n % 2][:, :], diag[:, t, :], r3[:, 8 * n + ky:8 * n + ky + 8, kx:kx + W],
                                 start=t == 0, stop=t == TAPS - 1)
                    ins.then_inc(vconv_ready, 1)
                pe.drain().then_inc(done_a, 1)
                pe.wait_ge(done_a, b * 5 + 5)
                hold(pe)

                def turn(t, s):
                    if s % 2 == 0:
                        pe.wait_ge(a_dve, t * 8 + s // 2 + 1)
                        pe.wait_ge(v_packed, t * 8 + min(s // 2 + 2, 8) + 1)
                    else:
                        pe.wait_ge(a_pool, t * 8 + s // 2 + 1)
                    jobs = [[("a", k) for k in range(4)], [("v", k) for k in range(4)], [("a", 4), ("v", 4)]]
                    for k, job in enumerate(jobs):
                        if s > 0:
                            pe.wait_ge(t_copied, t * (3 * PATCHES) + 3 * s + k - 1)
                        for c, (what, part) in enumerate(job):
                            if what == "a":
                                src = att[:, s % 2, KEYS * part:KEYS * (part + 1)]
                            else:
                                at = PCOLS * s * TAPS * WR + KEYS * part
                                src = vwin[:, at:at + KEYS]
                            ins = nc.tensor.transpose(P[4 + k][0:KEYS, 128 * c:128 * c + 128], src, ident[:, :])
                        ins.then_inc(t_ready, 1)

                def mix(t, s):
                    pe.wait_ge(t_copied, t * (3 * PATCHES) + 3 * s + 4)
                    if s % 4 == 0 and s:
                        pe.wait_ge(o_copied, t * 4 + s // 4)
                    for pair in range(5):
                        ins = mm(P[7][:, 128 * (s % 4):128 * (s % 4) + 128],
                                 keysT[0:KEYS, s % 2, 128 * (5 + pair):128 * (6 + pair)],
                                 keysT[0:KEYS, s % 2, 128 * pair:128 * pair + 128], start=pair == 0, stop=pair == 4)
                    ins.then_inc(o_ready, 1)

                def score(t, u):
                    ky, pair = divmod(u, 8)
                    if pair == 0:
                        pe.wait_ge(k_in[ky], t * 16 * G + 16 * G)
                    pe.wait_ge(s_used, t * UNITS + u + UNITS - 2)
                    for h in range(2):
                        s = 2 * pair + h
                        keys = view(kband[:, 3 * ky * BAND + PCOLS * s:3 * ky * BAND + PCOLS * s + 1],
                                    [[BAND, 3], [WP, WR], [1, WC]])
                        ins = mm(P[u % 3][:, 3 * WIN * h:3 * WIN * (h + 1)], qbd[:, 128 * s:128 * s + 128], keys,
                                 start=True, stop=True)
                    ins.then_inc(s_mm, 1)

                def pe_body(v, s, o):
                    for j in range(PATCHES):
                        if v is not None:
                            turn(b * BANDS + v, j)
                        if s is not None and j == 1:
                            pe.wait_ge(qbd_ready, (b * BANDS + s) * 4 + 4)
                        if s is not None and 1 <= j <= UNITS // 2:
                            score(b * BANDS + s, 2 * j - 2)
                            score(b * BANDS + s, 2 * j - 1)
                        if v is not None and j:
                            mix(b * BANDS + v, j - 1)
                        if o is not None and j == OFFSETS_AT:
                            pe.wait_ge(q_in, (b * BANDS + o) * 48 + 48)
                            hold(pe)
                            for ky in range(3):
                                mm(P[3][:, :], conv_w[:, ky, :], view(qstack[:, ky * RP:ky * RP + 1],
                                   [[PCOLS, PATCHES], [RP, ROWS], [1, PCOLS]]), start=ky == 0, stop=False)
                            mm(P[3][:, :], pass_w[:, :], view(qpad[:, bass.ds(o * (ROWS * RP) + RP + 1, 1)],
                               [[PCOLS, PATCHES], [RP, ROWS], [1, PCOLS]]), start=False, stop=True).then_inc(off_mm, 1)
                    if v is not None:
                        mix(b * BANDS + v, PATCHES - 1)

                pipeline(pe, pe_body)
                pe.drain().then_inc(done_b, 1)
                pe.wait_ge(done_b, b * 5 + 5)
                hold(pe)
                pe.wait_ge(peak_ready, b + 1)
                mm(P[0][0:1, 0:128], offmax[:, 0:1], ident[:, :], start=True, stop=True).then_inc(peak_row, 1)
                pe.drain().then_inc(done_f, 1)
                pe.wait_ge(done_f, b * 5 + 5)
                hold(pe)

                with pe.Fori(0, BANDS) as u:
                    t = b * BANDS + u
                    q4 = lambda a, j: a[:, 128 * j:128 * j + 128]
                    pe.wait_ge(ao_in, t * 16 + 16)
                    for j in range(4):
                        ins = mm(q4(P[0], j), q4(ao, j), wproj_sb[:, :], start=True, stop=True)
                    ins.then_inc(proj_ready, 1)
                    pe.wait_ge(ln_ready, t + 1)
                    for j in range(4):
                        ins = nc.tensor.transpose(q4(P[1], j), q4(ln, j), ident[:, :])
                    ins.then_inc(lnT_ready, 1)
                    pe.wait_ge(lnT_copied, t + 1)
                    mm(P[2][:, :], wa_sb[:, 0:C], lnT, start=True, stop=True)
                    mm(P[3][:, :], wa_sb[:, C:2 * C], lnT, start=True, stop=True).then_inc(qkv_c, 1)
                    for j in range(4):
                        ins = mm(q4(P[4], j), q4(lnT, j), wa_sb[:, 2 * C:3 * C], start=True, stop=True)
                    ins.then_inc(qkv_c, 1)
                    pe.wait_ge(qk_ready, t + 1)
                    for j in range(4):
                        ins = nc.tensor.transpose(q4(P[5], j), q4(qk[:, 512:1024], j), ident[:, :])
                    ins.then_inc(kt_ready, 1)
                    for j in range(4):
                        ins = mm(q4(P[6], j), q4(qk[:, 512:1024], j), q4(qk[:, 0:512], j), start=True, stop=True)
                    ins.then_inc(st_ready, 1)
                    pe.wait_ge(kt_copied, t + 1)
                    pe.wait_ge(v_c, t + 1)
                    vj = lambda j: vone[:, 129 * j:129 * j + 129]
                    sj = lambda j: state[:, 129 * j:129 * j + 129]
                    for j in range(4):
                        ins = mm(P[j // 2][:, 256 * (j % 2):256 * (j % 2) + 129], q4(ktok, j), vj(j), start=True, stop=True)
                    ins.then_inc(delta_ready, 1)
                    pe.wait_ge(pm_ready, t + 1)
                    pe.wait_ge(state_ready, t + 1)
                    for j in range(4):
                        o = P[2 + j // 2][:, 256 * (j % 2):256 * (j % 2) + 129]
                        mm(o, q4(pmask, j), vj(j), start=True, stop=False)
                        ins = mm(o, q4(qk[:, 0:512], j), sj(j), start=False, stop=True)
                    ins.then_inc(num_ready, 1)
                    pe.wait_ge(ln2_ready, t + 1)
                    for j in range(4):
                        ins = nc.tensor.transpose(q4(P[4], j), q4(ln, j), ident[:, :])
                    ins.then_inc(ln2T_ready, 1)
                    pe.wait_ge(ln2T_copied, t + 1)
                    for j in range(4):
                        ins = mm(P[5][:, E * j:E * j + E], q4(lnT, j), wr_sb[:, :], start=True, stop=True)
                    ins.then_inc(route_ready, 1)

                    def experts(j):
                        for h in range(2):
                            ins = mm(P[2 * (j % 2) + h][:, :], q4(lnT, j), we_sb[:, 512 * h:512 * h + 512], start=True, stop=True)
                        ins.then_inc(ex_ready, 1)

                    experts(0)
                    experts(1)
                    pe.wait_ge(gate_ready, t + 1)
                    for j in range(4):
                        ins = mm(P[6][0:E, 128 * j:128 * j + 128], rw[:, E * j:E * j + E], ident[:, :], start=True, stop=True)
                    ins.then_inc(gateT_ready, 1)
                    pe.wait_ge(gateT_copied, t + 1)
                    for j in range(4):
                        ins = mm(q4(P[7], j), wT[:, 128 * j:128 * j + 128], be_sb[:, :], start=True, stop=True)
                    ins.then_inc(bias_c, 1)
                    for j in range(2, 4):
                        pe.wait_ge(ex_used, t * 4 + j - 1)
                        experts(j)
                pe.drain().then_inc(done_c, 1)
                pe.wait_ge(done_c, b * 5 + 5)
                hold(pe)

        @block.scalar
        def _(act):
            A = nc.scalar.activation
            act.wait_ge(s_setup_pe, 1)
            A(rows[:, :], P[2][:, 0:2 * C + E], ACT.Copy)
            A(wa_sb[:, :], P[1][:, 0:3 * C], ACT.Copy)
            act.wait_ge(s_zero, 1)
            act.drain().then_inc(s_setup_cp, 1)
            act.sem_inc(t_copied, 1)
            act.sem_inc(hyw_ready, 1)
            act.wait_ge(s_ready, 1)
            with act.Fori(0, B) as b:
                for m in range(8):
                    act.wait_ge(xT_ready, b * 8 + m + 1)
                    A(xch[:, 512 * m:512 * m + 512], P[m % 2][:, :], ACT.Copy).then_inc(xT_copied, 1)
                act.wait_ge(raw_zero, b * 4 + 4)
                act.wait_ge(bias_ok, b + 1)
                for c in range(3):
                    r3 = raw[c % 2].rearrange("p (y x) -> p y x", x=RP)
                    if c == 2:
                        act.wait_ge(q_conv, b * 4 + 4)
                    for n in range(8):
                        act.wait_ge(qkv_ready, b * 24 + c * 8 + n + 1)
                        A(r3[:, 8 * n + 1:8 * n + 9, 1:W + 1], P[2 + n % 2][:, :].rearrange("p (y x) -> p y x", x=W),
                          ACT.Identity, bias=bn_sb[:, c:c + 1]).then_inc(raw_ready, 1)
                for n in range(8):
                    act.wait_ge(vconv_ready, b * 8 + n + 1)
                    A(view(vwide[:, wide_at(8 * n, 0):wide_at(8 * n, 0) + 1], [[WP, 8], [1, W]]),
                      P[4 + n % 2][:, :].rearrange("p (y x) -> p y x", x=W),
                      ACT.Identity, bias=db_sb[:, 2:3]).then_inc(v_ready, 1)
                act.drain().then_inc(done_a, 1)
                act.wait_ge(done_a, b * 5 + 5)
                hold(act)

                def act_body(v, s, o):
                    def hats(n, dst, ready):
                        t = b * BANDS + s
                        act.wait_ge(diff_ready, t * 2 + n)
                        A(dst, dst, ACT.Abs).then_inc(absd, 1)
                        act.wait_ge(absd, t * 2 + n)
                        A(dst, dst, ACT.Relu, bias=1.0, scale=-1.0).then_inc(ready, 1)

                    if s is not None:
                        hats(1, hx, hx_ready)
                    for j in range(PATCHES):
                        if v is not None:
                            t = b * BANDS + v
                            for k in range(3):
                                act.wait_ge(t_ready, t * (3 * PATCHES) + 3 * j + k + 1)
                                if k == 0 and j >= 2:
                                    act.wait_ge(o_ready, t * PATCHES + j - 1)
                                if k < 2:
                                    A(keysT[0:KEYS, j % 2, 640 * k:640 * k + 512], P[4 + k][0:KEYS, :],
                                      ACT.Copy).then_inc(t_copied, 1)
                                else:
                                    A(view(keysT[0:KEYS, j % 2, 512:513], [[640, 2], [1, 128]]),
                                      P[6][0:KEYS, 0:256].rearrange("p (a n) -> p a n", a=2), ACT.Copy).then_inc(t_copied, 1)
                        if s is not None and j == 1:
                            act.wait_ge(offt_ready, b * BANDS + s + 1)
                            A(msk.rearrange("p (a s c) -> p a s c", a=3, c=3),
                              view(offt[:, 18:19], [[3, 3], [32, PATCHES], [1, 3]]), ACT.Exp, scale=-1.0).then_inc(mexp, 1)
                        if o is not None and j == OFFSETS_AT:
                            act.wait_ge(off_mm, b * BANDS + o + 2)
                            A(offc, P[3][:, :], ACT.Identity, bias=ob_sb[:, 0:1]).then_inc(offc_ready, 1)
                        if s is not None and j == OFFSETS_AT + 2:
                            hats(2, hy, hat_ready)
                        if s is not None and j == SOFTMAX_AT + 1:
                            act.wait_ge(lg_ready, b * BANDS + s + 1)
                            A(lg, lg, ACT.Exp).then_inc(p_ready, 1)
                        if o is not None and j == SOFTMAX_AT:
                            t = b * BANDS + o
                            if s is not None:
                                act.wait_ge(s_mm, t * UNITS)
                                hold(act)
                            for g in range(G):
                                q = slice(32 * g, 32 * g + 32)
                                A(view(qbd[q, 32 * g:32 * g + 1], [[128, PATCHES], [PCOLS, ROWS], [1, PCOLS]]),
                                  view(qpad[q, bass.ds(o * (ROWS * RP) + RP + 1, 1)],
                                       [[PCOLS, PATCHES], [RP, ROWS], [1, PCOLS]]),
                                  ACT.Copy, scale=SCALE).then_inc(qbd_ready, 1)
                    if s is not None:
                        t = b * BANDS + s
                        act.wait_ge(hat_ready, t + 1)
                        if v is not None:
                            act.wait_ge(a_dve, t * 8)
                            act.wait_ge(a_pool, t * 8)
                        for ky in range(3):
                            ins = A(view(hyw[:, 30 * ky:30 * ky + 1], [[90, PATCHES], [WR, 3], [1, WR]]),
                                    view(hy[:, 480 * ky:480 * ky + 1], [[30, PATCHES], [WR, 3], [1, WR]]), ACT.Copy)
                        ins.then_inc(hyw_ready, 1)

                pipeline(act, act_body)
                act.drain().then_inc(done_b, 1)
                act.wait_ge(done_b, b * 5 + 5)
                act.wait_ge(flag_ready, b + 1)
                hold(act)
                with act.If(act.value_load(flag[0:1, 0:1], min_val=0, max_val=1) != 0):
                    with act.Fori(0, BANDS):
                        with act.Fori(0, PATCHES):
                            act.wait_ge(f_masked, 1)
                            act.sem_clear(f_masked)
                            A(f_mask, f_mask, ACT.Exp, scale=-1.0).then_inc(f_mexp, 1)
                            act.wait_ge(f_lgr, 1)
                            act.sem_clear(f_lgr)
                            A(f_lg, f_lg, ACT.Exp).then_inc(f_exp, 1)
                act.drain().then_inc(done_f, 1)
                act.wait_ge(done_f, b * 5 + 5)
                hold(act)

                with act.Fori(0, BANDS) as u:
                    t = b * BANDS + u
                    act.wait_ge(lnT_ready, t + 1)
                    A(lnT, P[1][:, :], ACT.Copy).then_inc(lnT_copied, 1)
                    act.wait_ge(qkv_c, t * 2 + 1)
                    A(qk_raw[:, 0:512], P[2][:, :], ACT.Identity, bias=ba_sb[:, 0:1])
                    A(qk_raw[:, 512:1024], P[3][:, :], ACT.Identity, bias=ba_sb[:, 1:2]).then_inc(qk_biased, 1)
                    act.wait_ge(clip_ready, t + 1)
                    A(qk_exp, qk_exp, ACT.Exp).then_inc(exp_ready, 1)
                    act.wait_ge(kt_ready, t + 1)
                    A(ktok, P[5][:, :], ACT.Copy).then_inc(kt_copied, 1)
                    act.wait_ge(ln2T_ready, t + 1)
                    A(lnT, P[4][:, :], ACT.Copy).then_inc(ln2T_copied, 1)
                    act.wait_ge(logit_ready, t + 1)
                    A(re_, rl, ACT.Exp).then_inc(rexp_ready, 1)
                    act.wait_ge(gateT_ready, t + 1)
                    A(wT, P[6][0:E, :], ACT.Copy).then_inc(gateT_copied, 1)
                act.drain().then_inc(done_c, 1)
                act.wait_ge(done_c, b * 5 + 5)
                hold(act)

        @block.vector
        def _(dve):
            V = nc.vector

            def general_path(dve):
                count = [0]

                def link(ins):
                    ins.then_inc(f_chain, 1)
                    count[0] += 1
                    dve.wait_ge(f_chain, count[0])

                def unchain():
                    dve.sem_clear(f_chain)
                    count[0] = 0

                with dve.Fori(0, H) as y:
                    link(V.tensor_copy(f_in[:, 0:64], kwide[:, bass.ds(y * WP + wide_at(0, 0), W)]))
                    link(V.tensor_copy(f_in[:, 64:128], vwide[:, bass.ds(y * WP + wide_at(0, 0), W)]))
                    for n in range(2):
                        for j in range(2):
                            link(V.transpose(f_out[:, 64 * j + 32 * n:64 * j + 32 * n + 32],
                                             f_in[:, 64 * n + 32 * j:64 * n + 32 * j + 32]))
                    unchain()
                    dve.sem_inc(f_turned, 1)
                    dve.wait_ge(f_table, 1)
                    dve.sem_clear(f_table)
                two = lambda a, n: view(a[:, n:n + 1], [[18, 2], [1, TAPS]])
                link(V.memset(f_at, 0.0))
                unchain()
                with dve.Fori(0, BANDS) as i:
                    dve.wait_ge(f_off_in, 1)
                    dve.sem_clear(f_off_in)
                    with dve.Fori(0, PATCHES) as s:
                        link(V.tensor_copy(f_q.rearrange("p (r c) -> p r c", c=PCOLS),
                                           view(qpad[:, bass.ds(i * (ROWS * RP) + s * PCOLS + RP + 1, 1)],
                                                [[RP, ROWS], [1, PCOLS]])))
                        link(V.transpose(f_qT, f_q))
                        link(V.tensor_scalar(f_qT, f_qT, SCALE, None, ALU.mult))
                        link(V.tensor_copy(f_mask, f_off[:, bass.ds(s * 32 + 18, TAPS)]))
                        dve.sem_inc(f_masked, 1)
                        for n in range(2):
                            link(V.tensor_scalar(f_pos[:, TAPS * n:TAPS * n + TAPS], place[:, TAPS * n:TAPS * n + TAPS],
                                                 f_at[:, n:n + 1], None, ALU.add))
                            link(V.tensor_copy(f_tmp[:, TAPS * n:TAPS * n + TAPS],
                                               view(f_off[:, bass.ds(s * 32 + n, 1)], [[2, TAPS]])))
                        link(V.tensor_tensor(f_pos, f_pos, f_tmp, ALU.add))
                        link(V.tensor_scalar(f_pos, f_pos, -3.0, W + 3.0, ALU.max, ALU.min))
                        link(V.tensor_copy(f_int, f_pos))
                        link(V.tensor_copy(f_low, f_int))
                        link(V.tensor_tensor(f_tmp, f_low, f_pos, ALU.is_gt))
                        link(V.tensor_tensor(f_low, f_low, f_tmp, ALU.subtract))
                        link(V.tensor_tensor(f_frac, f_pos, f_low, ALU.subtract))
                        link(V.tensor_scalar(f_wt[:, 0:18], f_frac, -1.0, 1.0, ALU.mult, ALU.add))
                        link(V.tensor_copy(f_wt[:, 18:36], f_frac))
                        link(V.tensor_copy(f_edge[:, 0:18], f_low))
                        link(V.tensor_scalar(f_edge[:, 18:36], f_low, 1.0, None, ALU.add))
                        link(V.scalar_tensor_tensor(f_wt, f_edge, 0.0, f_wt, ALU.is_ge, ALU.mult))
                        link(V.scalar_tensor_tensor(f_wt, f_edge, W - 1.0, f_wt, ALU.is_le, ALU.mult))
                        link(V.tensor_scalar(f_edge, f_edge, 0.0, W - 1.0, ALU.max, ALU.min))
                        link(V.tensor_scalar(two(f_edge, 0), two(f_edge, 0), float(W), None, ALU.mult))
                        corner = lambda a, at: view(a[:, at:at + 1], [[4, TAPS], [1, 2]])
                        for sy in range(2):
                            ys = lambda a: view(a[:, 18 * sy:18 * sy + 1], [[1, TAPS], [0, 2]])
                            xs = lambda a: view(a[:, TAPS:TAPS + 1], [[1, TAPS], [18, 2]])
                            link(V.tensor_tensor(corner(f_cw, 2 * sy), ys(f_wt), xs(f_wt), ALU.mult))
                            link(V.tensor_tensor(corner(f_flat, 2 * sy), ys(f_edge), xs(f_edge), ALU.add))
                        link(V.tensor_scalar(f_flat, f_flat, float(G), place[:, 2 * TAPS:2 * TAPS + 1], ALU.mult, ALU.add))
                        link(V.tensor_copy(f_idx, f_flat))
                        dve.sem_inc(f_ready, 1)
                        dve.wait_ge(f_mexp, 1)
                        dve.sem_clear(f_mexp)
                        link(V.tensor_scalar(f_mask, f_mask, 1.0, None, ALU.add))
                        link(V.reciprocal(f_mask, f_mask))
                        dve.wait_ge(f_gathered, 1)
                        dve.sem_clear(f_gathered)
                        link(V.tensor_tensor(f_part.rearrange("p (k e) -> p k e", e=64),
                                             f_corner.rearrange("p (k e) -> p k e", e=64),
                                             view(f_cw[:, 0:1], [[1, 4 * TAPS], [0, 64]]), ALU.mult))
                        link(V.tensor_reduce(f_sample.rearrange("p (k e) -> p k e", e=64),
                                             view(f_part[:, 0:1], [[256, TAPS], [1, 64], [64, 4]]), AX.X, ALU.add))
                        link(V.tensor_tensor(f_sample.rearrange("p (k e) -> p k e", e=64),
                                             f_sample.rearrange("p (k e) -> p k e", e=64),
                                             view(f_mask[:, 0:1], [[1, TAPS], [0, 64]]), ALU.mult))
                        products = view(f_part[:, 0:1], [[32, TAPS], [1, 32]])
                        link(V.tensor_tensor(products, view(f_sample[:, 0:1], [[64, TAPS], [1, 32]]),
                                             view(f_qT[:, 0:1], [[0, TAPS], [1, 32]]), ALU.mult))
                        link(V.tensor_reduce(f_lg, products, AX.X, ALU.add))
                        link(V.tensor_reduce(f_s[:, 0:1], f_lg, AX.X, ALU.max))
                        link(V.tensor_scalar(f_lg, f_lg, f_s[:, 0:1], None, ALU.subtract))
                        dve.sem_inc(f_lgr, 1)
                        dve.wait_ge(f_exp, 1)
                        dve.sem_clear(f_exp)
                        link(V.tensor_reduce(f_s[:, 1:2], f_lg, AX.X, ALU.add))
                        link(V.reciprocal(f_s[:, 2:3], f_s[:, 1:2]))
                        link(V.tensor_scalar(f_lg, f_lg, f_s[:, 2:3], None, ALU.mult))
                        link(V.tensor_tensor(products, view(f_sample[:, 32:33], [[64, TAPS], [1, 32]]),
                                             view(f_lg[:, 0:1], [[1, TAPS], [0, 32]]), ALU.mult))
                        link(V.tensor_reduce(f_o, view(f_part[:, 0:1], [[1, 32], [32, TAPS]]), AX.X, ALU.add))
                        link(V.transpose(f_oT, f_o))
                        link(V.tensor_copy(view(aband[:, bass.ds(s * PCOLS, 1)], [[W, ROWS], [1, PCOLS]]),
                                           f_oT.rearrange("p (r c) -> p r c", c=PCOLS)))
                        link(V.tensor_scalar(f_at[:, 1:2], f_at[:, 1:2], float(PCOLS), None, ALU.add))
                        unchain()
                    link(V.tensor_scalar(f_at[:, 0:1], f_at[:, 0:1], float(ROWS), None, ALU.add))
                    link(V.memset(f_at[:, 1:2], 0.0))
                    unchain()
                    dve.sem_inc(f_used, 1)

            dve.wait_ge(w_in, ALL_IN)
            dve.wait_ge(s_setup_pe, 1)
            V.tensor_copy(s_w1T, P[0][:, 0:128])
            V.memset(pass_w[0:32, :], 0.0)
            for g in range(1, 4):
                V.tensor_copy(pass_w[32 * g:32 * g + 32, :], P[0][32 * g:32 * g + 32, 0:128])
            V.memset(offmax[:, :], 0.0)
            dve.drain().then_inc(s_setup_cp, 1)
            dve.wait_ge(s_setup_cp, 2)
            dve.wait_ge(s_setup_pe, 2)
            V.tensor_copy(conv_w[:, :, :], P[3][0:96, 0:384].rearrange("p (a n) -> p a n", a=3))
            dve.sem_inc(s_used, UNITS)
            dve.sem_inc(turn_done, 1)
            dve.drain().then_inc(s_ready, 1)
            with dve.Fori(0, B) as b:
                for t in range(TAPS):
                    ins = V.tensor_scalar(diag[:, t, :], ident[:, :], dw_sb[:, 2, t:t + 1], None, ALU.mult)
                ins.then_inc(diag_ready, 1)
                for m in range(8):
                    dve.wait_ge(xT_copied, b * 8 + m + 1)
                    V.bn_stats(stats[:, m, :], xch[:, 512 * m:512 * m + 512]).then_inc(xT_stated, 1)
                dve.wait_ge(xT_stated, b * 8 + 8)
                hold(dve)
                ch = Chain(dve, dve_a, b, CHAIN_A)
                ch.link(V.bn_aggr(mom[:, 0:2], stats[:, :, :].rearrange("p a c -> p (a c)")))
                V.tensor_copy(mom[:, 2:3], mom[:, 0:1])
                V.scalar_tensor_tensor(mom[:, 3:4], mom[:, 0:1], mom[:, 0:1], mom[:, 1:2], ALU.mult, ALU.add).then_inc(moments, 1)
                dve.wait_ge(groups, b + 1)
                ch.link(V.tensor_copy(mom[:, 4:6], P[7][:, 0:2]))
                ch.link(V.tensor_tensor(mom[:, 6:7], mom[:, 4:5], mom[:, 4:5], ALU.mult))
                ch.link(V.tensor_tensor(mom[:, 6:7], mom[:, 5:6], mom[:, 6:7], ALU.subtract))
                V.tensor_scalar(mom[:, 6:7], mom[:, 6:7], 1e-5, None, ALU.add).then_inc(gvar_ready, 1)
                dve.wait_ge(gstd_ready, b + 1)
                ch.link(V.tensor_scalar(mom[:, 8:9], mom[:, 4:5], -1.0, None, ALU.mult))
                V.tensor_tensor(mom[:, 7:8], mom[:, 8:9], mom[:, 6:7], ALU.mult).then_inc(norm, 1)
                V.tensor_scalar(wn_sb[:, :], wq_sb[:, :], mom[:, 6:7], None, ALU.mult).then_inc(wnorm, 1)
                dve.wait_ge(biasmm, b + 1)
                V.tensor_tensor(bn_sb[:, :], P[6][:, 0:3], bq_sb[:, :], ALU.add).then_inc(bias_ok, 1)
                for c, (dst, pitch, at) in enumerate(((qpad, RP, RP + 1), (kwide, WP, wide_at(0, 0)))):
                    r3 = raw[c].rearrange("p (y x) -> p y x", x=RP)
                    dve.wait_ge(raw_ready, b * 24 + 8 * c + 8)
                    if c == 1:
                        dve.wait_ge(raw_zero, b * 4 + 4)
                    first = ch.n
                    for t in range(TAPS):
                        ky, kx = divmod(t, 3)
                        for h in range(4):
                            o = view(dst[:, at + 16 * h * pitch:at + 16 * h * pitch + 1], [[pitch, 16], [1, W]])
                            src = r3[:, 16 * h + ky:16 * h + ky + 16, kx:kx + W]
                            if t == 0:
                                ins = V.tensor_scalar(o, src, dw_sb[:, c, 0:1], db_sb[:, c:c + 1], ALU.mult, ALU.add)
                            else:
                                ch.after(first + 4 * (t - 1) + h + 1)
                                ins = V.scalar_tensor_tensor(o, src, dw_sb[:, c, t:t + 1], o, ALU.mult, ALU.add)
                            if t == TAPS - 1 and c == 0:
                                ins.then_inc(q_conv, 1)
                            else:
                                ch.did(ins)
                ch.close()
                dve.drain().then_inc(done_a, 1)
                dve.wait_ge(done_a, b * 5 + 5)
                hold(dve)

                reads = lambda ky, n: view(lg[:, 48 * ky:48 * ky + 1], [[3, PATCHES], [1, 3], [0, n]])
                taps3 = lambda a: a.rearrange("p (a s c) -> p a s c", a=3, c=3)
                spread = lambda a: view(a, [[0, 3], [1, PATCHES], [0, 3]])
                mx, tot, inv = (small[:, n * PATCHES:(n + 1) * PATCHES] for n in range(3))

                def own_blocks(t, q):
                    dve.wait_ge(o_ready, t * PATCHES + 4 * q + 4)
                    if q == 0:
                        dve.wait_ge(a_kept, t * 16 + 16)
                    for g in range(G):
                        r = slice(32 * g, 32 * g + 32)
                        ins = V.tensor_copy(
                            view(aband[r, 16 * q:16 * q + 1], [[PCOLS, 4], [W, ROWS], [1, PCOLS]]),
                            view(P[7][r, 32 * g:32 * g + 1], [[128, 4], [PCOLS, ROWS], [1, PCOLS]]))
                    ins.then_inc(o_copied, 1)

                def dve_body(v, s, o):
                    tb = b * BANDS
                    ch = Chain(dve, dve_b, tb + s, CHAIN_B) if s is not None else None
                    reduced = {}

                    def reduce_columns(u):
                        dve.wait_ge(s_used, (tb + s) * UNITS + u + 1 + UNITS)
                        reduced[u] = ch.did(V.tensor_reduce(
                            rsum[:, 60 * u:60 * u + 60], prod[:, u % 2, :].rearrange("p (n w) -> p n w", w=WC), AX.X, ALU.add))

                    def weights(j):
                        if j:
                            dve.wait_ge(t_ready, (tb + v) * (3 * PATCHES) + 3 * (j - 1))
                        else:
                            dve.wait_ge(gx_ready, tb + v + 1)
                            dve.wait_ge(hyw_ready, tb + v + 2)
                        weigh(V, j).then_inc(a_dve, 1)

                    if v is not None:
                        weights(0)
                    for j in range(PATCHES):
                        if v is not None and j % 2 and j < PATCHES - 1:
                            weights(j + 1)
                        if s is not None and 1 <= j <= UNITS // 2:
                            if j == 1:
                                dve.wait_ge(hx_ready, tb + s + 1)
                            for u in (2 * j - 2, 2 * j - 1):
                                dve.wait_ge(s_mm, (tb + s) * UNITS + u + 1)
                                if u >= 2:
                                    ch.after(reduced[u - 2])
                                V.tensor_tensor(
                                    prod[:, u % 2, :].rearrange("p (k v w) -> p k v w", v=WR, w=WC),
                                    P[u % 3][:, 0:6 * WIN].rearrange("p (k v w) -> p k v w", v=WR, w=WC),
                                    view(hx[:, 36 * u:36 * u + 1], [[WC, 6], [0, WR], [1, WC]]), ALU.mult).then_inc(s_used, 1)
                                if u:
                                    reduce_columns(u - 1)
                        if s is not None and j == 2:
                            dve.wait_ge(mexp, tb + s + 1)
                            ch.link(V.tensor_scalar(msk, msk, 1.0, None, ALU.add))
                            ch.did(V.reciprocal(msk, msk))
                        if v is not None and j % 4 == 0 and j:
                            own_blocks(tb + v, j // 4 - 1)
                        if o is not None and j == OFFSETS_AT + 1:
                            dve.wait_ge(offc_ready, tb + o + 1)
                            dve.wait_ge(off_kept, (tb + o) * 16 + 16)
                            if s is not None:
                                dve.wait_ge(diff_ready, (tb + s) * 2 + 2)
                            hold(dve)
                            V.transpose(offt[:, :], offc).then_inc(offt_ready, 1)
                        if s is not None and j == SOFTMAX_AT:
                            reduce_columns(UNITS - 1)
                            ch.after(reduced[UNITS - 1])
                            dve.wait_ge(hat_ready, tb + s + 1)
                            ch.link(V.tensor_tensor(rsum, rsum, hy, ALU.mult))
                            ch.link(V.tensor_reduce(lg, rsum.rearrange("p (n v) -> p n v", v=WR), AX.X, ALU.add))
                            ch.link(V.tensor_tensor(lg, lg, msk, ALU.mult))
                            ch.link(V.tensor_reduce(mx, view(lg[:, 0:1], [[3, PATCHES], [48, 3], [1, 3]]), AX.XY, ALU.max))
                            V.tensor_tensor(taps3(lg), taps3(lg), spread(mx), ALU.subtract).then_inc(lg_ready, 1)
                        if s is not None and j == SOFTMAX_AT + 1:
                            dve.wait_ge(p_ready, tb + s + 1)
                            ch.link(V.tensor_reduce(tot, view(lg[:, 0:1], [[3, PATCHES], [48, 3], [1, 3]]), AX.XY, ALU.add))
                            ch.link(V.reciprocal(inv, tot))
                            ch.link(V.tensor_tensor(lg, lg, msk, ALU.mult))
                            ch.link(V.tensor_tensor(taps3(lg), taps3(lg), spread(inv), ALU.mult))
                        if o is not None and j == PATCHES - 1:
                            co = Chain(dve, dve_o, tb + o, CHAIN_O)
                            dve.wait_ge(offt_ready, tb + o + 1)
                            offsets = offt[:, :].rearrange("p (s j) -> p s j", j=32)[:, :, 0:18]
                            co.did(V.tensor_reduce(offmax[:, 1:2], offsets, AX.XY, ALU.max))
                            co.link(V.tensor_reduce(offmax[:, 2:3], offsets, AX.XY, ALU.min))
                            co.link(V.scalar_tensor_tensor(offmax[:, 0:1], offmax[:, 2:3], -1.0, offmax[:, 0:1], ALU.mult, ALU.max))
                            co.link(V.tensor_tensor(offmax[:, 0:1], offmax[:, 0:1], offmax[:, 1:2], ALU.max))
                            co.close()
                    if v is not None:
                        own_blocks(tb + v, 3)
                    if s is not None:
                        if v is not None:
                            dve.wait_ge(a_pool, (tb + v) * 8 + 8)
                        for ky in range(3):
                            ins = V.tensor_tensor(
                                view(gx[:, 18 * ky:18 * ky + 1], [[TAPS * WC, PATCHES], [WC, 3], [1, WC]]),
                                view(hx[:, 288 * ky:288 * ky + 1], [[3 * WC, PATCHES], [WC, 3], [1, WC]]),
                                reads(ky, WC), ALU.mult)
                        ins.then_inc(gx_ready, 1)
                        ch.close()

                pipeline(dve, dve_body)
                dve.drain().then_inc(done_b, 1)
                dve.wait_ge(done_b, b * 5 + 5)
                hold(dve)
                V.tensor_scalar(offmax[:, 0:1], offmax[:, 0:1], 2.0, None, ALU.min).then_inc(peak_ready, 1)
                dve.wait_ge(peak_row, b + 1)
                V.tensor_reduce(offmax[0:1, 3:4], P[0][0:1, 0:128], AX.X, ALU.max).then_inc(peak_ok, 1)
                V.memset(offmax[:, 0:1], 0.0)
                dve.wait_ge(peak_ok, b + 1)
                V.tensor_scalar(flag[0:1, 0:1], offmax[0:1, 3:4], ONE_PIXEL, None, ALU.is_gt).then_inc(flag_ready, 1)
                dve.wait_ge(flag_ready, b + 1)
                hold(dve)
                with dve.If(dve.value_load(flag[0:1, 0:1], min_val=0, max_val=1) != 0):
                    general_path(dve)
                dve.drain().then_inc(done_f, 1)
                dve.wait_ge(done_f, b * 5 + 5)
                hold(dve)

                V.memset(state[:, 0:129], 0.0)
                V.memset(view(vone[:, 128:129], [[129, 4], [1, 1]]), 1.0)
                dve.drain()
                with dve.Fori(0, BANDS) as u:
                    t = b * BANDS + u
                    ch = Chain(dve, dve_c, t, CHAIN_C)
                    q4 = lambda a, j: a[:, 128 * j:128 * j + 128]
                    tiles = lambda a: a.rearrange("p (j n) -> p j n", j=4)
                    row = lambda at, n: view(rows[:, at:at + 1], [[0, 4], [1, n]])

                    def layernorm(src, signal):
                        for j in range(4):
                            ch.did(V.bn_stats(lstat[:, 6 * j:6 * j + 6], q4(src, j)))
                        ch.after(ch.n)
                        hold(dve)
                        for j in range(4):
                            ch.did(V.bn_aggr(lmom[:, 2 * j:2 * j + 2], lstat[:, 6 * j:6 * j + 6]))
                        ch.after(ch.n)
                        V.tensor_scalar(lrs[:, 0:4], view(lmom[:, 1:2], [[2, 4]]), 1e-5, None, ALU.add).then_inc(var_ready, 1)
                        dve.wait_ge(std_ready, t * 2 + (1 if signal is ln_ready else 2))
                        for j in range(4):
                            ins = V.tensor_scalar(q4(ln, j), q4(src, j), lmom[:, 2 * j:2 * j + 1], lrs[:, j:j + 1],
                                                  ALU.subtract, ALU.mult)
                        ins.then_inc(signal, 1)

                    dve.wait_ge(xr_in, t * 16 + 16)
                    ch.link(V.tensor_tensor(tiles(x1), tiles(x1), row(0, C), ALU.add))
                    dve.wait_ge(proj_ready, t + 1)
                    ch.link(V.tensor_tensor(x1, x1, P[0][:, :], ALU.add))
                    layernorm(x1, ln_ready)
                    dve.wait_ge(qk_biased, t + 1)
                    V.tensor_scalar(qk_exp, qk_raw, 0.0, None, ALU.min).then_inc(clip_ready, 1)
                    dve.wait_ge(qkv_c, t * 2 + 2)
                    V.tensor_tensor(view(vone[:, 0:1], [[129, 4], [1, C]]), tiles(P[4][:, :]), row(C, C),
                                    ALU.add).then_inc(v_c, 1)
                    dve.wait_ge(exp_ready, t + 1)
                    V.scalar_tensor_tensor(qk, qk_raw, 0.0, qk_exp, ALU.max, ALU.add).then_inc(qk_ready, 1)
                    dve.wait_ge(causal_in, b * 16 + 16)
                    dve.wait_ge(st_ready, t + 1)
                    V.tensor_tensor(tiles(pmask), tiles(P[6][:, :]), view(causal[:, 0:1], [[0, 4], [1, 128]]),
                                    ALU.mult).then_inc(pm_ready, 1)
                    dve.wait_ge(delta_ready, t + 1)
                    part = lambda p, j: P[p + j // 2][:, 256 * (j % 2):256 * (j % 2) + 129]
                    for j in range(4):
                        ins = V.tensor_tensor(state[:, 129 * (j + 1):129 * (j + 2)], state[:, 129 * j:129 * (j + 1)],
                                              part(0, j), ALU.add)
                        if j < 3:
                            ch.link(ins)
                    ins.then_inc(state_ready, 1)
                    dve.wait_ge(num_ready, t + 1)
                    for h in range(2):
                        ch.did(V.tensor_scalar(den[:, 2 * h:2 * h + 2], view(P[2 + h][:, 128:129], [[256, 2]]),
                                               1e-6, None, ALU.add))
                    ch.did(V.tensor_copy(state[:, 0:129], state[:, 516:645]))
                    ch.after(ch.n)
                    ch.link(V.reciprocal(den[:, :], den[:, :]))
                    for j in range(4):
                        ch.did(V.scalar_tensor_tensor(q4(t1, j), part(2, j)[:, 0:C], den[:, j:j + 1], q4(x1, j),
                                                      ALU.mult, ALU.add))
                    ch.after(ch.n)
                    layernorm(t1, ln2_ready)
                    dve.wait_ge(route_ready, t + 1)
                    le = lambda a: a.rearrange("p (j e) -> p j e", e=E)
                    ch.link(V.tensor_tensor(le(rl), le(P[5][:, 0:4 * E]), row(2 * C, E), ALU.add))
                    ch.link(V.tensor_reduce(rsm[:, 0:4], le(rl), AX.X, ALU.max))
                    V.tensor_tensor(le(rl), le(rl), view(rsm[:, 0:1], [[1, 4], [0, E]]), ALU.subtract).then_inc(logit_ready, 1)
                    dve.wait_ge(rexp_ready, t + 1)
                    pair = lambda a: a.rearrange("p (j i k) -> p j i k", j=4, i=E)
                    other, own = view(re_[:, 0:1], [[E, 4], [0, E], [1, E]]), view(re_[:, 0:1], [[E, 4], [1, E], [0, E]])
                    ch.did(V.tensor_tensor(pair(gt), other, own, ALU.is_gt))
                    ch.link(V.tensor_tensor(pair(eq), other, own, ALU.is_equal))
                    ch.link(V.tensor_tensor(pair(eq), pair(eq), view(before[:, 0:1], [[0, 4], [E, E], [1, E]]), ALU.mult))
                    ch.link(V.tensor_tensor(gt, gt, eq, ALU.add))
                    ch.link(V.tensor_reduce(rsel, gt.rearrange("p (n k) -> p n k", k=E), AX.X, ALU.add))
                    ch.link(V.scalar_tensor_tensor(rsel, rsel, 2.0, re_, ALU.is_lt, ALU.mult))
                    ch.link(V.tensor_reduce(rsm[:, 0:4], le(rsel), AX.X, ALU.add))
                    ch.link(V.reciprocal(rsm[:, 4:8], rsm[:, 0:4]))
                    V.tensor_tensor(le(rw), le(rsel), view(rsm[:, 4:5], [[1, 4], [0, E]]), ALU.mult).then_inc(gate_ready, 1)
                    dve.wait_ge(gate_ready, t + 1)
                    dve.wait_ge(bias_c, t + 1)
                    dve.wait_ge(st_out, t * 16 + 16)
                    ch.link(V.tensor_tensor(acc, t1, P[7][:, :], ALU.add))
                    for j in range(4):
                        dve.wait_ge(ex_ready, t * 4 + j + 1)
                        for e in range(E):
                            src = P[2 * (j % 2) + e // 4][:, 128 * (e % 4):128 * (e % 4) + 128]
                            w = rw[:, E * j + e:E * j + e + 1]
                            dst = q4((acc, accb)[e % 2], j)
                            if e == 1:
                                ins = V.tensor_scalar(dst, src, w, None, ALU.mult)
                            else:
                                if e > 1:
                                    ch.after(ch.n - 1)
                                ins = V.scalar_tensor_tensor(dst, src, w, dst, ALU.mult, ALU.add)
                            if e < E - 1:
                                ch.did(ins)
                        ins.then_inc(ex_used, 1)
                    ch.after(ch.n)
                    dve.wait_ge(ex_used, t * 4 + 4)
                    V.tensor_tensor(acc, acc, accb, ALU.add).then_inc(turn_done, 1)
                    ch.close()
                dve.drain().then_inc(done_c, 1)
                dve.wait_ge(done_c, b * 5 + 5)
                hold(dve)


_INS = ["x", "L0_conv_w_qkv", "L0_conv_b_qkv", "L0_conv_w_dw", "L0_conv_b_dw", "L0_conv_pconv_off_w", "L0_conv_w_off",
        "L0_conv_b_off", "L0_conv_pconv_mask_w", "L0_conv_w_mask", "L0_conv_b_mask", "L0_conv_w_proj",
        "L0_conv_b_proj", "L1_attn_W", "L1_attn_b", "L1_ffn_router_w", "L1_ffn_router_b", "L1_ffn_expert_w",
        "L1_ffn_expert_b"]


def _constants():
    import numpy as np
    p = np.arange(128)
    f32 = np.float32
    place_c, place_r = p % PCOLS, (p // PCOLS) % ROWS
    grid = np.concatenate([np.arange(WC)[None, :] - 1 - place_c[:, None],
                           np.arange(WR)[None, :] - 1 - place_r[:, None]], axis=1)
    e = np.arange(E)
    tap, group = np.arange(TAPS)[None, :], p // 32
    dilation = (2 * group + 1)[:, None]
    before = np.broadcast_to((e[None, :] < e[:, None]).reshape(1, E * E), (128, E * E))
    return [("ident", np.eye(128, dtype=f32)),
            ("gavg", ((p[:, None] // 4 == p[None, :] // 4) * 0.25).astype(f32)),
            ("causal", (p[:, None] <= p[None, :]).astype(f32)),
            ("grid", np.ascontiguousarray(grid.astype(f32))),
            ("before", np.ascontiguousarray(before.astype(f32))),
            ("place", np.ascontiguousarray(np.concatenate([
                place_r[:, None] + dilation * (tap // 3 - 1), place_c[:, None] + dilation * (tap % 3 - 1),
                group[:, None]], axis=1).astype(f32)))]


def kernel(**inputs):
    import numpy as _np
    import concourse.bacc as _bacc
    from concourse import mybir as _mybir
    from concourse.bass_utils import run_bass_kernel_spmd as _run

    nc = _bacc.Bacc("TRN2", target_bir_lowering=False, num_devices=1)
    arrays, args = {}, []
    for name, a in [(n, inputs[n]) for n in _INS] + _constants():
        a = _np.ascontiguousarray(a)
        arrays[f"in_{name}_dram"] = a
        args.append(nc.dram_tensor(f"in_{name}_dram", a.shape, _mybir.dt.from_np(a.dtype), kind="ExternalInput").ap())
    args.append(nc.dram_tensor("table_dram", (N * G, 2 * HC), FP32, kind="Internal").ap())
    args.append(nc.dram_tensor("offs_dram", (BANDS * 128, BPX), FP32, kind="Internal").ap())
    args.append(nc.dram_tensor("attn_dram", (128, N), FP32, kind="Internal").ap())
    args.append(nc.dram_tensor("out_0_dram", (B, H, W, C), FP32, kind="ExternalOutput").ap())
    hybrid_kernel(nc, *args)
    r = _run(nc, [arrays], core_ids=[0])
    return r.results[0]["out_0_dram"]
```

```python
import concourse.bass as bass
from concourse import mybir
from contextlib import ExitStack

FP32 = mybir.dt.float32
INT32 = mybir.dt.int32
ALU = mybir.AluOpType
ACT = mybir.ActivationFunctionType
AX = mybir.AxisListType

B, H, W, C = 4, 64, 64, 128
N = H * W
G, HC, TAPS = 4, 32, 9
E = 8
SCALE = HC ** -0.5
TILE = 128
TILES = N // TILE

ROWS, PCOLS = 8, 4
BANDS = H // ROWS
PATCHES = W // PCOLS
PIX = ROWS * PCOLS
WR, WC = ROWS + 2, PCOLS + 2
WIN = WR * WC
KEYS = TAPS * WIN // 5
BPX = ROWS * W

RP = W + 2
RAW = (H + 2) * RP
FAR = 8
WP = W + FAR
WIDE = (H + 2 * FAR) * WP + 16
BAND = WR * WP


CHAIN_A, CHAIN_B, CHAIN_O, CHAIN_C1, CHAIN_C2, CHAIN_P = 59, 34, 4, 20, 30, 15


ONE_PIXEL = 1.0


def view(ap, dims):
    return bass.AP(tensor=ap.tensor, offset=ap.offset, ap=[ap.ap[0]] + dims)


class Chain:

    def __init__(self, eng, sem, turn, per_turn):
        self.eng, self.sem, self.base, self.per_turn, self.n = eng, sem, turn * per_turn, per_turn, 0

    def did(self, ins):
        ins.then_inc(self.sem, 1)
        self.n += 1
        return self.n

    def after(self, n):
        self.eng.wait_ge(self.sem, self.base + n)

    def link(self, ins):
        self.after(self.did(ins))

    def close(self):
        assert self.n == self.per_turn, (self.n, self.per_turn)


def hybrid_kernel(nc, x, w_qkv, b_qkv, w_dw, b_dw, wp_off, w_off, b_off, wp_mask, w_mask, b_mask, w_proj, b_proj,
                  wa, ba, wr, br, we, be, c_ident, c_gavg, c_causal, c_grid, c_before, c_place, table, offs, attn, out):
    ctx = ExitStack()
    with ctx:
        def sb(name, shape, dt=FP32):
            return ctx.enter_context(nc.sbuf_tensor(name, shape, dt))

        def sem(name):
            return ctx.enter_context(nc.semaphore(name))

        ident = sb("ident", [128, 128])
        gavg = sb("gavg", [128, 128])
        grid = sb("grid", [128, WC + WR])
        before = sb("before", [128, E * E])
        place = sb("place", [128, 2 * TAPS + 1])
        wq_sb = sb("wq_sb", [128, 3 * C])
        bq_sb = sb("bq_sb", [128, 3])
        bn_sb = sb("bn_sb", [128, 3])
        dw_sb = sb("dw_sb", [128, 3, TAPS])
        db_sb = sb("db_sb", [128, 3])
        conv_w = sb("conv_w", [96, 3, 128])
        pass_w = sb("pass_w", [128, 128])
        ob_sb = sb("ob_sb", [128, 1])
        wproj_sb = sb("wproj_sb", [128, C])
        rows = sb("rows", [128, 2 * C + E])
        wa_sb = sb("wa_sb", [128, 3 * C])
        ba_sb = sb("ba_sb", [128, 2])
        wr_sb = sb("wr_sb", [128, E])
        we_sb = sb("we_sb", [128, E * C])
        be_sb = sb("be_sb", [E, C])
        big = sb("big", [128, 2 * N])
        xtok, xch = big[:, 0:N], big[:, N:2 * N]
        qpad = sb("qpad", [128, RAW])
        kwide = sb("kwide", [128, WIDE])
        vwide = sb("vwide", [128, WIDE])
        kband = sb("kband", [128, TAPS * BAND])
        vwin = sb("vwin", [128, (W + 2) * TAPS * WR])
        vband = sb("vband", [128, TAPS * BAND])
        diag = vband[:, 0:TAPS * 128].rearrange("p (t n) -> p t n", t=TAPS)
        wn_sb = vband[:, TAPS * 128:TAPS * 128 + 3 * C]
        taps_of = xtok[:, 0:2048].rearrange("p (a y x) -> p a y x", a=2, x=W)
        raw = [kband[:, 0:RAW], vwin[:, 0:RAW], vband[:, TAPS * 128 + 3 * C:TAPS * 128 + 3 * C + RAW]]
        qstack = sb("qstack", [96, WR * RP])
        offt = sb("offt", [128, BPX])
        HN = PATCHES * TAPS
        parts, at = {}, 0
        for name, n in (("hx", HN * WC), ("hy", HN * WR), ("rsum", HN * WR), ("hyw", HN * WR), ("gx", HN * WC),
                        ("prod", 2 * 6 * WIN), ("aband", BPX), ("offc", BPX), ("msk", HN), ("lg", HN),
                        ("small", 3 * PATCHES)):
            parts[name] = big[:, at:at + n]
            at += n
        assert at <= 2 * N
        hx, hy, rsum = parts["hx"], parts["hy"], parts["rsum"]
        hyw, gx = parts["hyw"], parts["gx"]
        prod = parts["prod"].rearrange("p (a n) -> p a n", a=2)
        aband, offc, msk, lg, small = (parts[n] for n in ("aband", "offc", "msk", "lg", "small"))
        qbd = sb("qbd", [128, PATCHES * 128])
        attbuf = sb("attbuf", [128, 2 * TAPS * WIN])
        att = attbuf[:, :].rearrange("p (a n) -> p a n", a=2)
        keysT = sb("keysT", [128, 2, 10 * 128])
        half = sb("half", [128, 4])
        offmax = sb("offmax", [128, 1 + BANDS])
        stats, mom = keysT[:, 0, 0:48].rearrange("p (m s) -> p m s", s=6), keysT[:, 0, 48:60]
        cbuf = [kwide[:, 0:5760], vwide[:, 0:5760]]
        x1, ln, lnT = cbuf[0][:, 0:512], cbuf[0][:, 512:1024], cbuf[0][:, 1024:1536]
        qk_raw, qk_exp, qk = cbuf[0][:, 1536:2560], cbuf[0][:, 2560:3584], cbuf[0][:, 3584:4608]
        ktok, pmask = cbuf[0][:, 4608:5120], cbuf[0][:, 5120:5632]
        vone, state = cbuf[1][:, 0:516], cbuf[1][:, 516:516 + 645]
        t1, acc, accb = cbuf[1][:, 1280:1792], cbuf[1][:, 1792:2304], cbuf[1][:, 2304:2816]
        wT = cbuf[1][0:E, 3328:3840]
        lstat, lmom, lrs = ([cbuf[1][:, at + 60 * i:at + 60 * i + n] for i in range(2)]
                            for at, n in ((3840, 24), (3864, 8), (3872, 8)))
        lneg = cbuf[1][:, 3880:3884]
        den = cbuf[1][:, 3960:3964]
        rsm = cbuf[1][:, 3964:3972]
        rl, re_, rsel, rw = (cbuf[1][:, 3972 + 32 * i:4004 + 32 * i] for i in range(4))
        gt, eq = cbuf[1][:, 4100:4356], cbuf[1][:, 4356:4612]
        xin, ln2, ln2T = (xtok[:, 512 * i:512 * i + 512] for i in range(3))
        late_ex = xtok[:, 1536:3584]
        ao = cbuf[1][:, 2816:3328]
        causal = cbuf[0][:, 5632:5760]

        f_corner, f_part, f_sample = kband[:, 0:2304], kband[:, 2304:4608], kband[:, 4608:5184]
        f_off, f_q, f_qT = vband[:, 0:512], vband[:, 512:544], vband[:, 544:576]
        f_in, f_out = vband[:, 576:704], vband[:, 704:832]
        f_o, f_oT = vband[:, 832:864], vband[:, 864:896]
        f_pos, f_low, f_frac, f_tmp = (vband[:, 900 + 18 * n:918 + 18 * n] for n in range(4))
        f_edge, f_wt = vband[:, 1000:1036], vband[:, 1040:1076]
        f_int, f_idx = vband[:, 1080:1098].bitcast(INT32), vband[:, 1100:1136].bitcast(INT32)
        f_flat, f_cw = vband[:, 1140:1176], vband[:, 1180:1216]
        f_mask, f_lg, f_s = vband[:, 1220:1229], vband[:, 1230:1239], vband[:, 1240:1244]
        f_at = vband[:, 1250:1252]
        flag = sb("flag", [1, 2], INT32)

        P = [ctx.enter_context(nc.psum_tensor(f"P{i}", [128, 512], FP32)) for i in range(8)]

        s_hold = sem("s_hold")
        w_in = sem("w_in")
        s_zero, s_setup_pe, s_setup_cp, s_ready = sem("s_zero"), sem("s_setup_pe"), sem("s_setup_cp"), sem("s_ready")
        done_a, done_b, done_c = sem("done_a"), sem("done_b"), sem("done_c")
        x_in = [sem(f"x_in{j}") for j in range(4)]
        xT_ready, xT_copied, xT_stated = sem("xT_ready"), sem("xT_copied"), sem("xT_stated")
        moments, groups, norm, wnorm, biasmm, bias_ok = (sem(n) for n in
            ("moments", "groups", "norm", "wnorm", "biasmm", "bias_ok"))
        raw_zero, qkv_ready, raw_ready = sem("raw_zero"), sem("qkv_ready"), sem("raw_ready")
        conv_ready, conv_copied = sem("conv_ready"), sem("conv_copied")
        tap_ready, tap_added = sem("tap_ready"), sem("tap_added")
        diag_ready = sem("diag_ready")
        gvar_ready, gstd_ready, var_ready, std_ready = (
            sem("gvar_ready"), sem("gstd_ready"), [sem(f"var_ready{i}") for i in range(2)],
            [sem(f"std_ready{i}") for i in range(2)])
        pow_ready = sem("pow_ready")
        dve_o = sem("dve_o")
        dve_a, dve_b, dve_c1, dve_c2, pool_c = sem("dve_a"), sem("dve_b"), sem("dve_c1"), sem("dve_c2"), sem("pool_c")
        q_in, k_in, v_in = sem("q_in"), [sem(f"k_in{ky}") for ky in range(3)], sem("v_in")
        v_packed = sem("v_packed")
        off_mm, offc_ready, offt_ready, diff_ready, hat_ready = (sem(n) for n in
            ("off_mm", "offc_ready", "offt_ready", "diff_ready", "hat_ready"))
        absd, mexp, qbd_ready = sem("absd"), sem("mexp"), sem("qbd_ready")
        s_mm, s_used = sem("s_mm"), sem("s_used")
        lg_ready, p_ready, gx_ready, a_dve, a_pool = (sem(n) for n in ("lg_ready", "p_ready", "gx_ready", "a_dve", "a_pool"))
        t_ready, t_copied, o_ready, o_copied = sem("t_ready"), sem("t_copied"), sem("o_ready"), sem("o_copied")
        xr_in, causal_in, ao_in, st_out = sem("xr_in"), sem("causal_in"), sem("ao_in"), sem("st_out")
        a_kept, hyw_ready, hx_ready = sem("a_kept"), sem("hyw_ready"), sem("hx_ready")
        peak_ok = sem("peak_ok")
        off_kept, peak_ready, peak_row, flag_ready, done_f = (sem(n) for n in
            ("off_kept", "peak_ready", "peak_row", "flag_ready", "done_f"))
        (f_chain, f_turned, f_stored, f_table, f_off_in, f_mexp, f_masked, f_ready, f_gather, f_gathered, f_lgr, f_exp,
         f_used) = (sem(n) for n in ("f_chain f_turned f_stored f_table f_off_in f_mexp f_masked f_ready f_gather "
                                     "f_gathered f_lgr f_exp f_used").split())
        xr_used, acc_ready, turn_done = sem("xr_used"), sem("acc_ready"), sem("turn_done")
        ex_scaled = sem("ex_scaled")
        (proj_ready, ln_ready, lnT_ready, lnT_copied, qkv_c, qk_biased, clip_ready, exp_ready, qk_ready, v_c, kt_ready,
         kt_copied, st_ready, pm_ready, delta_ready, state_ready, num_ready, ln2_ready, ln2T_ready, ln2T_copied,
         route_ready, logit_ready, rexp_ready, gate_ready, gateT_ready, gateT_copied, bias_c, ex_ready, ex_used) = (
            sem(n) for n in ("proj_ready ln_ready lnT_ready lnT_copied qkv_c qk_biased clip_ready exp_ready qk_ready "
                             "v_c kt_ready kt_copied st_ready pm_ready delta_ready state_ready num_ready ln2_ready "
                             "ln2T_ready ln2T_copied route_ready logit_ready rexp_ready gate_ready gateT_ready "
                             "gateT_copied bias_c ex_ready ex_used").split())

        block = ctx.enter_context(nc.Block())

        def hold(eng):
            eng.sem_inc(s_hold, 1)

        x_tok = x.rearrange("b h w c -> (b h w) c")
        out_tok = out.rearrange("b h w c -> (b h w) c")
        wide_at = lambda y, xx: (y + FAR) * WP + xx + FAR

        loads = [
            (ident[:, :], c_ident), (gavg[:, :], c_gavg), (grid[:, :], c_grid),
            (before[:, :], c_before), (place[:, :], c_place),
            (wq_sb[:, :], w_qkv), (bq_sb[:, :], b_qkv.rearrange("(c p) -> p c", p=128)),
            (dw_sb[:, :, :], w_dw.rearrange("(c p) i a b -> p c (i a b)", p=128)),
            (db_sb[:, :], b_dw.rearrange("(c p) -> p c", p=128)),
            (wproj_sb[:, :], w_proj), (ba_sb[:, :], ba[0:2 * C].rearrange("(c p) -> p c", p=128)),
            (wr_sb[:, :], wr), (we_sb[:, :].rearrange("p (e c) -> p e c", e=E), we.rearrange("e d c -> d e c")),
            (be_sb[:, :], be),
        ]
        s_wpo = kband[0:32, 0:G * 32 * TAPS].rearrange("o (g i t) -> o g i t", g=G, t=TAPS)
        s_wpm = kband[0:32, 1152:1152 + 288].rearrange("o (i t) -> o i t", t=TAPS)
        s_w1 = kband[:, 1536:1664]
        s_wa = kband[:, 1664:2048].rearrange("p (c i) -> p c i", c=3)
        s_row = kband[0:1, 2048:2048 + 2 * C + E]
        s_one = kband[0:1, 2432:2560]
        s_w1T = kband[:, 2560:2688]
        loads += [(s_wpo, wp_off.rearrange("g o i a b -> o g i (a b)")),
                  (s_wpm, wp_mask.rearrange("o i a b -> o i (a b)")),
                  (s_wa, wa.rearrange("(c p) i -> p c i", p=128)),
                  (s_row[:, 0:C], b_proj.rearrange("(a n) -> a n", a=1)),
                  (s_row[:, C:2 * C], ba[2 * C:3 * C].rearrange("(a n) -> a n", a=1)),
                  (s_row[:, 2 * C:], br.rearrange("(a n) -> a n", a=1))]
        late = []
        for g in range(G):
            late += [(s_w1[32 * g:32 * g + 18, :], w_off[g]), (s_w1[32 * g + 18:32 * g + 27, :], w_mask),
                     (ob_sb[32 * g:32 * g + 18, :], b_off[g].rearrange("(n a) -> n a", a=1)),
                     (ob_sb[32 * g + 18:32 * g + 27, :], b_mask.rearrange("(n a) -> n a", a=1))]
        UNITS = 24
        OFFSETS_AT, SOFTMAX_AT = 5, 13
        PE_STRIPS = 6
        DVE_STRIPS = [[(0, 16), (16, 16), (32, 16), (48, 16)], [(0, 22), (22, 22)]]
        SUM_STRIPS = [(1, 44, 10), (1, 54, 10), (2, 48, 16)]
        COPY_AFTER = (4, 10, 15, 20, 24, 26)
        SUMS = len(SUM_STRIPS) * (TAPS - 1)
        BAND_IN = 16 * 3 * G
        ALL_IN = 16 * (len(loads) + len(late))

        def pipeline(eng, body):
            body(None, None, 0)
            body(None, 0, 1)
            with eng.Fori(0, BANDS - 2) as i:
                body(i, i + 1, i + 2)
            body(BANDS - 2, BANDS - 1, None)
            body(BANDS - 1, None, None)

        def two_stages(eng, body):
            body(0, None)
            with eng.Fori(0, BANDS - 1) as i:
                body(i + 1, i)
            body(None, BANDS - 1)

        def offsets_at(v, s):
            return OFFSETS_AT if v is not None or s is None else 11

        def weigh(eng, s):
            return eng.tensor_tensor(
                view(att[:, s % 2, 0:1], [[TAPS * WR, WC], [WR, TAPS], [1, WR]]),
                view(gx[:, s * TAPS * WC:s * TAPS * WC + 1], [[1, WC], [WC, TAPS], [0, WR]]),
                view(hyw[:, s * TAPS * WR:s * TAPS * WR + 1], [[0, WC], [WR, TAPS], [1, WR]]), ALU.mult)

        def strip(c, y, rows):
            return view((kwide, vwide)[c - 1][:, wide_at(y, 0):wide_at(y, 0) + 1], [[WP, rows], [1, W]])

        def shifted(eng, i, ky, wide, dst, load):
            for g in range(G):
                d = 2 * g + 1
                start = wide_at(-1 + d * (ky - 1), -1 - d)
                eng.dma_start(dst[32 * g:32 * g + 32, :].rearrange("p (c n) -> p c n", c=3),
                              view(wide[32 * g:32 * g + 32, bass.ds(i * (ROWS * WP) + start, 1)],
                                   [[d, 3], [1, BAND]])).then_inc(load, 16)

        @block.sync
        def _(sp):
            sp.sem_inc(st_out, 16)
            sp.sem_inc(off_kept, 16)
            sp.sem_inc(a_kept, 16)
            for dst, src in loads:
                sp.dma_start(dst, src, allow_slow_non_contiguous=True).then_inc(w_in, 16)
            sp.wait_ge(s_zero, 1)
            for dst, src in late:
                sp.dma_start(dst, src, allow_slow_non_contiguous=True).then_inc(w_in, 16)
            sp.wait_ge(s_ready, 1)
            with sp.Fori(0, B) as b:
                for j in range(4):
                    src = x_tok[bass.ds(b * N + j * N // 4, N // 4), :].rearrange("(t p) c -> p t c", p=128)
                    dst = xtok[:, j * 1024:(j + 1) * 1024].rearrange("p (t c) -> p t c", c=C)
                    sp.dma_start(dst, src).then_inc(x_in[j], 16)
                sp.sem_inc(done_a, 1)
                sp.wait_ge(done_a, b * 5 + 5)
                hold(sp)
                def sp_body(v, s, o):
                    def keys(ky):
                        sp.wait_ge(s_used, t * UNITS + 8 * (ky + 1))
                        hold(sp)
                        shifted(sp, o, ky, kwide, kband[:, 3 * ky * BAND:3 * (ky + 1) * BAND], k_in[ky])

                    if o is not None:
                        t = b * BANDS + o
                        sp.wait_ge(off_mm, t + 1)
                        hold(sp)
                        for kx in range(3):
                            sp.dma_start(qstack[32 * kx:32 * kx + 32, 0:WR * RP - 2],
                                         qpad[0:32, bass.ds(o * (ROWS * RP) + kx, WR * RP - 2)]).then_inc(q_in, 16)
                        keys(0)
                        sp.wait_ge(offt_ready, t + 1)
                        hold(sp)
                        sp.dma_start(offs[bass.ds(o * 128, 128), :], offt[:, :]).then_inc(off_kept, 16)
                        keys(1)
                        keys(2)
                        sp.wait_ge(v_packed, t * 8 + 1)
                        hold(sp)
                        for ky in range(3):
                            shifted(sp, o, ky, vwide, vband[:, 3 * ky * BAND:3 * (ky + 1) * BAND], v_in)
                    if v is not None:
                        t = b * BANDS + v
                        sp.wait_ge(o_copied, t * 4 + 4)
                        hold(sp)
                        sp.dma_start(attn[:, bass.ds(v * BPX, BPX)], aband).then_inc(a_kept, 16)

                pipeline(sp, sp_body)
                sp.wait_ge(a_kept, b * (16 * BANDS) + 16 * BANDS + 16)
                hold(sp)
                sp.wait_ge(off_kept, b * (16 * BANDS) + 16 * BANDS + 16)
                hold(sp)
                sp.sem_inc(done_b, 1)
                sp.wait_ge(done_b, b * 5 + 5)
                hold(sp)
                sp.sem_inc(done_f, 1)
                sp.wait_ge(done_f, b * 5 + 5)
                hold(sp)
                sp.dma_start(causal, c_causal).then_inc(causal_in, 16)

                def load(u):
                    t = b * BANDS + u
                    sp.wait_ge(proj_ready, t + 1)
                    sp.wait_ge(xr_used, t + 1)
                    hold(sp)
                    sp.dma_start(ao, attn[:, bass.ds(u * 512, 512)]).then_inc(ao_in, 16)
                    src = x_tok[bass.ds(b * N + u * 512, 512), :].rearrange("(t p) c -> p t c", p=128)
                    sp.dma_start(xin.rearrange("p (t c) -> p t c", c=C), src).then_inc(xr_in, 16)

                def store(u):
                    sp.wait_ge(turn_done, b * BANDS + u + 2)
                    hold(sp)
                    dst = out_tok[bass.ds(b * N + u * 512, 512), :].rearrange("(t p) c -> p t c", p=128)
                    sp.dma_start(dst, acc.rearrange("p (t c) -> p t c", c=C)).then_inc(st_out, 16)

                load(0)
                load(1)
                with sp.Fori(0, BANDS - 2) as u:
                    load(u + 2)
                    store(u)
                store(BANDS - 2)
                store(BANDS - 1)
                sp.wait_ge(st_out, b * (16 * BANDS) + 16 * BANDS + 16)
                hold(sp)
                sp.sem_inc(done_c, 1)
                sp.wait_ge(done_c, b * 5 + 5)
                hold(sp)

        @block.gpsimd
        def _(pool):
            nc.gpsimd.memset(s_w1, 0.0)
            nc.gpsimd.memset(s_one, 1.0)
            nc.gpsimd.memset(half[:, :], -0.5)
            nc.gpsimd.memset(ob_sb[:, :], 0.0)
            nc.gpsimd.memset(qpad[:, :], 0.0)
            nc.gpsimd.memset(kwide[:, :], 0.0)
            nc.gpsimd.memset(vwide[:, :], 0.0)
            nc.gpsimd.memset(qbd[:, :], 0.0)
            pool.drain().then_inc(s_zero, 1)
            pool.sem_inc(v_packed, 1)
            pool.wait_ge(s_ready, 1)
            with pool.Fori(0, B) as b:
                for r in raw:
                    nc.gpsimd.memset(r, 0.0).then_inc(raw_zero, 1)
                pool.wait_ge(gvar_ready, b + 1)
                nc.gpsimd.tensor_tensor(mom[:, 6:7], mom[:, 6:7], half[:, 0:1], ALU.pow).then_inc(gstd_ready, 1)
                for r in (kwide[:, :], vwide[:, :]):
                    nc.gpsimd.memset(r, 0.0).then_inc(raw_zero, 1)
                for n, (c, y, height) in enumerate(SUM_STRIPS):
                    for t in range(TAPS - 1):
                        m = n * (TAPS - 1) + t
                        if m:
                            pool.wait_ge(tap_added, b * SUMS + m)
                        pool.wait_ge(tap_ready, b * SUMS + m + 1)
                        nc.gpsimd.tensor_tensor(strip(c, y, height), strip(c, y, height), taps_of[:, m % 2, 0:height],
                                                ALU.add).then_inc(tap_added, 1)
                pool.drain().then_inc(done_a, 1)
                pool.wait_ge(done_a, b * 5 + 5)
                hold(pool)
                def distances(s, dst, n, at, axis):
                    for ky in range(3):
                        ins = nc.gpsimd.tensor_tensor(
                            view(dst[:, ky * 48 * n:ky * 48 * n + 1], [[3 * n, PATCHES], [n, 3], [1, n]]),
                            view(grid[:, at:at + 1], [[0, PATCHES], [0, 3], [1, n]]),
                            view(offt[:, 6 * ky + axis:6 * ky + axis + 1], [[32, PATCHES], [2, 3], [0, n]]),
                            ALU.subtract)
                    ins.then_inc(diff_ready, 1)

                def pool_body(v, s, o):
                    for m in range(8):
                        if v is not None:
                            t = b * BANDS + v
                            if m == 0:
                                pool.wait_ge(gx_ready, t + 1)
                                pool.wait_ge(hyw_ready, t + 2)
                            else:
                                pool.wait_ge(t_ready, t * (3 * PATCHES) + 6 * m)
                            weigh(nc.gpsimd, 2 * m + 1).then_inc(a_pool, 1)
                        if s is not None and m == 0:
                            pool.wait_ge(offt_ready, b * BANDS + s + 1)
                            if v is not None:
                                pool.wait_ge(gx_ready, b * BANDS + s)
                            distances(s, hx, WC, 0, 1)
                            pool.wait_ge(hyw_ready, b * BANDS + s + 1)
                            distances(s, hy, WR, WC, 0)
                        if s is not None and m:
                            pack(s, m - 1)
                    if s is not None:
                        if v is not None:
                            pool.wait_ge(t_ready, (b * BANDS + v) * (3 * PATCHES) + 3 * PATCHES)
                            hold(pool)
                        pack(s, 7)

                def pack(s, c):
                    if c == 0:
                        pool.wait_ge(v_in, (b * BANDS + s) * BAND_IN + BAND_IN)
                        hold(pool)
                    n = 8 if c < 7 else 10
                    nc.gpsimd.tensor_copy(
                        view(vwin[:, 8 * c * TAPS * WR:8 * c * TAPS * WR + 1], [[TAPS * WR, n], [WR, TAPS], [1, WR]]),
                        view(vband[:, 8 * c:8 * c + 1], [[1, n], [BAND, TAPS], [WP, WR]])).then_inc(v_packed, 1)

                pipeline(pool, pool_body)
                pool.drain().then_inc(done_b, 1)
                pool.wait_ge(done_b, b * 5 + 5)
                pool.wait_ge(flag_ready, b + 1)
                hold(pool)
                with pool.If(pool.value_load(flag[0:1, 0:1], min_val=0, max_val=1) != 0):
                    with pool.Fori(0, H) as y:
                        pool.wait_ge(f_turned, 1)
                        pool.sem_clear(f_turned)
                        for g in range(G):
                            dst = table.rearrange("(n g) e -> g n e", g=G)[g, bass.ds(y * W, W), :]
                            pool.dma_start(dst.rearrange("(j p) e -> p j e", p=32),
                                           f_out[32 * g:32 * g + 32, :].rearrange("p (j e) -> p j e", j=2)).then_inc(f_stored, 16)
                        pool.wait_ge(f_stored, 16 * G)
                        pool.dma_reset(range(f_stored.num, f_stored.num + 1))
                        pool.sem_clear(f_stored)
                        pool.sem_inc(f_table, 1)
                    with pool.Fori(0, BANDS) as i:
                        pool.dma_start(f_off, offs[bass.ds(i * 128, 128), :]).then_inc(f_stored, 16)
                        pool.wait_ge(f_stored, 16)
                        pool.dma_reset(range(f_stored.num, f_stored.num + 1))
                        pool.sem_clear(f_stored)
                        pool.sem_inc(f_off_in, 1)
                        with pool.Fori(0, PATCHES):
                            pool.wait_ge(f_ready, 1)
                            pool.sem_clear(f_ready)
                            for k in range(4 * TAPS):
                                pool.indirect_dma_start(
                                    out=f_corner[:, 64 * k:64 * k + 64], out_offset=None, in_=table,
                                    in_offset=bass.IndirectOffsetOnAxis(ap=f_idx[:, k:k + 1], axis=0)).then_inc(f_gather, 16)
                            pool.wait_ge(f_gather, 16 * 4 * TAPS)
                            pool.dma_reset(range(f_gather.num, f_gather.num + 1))
                            pool.sem_clear(f_gather)
                            pool.sem_inc(f_gathered, 1)
                        pool.wait_ge(f_used, 1)
                        pool.sem_clear(f_used)
                        pool.dma_start(attn[:, bass.ds(i * BPX, BPX)], aband).then_inc(f_stored, 16)
                        pool.wait_ge(f_stored, 16)
                        pool.dma_reset(range(f_stored.num, f_stored.num + 1))
                        pool.sem_clear(f_stored)
                pool.drain().then_inc(done_f, 1)
                pool.wait_ge(done_f, b * 5 + 5)
                hold(pool)
                def pool_turn(c1, c2):
                    for k, u in ((1, c2), (0, c1)):
                        if u is not None:
                            pool.wait_ge(var_ready[k], b * BANDS + u + 1)
                            ins = nc.gpsimd.tensor_tensor(lrs[k][:, 0:4], lrs[k][:, 0:4], half[:, :], ALU.pow)
                            if k == 1:
                                ins.then_inc(pow_ready, 1)
                                pool.wait_ge(pow_ready, b * BANDS + u + 1)
                                ins = nc.gpsimd.tensor_tensor(lneg, lneg, lrs[k][:, 0:4], ALU.mult)
                            ins.then_inc(std_ready[k], 1)
                    if c2 is not None:
                        t = b * BANDS + c2
                        ch = Chain(pool, pool_c, t, CHAIN_P)
                        add = lambda out, other: nc.gpsimd.tensor_tensor(out, out, other, ALU.add)
                        for j in range(4):
                            e4 = late_ex[:, 512 * j:512 * j + 512]
                            q = slice(128 * j, 128 * j + 128)
                            pool.wait_ge(ex_scaled, t * 4 + j + 1)
                            ch.link(add(e4[:, 0:256], e4[:, 256:512]))
                            ch.did(add(e4[:, 0:128], e4[:, 128:256]))
                            pool.wait_ge(ex_used, t * 4 + j + 1)
                            ch.did(add(acc[:, q], accb[:, q]))
                            ch.after(ch.n)
                            ins = add(acc[:, q], e4[:, 0:128])
                            if j < 3:
                                ch.did(ins)
                            else:
                                ins.then_inc(turn_done, 1)
                        ch.close()

                two_stages(pool, pool_turn)
                pool.drain().then_inc(done_c, 1)
                pool.wait_ge(done_c, b * 5 + 5)
                hold(pool)

        @block.tensor
        def _(pe):
            mm = nc.tensor.matmul

            pe.wait_ge(w_in, ALL_IN)
            nc.tensor.transpose(P[0][:, 0:128], s_w1, ident[:, :])
            for c in range(3):
                nc.tensor.transpose(P[1][:, 128 * c:128 * c + 128], s_wa[:, c, :], ident[:, :])
            mm(P[2][:, 0:2 * C + E], s_one, s_row, start=True, stop=True)
            pe.drain().then_inc(s_setup_pe, 1)
            pe.wait_ge(s_setup_cp, 2)
            for t in range(TAPS):
                ky, kx = divmod(t, 3)
                for g in range(G):
                    o = P[3][32 * kx:32 * kx + 32, ky * 128 + 32 * g:ky * 128 + 32 * g + 32]
                    mm(o[:, 0:18], s_wpo[:, g, :, t], s_w1T[0:32, 32 * g:32 * g + 18], start=True, stop=True)
                    mm(o[:, 18:32], s_wpm[:, :, t], s_w1T[0:32, 32 * g + 18:32 * g + 32], start=True, stop=True)
            pe.drain().then_inc(s_setup_pe, 1)
            pe.sem_inc(off_mm, 1)
            pe.sem_inc(proj_ready, 1)
            pe.wait_ge(s_ready, 1)

            with pe.Fori(0, B) as b:
                for m in range(8):
                    if m % 2 == 0:
                        pe.wait_ge(x_in[m // 2], b * 16 + 16)
                    if m >= 2:
                        pe.wait_ge(xT_copied, b * 8 + m - 1)
                    for j in range(4):
                        ins = nc.tensor.transpose(P[m % 2][:, 128 * j:128 * j + 128],
                                                  xtok[:, (4 * m + j) * C:(4 * m + j + 1) * C], ident[:, :])
                    ins.then_inc(xT_ready, 1)
                pe.wait_ge(moments, b + 1)
                mm(P[7][:, 0:2], gavg[:, :], mom[:, 2:4], start=True, stop=True).then_inc(groups, 1)
                pe.wait_ge(norm, b + 1)
                for c in range(3):
                    ins = mm(P[6][:, c:c + 1], wq_sb[:, c * C:c * C + C], mom[:, 7:8], start=True, stop=True)
                ins.then_inc(biasmm, 1)
                pe.wait_ge(wnorm, b + 1)
                pe.wait_ge(xT_copied, b * 8 + 8)
                for c in range(3):
                    for n in range(8):
                        k = c * 8 + n
                        if k >= 2:
                            pe.wait_ge(raw_ready, b * 24 + k - 1)
                        mm(P[2 + k % 2][:, :], wn_sb[:, c * C:c * C + C], xch[:, 512 * n:512 * n + 512],
                           start=True, stop=True).then_inc(qkv_ready, 1)
                r3 = raw[2].rearrange("p (y x) -> p y x", x=RP)
                pe.wait_ge(diag_ready, b + 1)
                pe.wait_ge(raw_ready, b * 24 + 24)
                for n in range(PE_STRIPS):
                    if n >= 2:
                        pe.wait_ge(conv_copied, b * PE_STRIPS + n - 1)
                    for t in range(TAPS):
                        ky, kx = divmod(t, 3)
                        ins = mm(P[4 + n % 2][:, :], diag[:, t, :], r3[:, 8 * n + ky:8 * n + ky + 8, kx:kx + W],
                                 start=t == 0, stop=t == TAPS - 1)
                    ins.then_inc(conv_ready, 1)
                pe.drain().then_inc(done_a, 1)
                pe.wait_ge(done_a, b * 5 + 5)
                hold(pe)

                def turn(t, s):
                    if s % 2 == 0:
                        pe.wait_ge(a_dve, t * 8 + s // 2 + 1)
                        pe.wait_ge(v_packed, t * 8 + min(s // 2 + 2, 8) + 1)
                    else:
                        pe.wait_ge(a_pool, t * 8 + s // 2 + 1)
                    jobs = [[("a", k) for k in range(4)], [("v", k) for k in range(4)], [("a", 4), ("v", 4)]]
                    for k, job in enumerate(jobs):
                        if s > 0:
                            pe.wait_ge(t_copied, t * (3 * PATCHES) + 3 * s + k - 1)
                        for c, (what, part) in enumerate(job):
                            if what == "a":
                                src = att[:, s % 2, KEYS * part:KEYS * (part + 1)]
                            else:
                                at = PCOLS * s * TAPS * WR + KEYS * part
                                src = vwin[:, at:at + KEYS]
                            ins = nc.tensor.transpose(P[4 + k][0:KEYS, 128 * c:128 * c + 128], src, ident[:, :])
                        ins.then_inc(t_ready, 1)

                def mix(t, s):
                    pe.wait_ge(t_copied, t * (3 * PATCHES) + 3 * s + 4)
                    if s % 4 == 0 and s:
                        pe.wait_ge(o_copied, t * 4 + s // 4)
                    for pair in range(5):
                        ins = mm(P[7][:, 128 * (s % 4):128 * (s % 4) + 128],
                                 keysT[0:KEYS, s % 2, 128 * (5 + pair):128 * (6 + pair)],
                                 keysT[0:KEYS, s % 2, 128 * pair:128 * pair + 128], start=pair == 0, stop=pair == 4)
                    ins.then_inc(o_ready, 1)

                def score(t, u):
                    ky, pair = divmod(u, 8)
                    if pair == 0:
                        pe.wait_ge(k_in[ky], t * 16 * G + 16 * G)
                    pe.wait_ge(s_used, t * UNITS + u + UNITS - 2)
                    for h in range(2):
                        s = 2 * pair + h
                        keys = view(kband[:, 3 * ky * BAND + PCOLS * s:3 * ky * BAND + PCOLS * s + 1],
                                    [[BAND, 3], [WP, WR], [1, WC]])
                        ins = mm(P[u % 3][:, 3 * WIN * h:3 * WIN * (h + 1)], qbd[:, 128 * s:128 * s + 128], keys,
                                 start=True, stop=True)
                    ins.then_inc(s_mm, 1)

                def pe_body(v, s, o):
                    for j in range(PATCHES):
                        if v is not None:
                            turn(b * BANDS + v, j)
                        if s is not None and j == 1:
                            pe.wait_ge(qbd_ready, (b * BANDS + s) * 4 + 4)
                        if s is not None and 1 <= j <= UNITS // 2:
                            score(b * BANDS + s, 2 * j - 2)
                            score(b * BANDS + s, 2 * j - 1)
                        if v is not None and j:
                            mix(b * BANDS + v, j - 1)
                        if o is not None and j == offsets_at(v, s):
                            pe.wait_ge(q_in, (b * BANDS + o) * 48 + 48)
                            hold(pe)
                            for ky in range(3):
                                mm(P[3][:, :], conv_w[:, ky, :], view(qstack[:, ky * RP:ky * RP + 1],
                                   [[PCOLS, PATCHES], [RP, ROWS], [1, PCOLS]]), start=ky == 0, stop=False)
                            mm(P[3][:, :], pass_w[:, :], view(qpad[:, bass.ds(o * (ROWS * RP) + RP + 1, 1)],
                               [[PCOLS, PATCHES], [RP, ROWS], [1, PCOLS]]), start=False, stop=True).then_inc(off_mm, 1)
                    if v is not None:
                        mix(b * BANDS + v, PATCHES - 1)

                pipeline(pe, pe_body)
                pe.drain().then_inc(done_b, 1)
                pe.wait_ge(done_b, b * 5 + 5)
                hold(pe)
                pe.wait_ge(peak_ready, b + 1)
                mm(P[0][0:1, 0:128], offmax[:, 0:1], ident[:, :], start=True, stop=True).then_inc(peak_row, 1)
                pe.drain().then_inc(done_f, 1)
                pe.wait_ge(done_f, b * 5 + 5)
                hold(pe)

                q4 = lambda a, j: a[:, 128 * j:128 * j + 128]
                vj = lambda j: vone[:, 129 * j:129 * j + 129]
                sj = lambda j: state[:, 129 * j:129 * j + 129]

                def turned(dst, src, signal):
                    for j in range(4):
                        ins = nc.tensor.transpose(q4(dst, j), q4(src, j), ident[:, :])
                    ins.then_inc(signal, 1)

                def experts(j):
                    for h in range(2):
                        ins = mm(P[4 + 2 * (j % 2) + h][:, :], q4(ln2T, j), we_sb[:, 512 * h:512 * h + 512],
                                 start=True, stop=True)
                    ins.then_inc(ex_ready, 1)

                def pe_turn(c1, c2):
                    one, two = c1 is not None, c2 is not None
                    turn1 = b * BANDS + c1 if one else None
                    turn2 = b * BANDS + c2 if two else None
                    if one:
                        pe.wait_ge(ao_in, turn1 * 16 + 16)
                        for j in range(4):
                            ins = mm(q4(P[0], j), q4(ao, j), wproj_sb[:, :], start=True, stop=True)
                        ins.then_inc(proj_ready, 1)
                    if two:
                        pe.wait_ge(ln2_ready, turn2 + 1)
                        turned(P[6], ln2, ln2T_ready)
                    if one:
                        pe.wait_ge(ln_ready, turn1 + 1)
                        turned(P[1], ln, lnT_ready)
                    if two:
                        pe.wait_ge(ln2T_copied, turn2 + 1)
                        for j in range(4):
                            ins = mm(P[7][:, E * j:E * j + E], q4(ln2T, j), wr_sb[:, :], start=True, stop=True)
                        ins.then_inc(route_ready, 1)
                    if one:
                        pe.wait_ge(lnT_copied, turn1 + 1)
                        mm(P[2][:, :], wa_sb[:, 0:C], lnT, start=True, stop=True).then_inc(qkv_c, 1)
                        mm(P[3][:, :], wa_sb[:, C:2 * C], lnT, start=True, stop=True).then_inc(qkv_c, 1)
                        for j in range(4):
                            ins = mm(q4(P[0], j), q4(lnT, j), wa_sb[:, 2 * C:3 * C], start=True, stop=True)
                        ins.then_inc(qkv_c, 1)
                    if two:
                        pe.wait_ge(gate_ready, turn2 + 1)
                        for j in range(4):
                            ins = mm(P[7][0:E, 128 * j:128 * j + 128], rw[:, E * j:E * j + E], ident[:, :],
                                     start=True, stop=True)
                        ins.then_inc(gateT_ready, 1)
                        experts(0)
                    if one:
                        pe.wait_ge(qk_ready, turn1 + 1)
                        turned(P[1], qk[:, 512:1024], kt_ready)
                        for j in range(4):
                            ins = mm(q4(P[2], j), q4(qk[:, 512:1024], j), q4(qk[:, 0:512], j), start=True, stop=True)
                        ins.then_inc(st_ready, 1)
                    if two:
                        pe.wait_ge(gateT_copied, turn2 + 1)
                        for j in range(4):
                            ins = mm(q4(P[6], j), wT[:, 128 * j:128 * j + 128], be_sb[:, :], start=True, stop=True)
                        ins.then_inc(bias_c, 1)
                    if one:
                        pe.wait_ge(kt_copied, turn1 + 1)
                        pe.wait_ge(v_c, turn1 + 1)
                        for j in range(4):
                            ins = mm(P[j // 2][:, 256 * (j % 2):256 * (j % 2) + 129], q4(ktok, j), vj(j),
                                     start=True, stop=True)
                        ins.then_inc(delta_ready, 1)
                    if two:
                        pe.wait_ge(acc_ready, turn2 + 1)
                        experts(1)
                    if one:
                        pe.wait_ge(pm_ready, turn1 + 1)
                        pe.wait_ge(state_ready, turn1 + 1)
                        for j in range(4):
                            o = P[2 + j // 2][:, 256 * (j % 2):256 * (j % 2) + 129]
                            mm(o, q4(pmask, j), vj(j), start=True, stop=False)
                            ins = mm(o, q4(qk[:, 0:512], j), sj(j), start=False, stop=True)
                        ins.then_inc(num_ready, 1)
                    if two:
                        for j in range(2, 4):
                            pe.wait_ge(ex_used, turn2 * 4 + j - 1)
                            pe.wait_ge(ex_scaled, turn2 * 4 + j - 1)
                            experts(j)

                two_stages(pe, pe_turn)
                pe.drain().then_inc(done_c, 1)
                pe.wait_ge(done_c, b * 5 + 5)
                hold(pe)

        @block.scalar
        def _(act):
            A = nc.scalar.activation
            act.wait_ge(s_setup_pe, 1)
            A(rows[:, :], P[2][:, 0:2 * C + E], ACT.Copy)
            A(wa_sb[:, :], P[1][:, 0:3 * C], ACT.Copy)
            act.wait_ge(s_zero, 1)
            act.drain().then_inc(s_setup_cp, 1)
            act.sem_inc(t_copied, 1)
            act.sem_inc(hyw_ready, 1)
            act.wait_ge(s_ready, 1)
            with act.Fori(0, B) as b:
                for m in range(8):
                    act.wait_ge(xT_ready, b * 8 + m + 1)
                    A(xch[:, 512 * m:512 * m + 512], P[m % 2][:, :], ACT.Copy).then_inc(xT_copied, 1)
                act.wait_ge(bias_ok, b + 1)
                for c in range(3):
                    r3 = raw[c].rearrange("p (y x) -> p y x", x=RP)
                    act.wait_ge(raw_zero, b * 5 + c + 1)
                    for n in range(8):
                        act.wait_ge(qkv_ready, b * 24 + c * 8 + n + 1)
                        A(r3[:, 8 * n + 1:8 * n + 9, 1:W + 1], P[2 + n % 2][:, :].rearrange("p (y x) -> p y x", x=W),
                          ACT.Identity, bias=bn_sb[:, c:c + 1]).then_inc(raw_ready, 1)
                act.wait_ge(raw_zero, b * 5 + 5)
                act.wait_ge(raw_ready, b * 24 + 24)
                taps, strips = [(*part, t) for part in SUM_STRIPS for t in range(TAPS)], 0
                for k, (c, y, height, t) in enumerate(taps):
                    m = k - k // TAPS - 1
                    ky, kx = divmod(t, 3)
                    src = raw[c].rearrange("p (y x) -> p y x", x=RP)[:, y + ky:y + ky + height, kx:kx + W]
                    if t == 0:
                        A(strip(c, y, height), src, ACT.Identity, bias=db_sb[:, c:c + 1], scale=dw_sb[:, c, 0:1])
                    else:
                        if m >= 2:
                            act.wait_ge(tap_added, b * SUMS + m - 1)
                        A(taps_of[:, m % 2, 0:height], src, ACT.Copy, scale=dw_sb[:, c, t:t + 1]).then_inc(tap_ready, 1)
                    if k in COPY_AFTER:
                        act.wait_ge(conv_ready, b * PE_STRIPS + strips + 1)
                        A(strip(2, 8 * strips, 8), P[4 + strips % 2][:, :].rearrange("p (y x) -> p y x", x=W),
                          ACT.Identity, bias=db_sb[:, 2:3]).then_inc(conv_copied, 1)
                        strips += 1
                assert strips == PE_STRIPS
                act.drain().then_inc(done_a, 1)
                act.wait_ge(done_a, b * 5 + 5)
                hold(act)

                def own_blocks(t, q):
                    act.wait_ge(o_ready, t * PATCHES + 4 * q + 4)
                    if q == 0:
                        act.wait_ge(a_kept, t * 16 + 16)
                    for g in range(G):
                        r = slice(32 * g, 32 * g + 32)
                        ins = A(view(aband[r, 16 * q:16 * q + 1], [[PCOLS, 4], [W, ROWS], [1, PCOLS]]),
                                view(P[7][r, 32 * g:32 * g + 1], [[128, 4], [PCOLS, ROWS], [1, PCOLS]]), ACT.Copy)
                    ins.then_inc(o_copied, 1)

                def act_body(v, s, o):
                    def hats(n, dst, ready):
                        t = b * BANDS + s
                        act.wait_ge(diff_ready, t * 2 + n)
                        A(dst, dst, ACT.Abs).then_inc(absd, 1)
                        act.wait_ge(absd, t * 2 + n)
                        A(dst, dst, ACT.Relu, bias=1.0, scale=-1.0).then_inc(ready, 1)

                    for j in range(PATCHES):
                        if s is not None and j == PATCHES - 1:
                            t = b * BANDS + s
                            act.wait_ge(hat_ready, t + 1)
                            if v is not None:
                                act.wait_ge(a_dve, t * 8)
                                act.wait_ge(a_pool, t * 8)
                            for ky in range(3):
                                ins = A(view(hyw[:, 30 * ky:30 * ky + 1], [[90, PATCHES], [WR, 3], [1, WR]]),
                                        view(hy[:, 480 * ky:480 * ky + 1], [[30, PATCHES], [WR, 3], [1, WR]]), ACT.Copy)
                            ins.then_inc(hyw_ready, 1)
                        if v is not None:
                            t = b * BANDS + v
                            for k in range(3):
                                act.wait_ge(t_ready, t * (3 * PATCHES) + 3 * j + k + 1)
                                if k == 0 and j >= 2:
                                    act.wait_ge(o_ready, t * PATCHES + j - 1)
                                if k < 2:
                                    A(keysT[0:KEYS, j % 2, 640 * k:640 * k + 512], P[4 + k][0:KEYS, :],
                                      ACT.Copy).then_inc(t_copied, 1)
                                else:
                                    A(view(keysT[0:KEYS, j % 2, 512:513], [[640, 2], [1, 128]]),
                                      P[6][0:KEYS, 0:256].rearrange("p (a n) -> p a n", a=2), ACT.Copy).then_inc(t_copied, 1)
                        if s is not None and j == 0:
                            hats(1, hx, hx_ready)
                        if v is not None and j % 4 == 0 and j:
                            own_blocks(b * BANDS + v, j // 4 - 1)
                        if s is not None and j == 1:
                            act.wait_ge(offt_ready, b * BANDS + s + 1)
                            A(msk.rearrange("p (a s c) -> p a s c", a=3, c=3),
                              view(offt[:, 18:19], [[3, 3], [32, PATCHES], [1, 3]]), ACT.Exp, scale=-1.0).then_inc(mexp, 1)
                        if o is not None and j == offsets_at(v, s):
                            act.wait_ge(off_mm, b * BANDS + o + 2)
                            A(offc, P[3][:, :], ACT.Identity, bias=ob_sb[:, 0:1]).then_inc(offc_ready, 1)
                        if s is not None and j == OFFSETS_AT + 2:
                            hats(2, hy, hat_ready)
                        if s is not None and j == SOFTMAX_AT + 1:
                            act.wait_ge(lg_ready, b * BANDS + s + 1)
                            A(lg, lg, ACT.Exp).then_inc(p_ready, 1)
                        if o is not None and j == SOFTMAX_AT:
                            t = b * BANDS + o
                            if s is not None:
                                act.wait_ge(s_mm, t * UNITS)
                                hold(act)
                            for g in range(G):
                                q = slice(32 * g, 32 * g + 32)
                                A(view(qbd[q, 32 * g:32 * g + 1], [[128, PATCHES], [PCOLS, ROWS], [1, PCOLS]]),
                                  view(qpad[q, bass.ds(o * (ROWS * RP) + RP + 1, 1)],
                                       [[PCOLS, PATCHES], [RP, ROWS], [1, PCOLS]]),
                                  ACT.Copy, scale=SCALE).then_inc(qbd_ready, 1)
                    if v is not None:
                        own_blocks(b * BANDS + v, 3)

                pipeline(act, act_body)
                act.drain().then_inc(done_b, 1)
                act.wait_ge(done_b, b * 5 + 5)
                act.wait_ge(flag_ready, b + 1)
                hold(act)
                with act.If(act.value_load(flag[0:1, 0:1], min_val=0, max_val=1) != 0):
                    with act.Fori(0, BANDS):
                        with act.Fori(0, PATCHES):
                            act.wait_ge(f_masked, 1)
                            act.sem_clear(f_masked)
                            A(f_mask, f_mask, ACT.Exp, scale=-1.0).then_inc(f_mexp, 1)
                            act.wait_ge(f_lgr, 1)
                            act.sem_clear(f_lgr)
                            A(f_lg, f_lg, ACT.Exp).then_inc(f_exp, 1)
                act.drain().then_inc(done_f, 1)
                act.wait_ge(done_f, b * 5 + 5)
                hold(act)

                def act_turn(c1, c2):
                    one, two = c1 is not None, c2 is not None
                    n1 = b * BANDS + c1 + 1 if one else None
                    n2 = b * BANDS + c2 + 1 if two else None
                    if two:
                        act.wait_ge(std_ready[1], n2)
                        for j in range(4):
                            q = slice(128 * j, 128 * j + 128)
                            ins = A(ln2[:, q], t1[:, q], ACT.Identity, bias=lneg[:, j:j + 1], scale=lrs[1][:, j:j + 1])
                        ins.then_inc(ln2_ready, 1)
                        act.wait_ge(ln2T_ready, n2)
                        A(ln2T, P[6][:, :], ACT.Copy).then_inc(ln2T_copied, 1)
                    if one:
                        act.wait_ge(lnT_ready, n1)
                        A(lnT, P[1][:, :], ACT.Copy).then_inc(lnT_copied, 1)
                    if two:
                        act.wait_ge(logit_ready, n2)
                        A(re_, rl, ACT.Exp).then_inc(rexp_ready, 1)
                    if one:
                        act.wait_ge(qkv_c, n1 * 3 - 2)
                        A(qk_raw[:, 0:512], P[2][:, :], ACT.Identity, bias=ba_sb[:, 0:1])
                        act.wait_ge(qkv_c, n1 * 3 - 1)
                        A(qk_raw[:, 512:1024], P[3][:, :], ACT.Identity, bias=ba_sb[:, 1:2]).then_inc(qk_biased, 1)
                    if two:
                        act.wait_ge(gateT_ready, n2)
                        A(wT, P[7][0:E, :], ACT.Copy).then_inc(gateT_copied, 1)
                    if one:
                        act.wait_ge(clip_ready, n1)
                        A(qk_exp, qk_exp, ACT.Exp).then_inc(exp_ready, 1)
                    if one:
                        act.wait_ge(kt_ready, n1)
                        A(ktok, P[1][:, :], ACT.Copy).then_inc(kt_copied, 1)
                    if two:
                        act.wait_ge(turn_done, n2)
                        for j in range(4):
                            act.wait_ge(ex_ready, n2 * 4 - 3 + j)
                            for e in range(4, E):
                                ins = A(late_ex[:, 512 * j + 128 * (e - 4):512 * j + 128 * (e - 3)],
                                        P[5 + 2 * (j % 2)][:, 128 * (e - 4):128 * (e - 3)], ACT.Copy,
                                        scale=rw[:, E * j + e:E * j + e + 1])
                            ins.then_inc(ex_scaled, 1)

                two_stages(act, act_turn)
                act.drain().then_inc(done_c, 1)
                act.wait_ge(done_c, b * 5 + 5)
                hold(act)

        @block.vector
        def _(dve):
            V = nc.vector

            def general_path(dve):
                count = [0]

                def link(ins):
                    ins.then_inc(f_chain, 1)
                    count[0] += 1
                    dve.wait_ge(f_chain, count[0])

                def unchain():
                    dve.sem_clear(f_chain)
                    count[0] = 0

                with dve.Fori(0, H) as y:
                    link(V.tensor_copy(f_in[:, 0:64], kwide[:, bass.ds(y * WP + wide_at(0, 0), W)]))
                    link(V.tensor_copy(f_in[:, 64:128], vwide[:, bass.ds(y * WP + wide_at(0, 0), W)]))
                    for n in range(2):
                        for j in range(2):
                            link(V.transpose(f_out[:, 64 * j + 32 * n:64 * j + 32 * n + 32],
                                             f_in[:, 64 * n + 32 * j:64 * n + 32 * j + 32]))
                    unchain()
                    dve.sem_inc(f_turned, 1)
                    dve.wait_ge(f_table, 1)
                    dve.sem_clear(f_table)
                two = lambda a, n: view(a[:, n:n + 1], [[18, 2], [1, TAPS]])
                link(V.memset(f_at, 0.0))
                unchain()
                with dve.Fori(0, BANDS) as i:
                    dve.wait_ge(f_off_in, 1)
                    dve.sem_clear(f_off_in)
                    with dve.Fori(0, PATCHES) as s:
                        link(V.tensor_copy(f_q.rearrange("p (r c) -> p r c", c=PCOLS),
                                           view(qpad[:, bass.ds(i * (ROWS * RP) + s * PCOLS + RP + 1, 1)],
                                                [[RP, ROWS], [1, PCOLS]])))
                        link(V.transpose(f_qT, f_q))
                        link(V.tensor_scalar(f_qT, f_qT, SCALE, None, ALU.mult))
                        link(V.tensor_copy(f_mask, f_off[:, bass.ds(s * 32 + 18, TAPS)]))
                        dve.sem_inc(f_masked, 1)
                        for n in range(2):
                            link(V.tensor_scalar(f_pos[:, TAPS * n:TAPS * n + TAPS], place[:, TAPS * n:TAPS * n + TAPS],
                                                 f_at[:, n:n + 1], None, ALU.add))
                            link(V.tensor_copy(f_tmp[:, TAPS * n:TAPS * n + TAPS],
                                               view(f_off[:, bass.ds(s * 32 + n, 1)], [[2, TAPS]])))
                        link(V.tensor_tensor(f_pos, f_pos, f_tmp, ALU.add))
                        link(V.tensor_scalar(f_pos, f_pos, -3.0, W + 3.0, ALU.max, ALU.min))
                        link(V.tensor_copy(f_int, f_pos))
                        link(V.tensor_copy(f_low, f_int))
                        link(V.tensor_tensor(f_tmp, f_low, f_pos, ALU.is_gt))
                        link(V.tensor_tensor(f_low, f_low, f_tmp, ALU.subtract))
                        link(V.tensor_tensor(f_frac, f_pos, f_low, ALU.subtract))
                        link(V.tensor_scalar(f_wt[:, 0:18], f_frac, -1.0, 1.0, ALU.mult, ALU.add))
                        link(V.tensor_copy(f_wt[:, 18:36], f_frac))
                        link(V.tensor_copy(f_edge[:, 0:18], f_low))
                        link(V.tensor_scalar(f_edge[:, 18:36], f_low, 1.0, None, ALU.add))
                        link(V.scalar_tensor_tensor(f_wt, f_edge, 0.0, f_wt, ALU.is_ge, ALU.mult))
                        link(V.scalar_tensor_tensor(f_wt, f_edge, W - 1.0, f_wt, ALU.is_le, ALU.mult))
                        link(V.tensor_scalar(f_edge, f_edge, 0.0, W - 1.0, ALU.max, ALU.min))
                        link(V.tensor_scalar(two(f_edge, 0), two(f_edge, 0), float(W), None, ALU.mult))
                        corner = lambda a, at: view(a[:, at:at + 1], [[4, TAPS], [1, 2]])
                        for sy in range(2):
                            ys = lambda a: view(a[:, 18 * sy:18 * sy + 1], [[1, TAPS], [0, 2]])
                            xs = lambda a: view(a[:, TAPS:TAPS + 1], [[1, TAPS], [18, 2]])
                            link(V.tensor_tensor(corner(f_cw, 2 * sy), ys(f_wt), xs(f_wt), ALU.mult))
                            link(V.tensor_tensor(corner(f_flat, 2 * sy), ys(f_edge), xs(f_edge), ALU.add))
                        link(V.tensor_scalar(f_flat, f_flat, float(G), place[:, 2 * TAPS:2 * TAPS + 1], ALU.mult, ALU.add))
                        link(V.tensor_copy(f_idx, f_flat))
                        dve.sem_inc(f_ready, 1)
                        dve.wait_ge(f_mexp, 1)
                        dve.sem_clear(f_mexp)
                        link(V.tensor_scalar(f_mask, f_mask, 1.0, None, ALU.add))
                        link(V.reciprocal(f_mask, f_mask))
                        dve.wait_ge(f_gathered, 1)
                        dve.sem_clear(f_gathered)
                        link(V.tensor_tensor(f_part.rearrange("p (k e) -> p k e", e=64),
                                             f_corner.rearrange("p (k e) -> p k e", e=64),
                                             view(f_cw[:, 0:1], [[1, 4 * TAPS], [0, 64]]), ALU.mult))
                        link(V.tensor_reduce(f_sample.rearrange("p (k e) -> p k e", e=64),
                                             view(f_part[:, 0:1], [[256, TAPS], [1, 64], [64, 4]]), AX.X, ALU.add))
                        link(V.tensor_tensor(f_sample.rearrange("p (k e) -> p k e", e=64),
                                             f_sample.rearrange("p (k e) -> p k e", e=64),
                                             view(f_mask[:, 0:1], [[1, TAPS], [0, 64]]), ALU.mult))
                        products = view(f_part[:, 0:1], [[32, TAPS], [1, 32]])
                        link(V.tensor_tensor(products, view(f_sample[:, 0:1], [[64, TAPS], [1, 32]]),
                                             view(f_qT[:, 0:1], [[0, TAPS], [1, 32]]), ALU.mult))
                        link(V.tensor_reduce(f_lg, products, AX.X, ALU.add))
                        link(V.tensor_reduce(f_s[:, 0:1], f_lg, AX.X, ALU.max))
                        link(V.tensor_scalar(f_lg, f_lg, f_s[:, 0:1], None, ALU.subtract))
                        dve.sem_inc(f_lgr, 1)
                        dve.wait_ge(f_exp, 1)
                        dve.sem_clear(f_exp)
                        link(V.tensor_reduce(f_s[:, 1:2], f_lg, AX.X, ALU.add))
                        link(V.reciprocal(f_s[:, 2:3], f_s[:, 1:2]))
                        link(V.tensor_scalar(f_lg, f_lg, f_s[:, 2:3], None, ALU.mult))
                        link(V.tensor_tensor(products, view(f_sample[:, 32:33], [[64, TAPS], [1, 32]]),
                                             view(f_lg[:, 0:1], [[1, TAPS], [0, 32]]), ALU.mult))
                        link(V.tensor_reduce(f_o, view(f_part[:, 0:1], [[1, 32], [32, TAPS]]), AX.X, ALU.add))
                        link(V.transpose(f_oT, f_o))
                        link(V.tensor_copy(view(aband[:, bass.ds(s * PCOLS, 1)], [[W, ROWS], [1, PCOLS]]),
                                           f_oT.rearrange("p (r c) -> p r c", c=PCOLS)))
                        link(V.tensor_scalar(f_at[:, 1:2], f_at[:, 1:2], float(PCOLS), None, ALU.add))
                        unchain()
                    link(V.tensor_scalar(f_at[:, 0:1], f_at[:, 0:1], float(ROWS), None, ALU.add))
                    link(V.memset(f_at[:, 1:2], 0.0))
                    unchain()
                    dve.sem_inc(f_used, 1)

            dve.wait_ge(w_in, ALL_IN)
            dve.wait_ge(s_setup_pe, 1)
            V.tensor_copy(s_w1T, P[0][:, 0:128])
            V.memset(pass_w[0:32, :], 0.0)
            for g in range(1, 4):
                V.tensor_copy(pass_w[32 * g:32 * g + 32, :], P[0][32 * g:32 * g + 32, 0:128])
            V.memset(offmax[:, :], 0.0)
            dve.drain().then_inc(s_setup_cp, 1)
            dve.wait_ge(s_setup_cp, 2)
            dve.wait_ge(s_setup_pe, 2)
            V.tensor_copy(conv_w[:, :, :], P[3][0:96, 0:384].rearrange("p (a n) -> p a n", a=3))
            dve.sem_inc(s_used, UNITS)
            dve.sem_inc(xr_used, 1)
            dve.sem_inc(turn_done, 1)
            dve.drain().then_inc(s_ready, 1)
            with dve.Fori(0, B) as b:
                for t in range(TAPS):
                    ins = V.tensor_scalar(diag[:, t, :], ident[:, :], dw_sb[:, 2, t:t + 1], None, ALU.mult)
                ins.then_inc(diag_ready, 1)
                for m in range(8):
                    dve.wait_ge(xT_copied, b * 8 + m + 1)
                    V.bn_stats(stats[:, m, :], xch[:, 512 * m:512 * m + 512]).then_inc(xT_stated, 1)
                dve.wait_ge(xT_stated, b * 8 + 8)
                hold(dve)
                ch = Chain(dve, dve_a, b, CHAIN_A)
                ch.link(V.bn_aggr(mom[:, 0:2], stats[:, :, :].rearrange("p a c -> p (a c)")))
                V.tensor_copy(mom[:, 2:3], mom[:, 0:1])
                V.scalar_tensor_tensor(mom[:, 3:4], mom[:, 0:1], mom[:, 0:1], mom[:, 1:2], ALU.mult, ALU.add).then_inc(moments, 1)
                dve.wait_ge(groups, b + 1)
                ch.link(V.tensor_copy(mom[:, 4:6], P[7][:, 0:2]))
                ch.link(V.tensor_tensor(mom[:, 6:7], mom[:, 4:5], mom[:, 4:5], ALU.mult))
                ch.link(V.tensor_tensor(mom[:, 6:7], mom[:, 5:6], mom[:, 6:7], ALU.subtract))
                V.tensor_scalar(mom[:, 6:7], mom[:, 6:7], 1e-5, None, ALU.add).then_inc(gvar_ready, 1)
                dve.wait_ge(gstd_ready, b + 1)
                ch.link(V.tensor_scalar(mom[:, 8:9], mom[:, 4:5], -1.0, None, ALU.mult))
                V.tensor_tensor(mom[:, 7:8], mom[:, 8:9], mom[:, 6:7], ALU.mult).then_inc(norm, 1)
                V.tensor_scalar(wn_sb[:, :], wq_sb[:, :], mom[:, 6:7], None, ALU.mult).then_inc(wnorm, 1)
                dve.wait_ge(biasmm, b + 1)
                V.tensor_tensor(bn_sb[:, :], P[6][:, 0:3], bq_sb[:, :], ALU.add).then_inc(bias_ok, 1)
                for c, (dst, pitch, at) in enumerate(((qpad, RP, RP + 1), (kwide, WP, wide_at(0, 0)))):
                    r3 = raw[c].rearrange("p (y x) -> p y x", x=RP)
                    if c == 1:
                        dve.wait_ge(raw_zero, b * 5 + 4)
                    first, strips = ch.n, DVE_STRIPS[c]
                    for t in range(TAPS):
                        ky, kx = divmod(t, 3)
                        for h, (y, n) in enumerate(strips):
                            o = view(dst[:, at + y * pitch:at + y * pitch + 1], [[pitch, n], [1, W]])
                            src = r3[:, y + ky:y + ky + n, kx:kx + W]
                            if t == 0:
                                dve.wait_ge(raw_ready, b * 24 + 8 * c + min(8, -(-(y + n + 1) // 8)))
                                ins = V.tensor_scalar(o, src, dw_sb[:, c, 0:1], db_sb[:, c:c + 1], ALU.mult, ALU.add)
                            else:
                                ch.after(first + len(strips) * (t - 1) + h + 1)
                                ins = V.scalar_tensor_tensor(o, src, dw_sb[:, c, t:t + 1], o, ALU.mult, ALU.add)
                            ch.did(ins)
                ch.close()
                dve.drain().then_inc(done_a, 1)
                dve.wait_ge(done_a, b * 5 + 5)
                hold(dve)

                reads = lambda ky, n: view(lg[:, 48 * ky:48 * ky + 1], [[3, PATCHES], [1, 3], [0, n]])
                taps3 = lambda a: a.rearrange("p (a s c) -> p a s c", a=3, c=3)
                spread = lambda a: view(a, [[0, 3], [1, PATCHES], [0, 3]])
                mx, tot, inv = (small[:, n * PATCHES:(n + 1) * PATCHES] for n in range(3))

                def dve_body(v, s, o):
                    tb = b * BANDS
                    ch = Chain(dve, dve_b, tb + s, CHAIN_B) if s is not None else None
                    reduced = {}

                    def reduce_columns(u):
                        dve.wait_ge(s_used, (tb + s) * UNITS + u + 1 + UNITS)
                        reduced[u] = ch.did(V.tensor_reduce(
                            rsum[:, 60 * u:60 * u + 60], prod[:, u % 2, :].rearrange("p (n w) -> p n w", w=WC), AX.X, ALU.add))

                    def weights(j):
                        if j:
                            dve.wait_ge(t_ready, (tb + v) * (3 * PATCHES) + 3 * (j - 1))
                        else:
                            dve.wait_ge(gx_ready, tb + v + 1)
                            dve.wait_ge(hyw_ready, tb + v + 2)
                        weigh(V, j).then_inc(a_dve, 1)

                    if v is not None:
                        weights(0)
                    for j in range(PATCHES):
                        if v is not None and j % 2 and j < PATCHES - 1:
                            weights(j + 1)
                        if s is not None and 1 <= j <= UNITS // 2:
                            if j == 1:
                                dve.wait_ge(hx_ready, tb + s + 1)
                            for u in (2 * j - 2, 2 * j - 1):
                                dve.wait_ge(s_mm, (tb + s) * UNITS + u + 1)
                                if u >= 2:
                                    ch.after(reduced[u - 2])
                                V.tensor_tensor(
                                    prod[:, u % 2, :].rearrange("p (k v w) -> p k v w", v=WR, w=WC),
                                    P[u % 3][:, 0:6 * WIN].rearrange("p (k v w) -> p k v w", v=WR, w=WC),
                                    view(hx[:, 36 * u:36 * u + 1], [[WC, 6], [0, WR], [1, WC]]), ALU.mult).then_inc(s_used, 1)
                                if u:
                                    reduce_columns(u - 1)
                        if s is not None and j == 2:
                            dve.wait_ge(mexp, tb + s + 1)
                            ch.link(V.tensor_scalar(msk, msk, 1.0, None, ALU.add))
                            ch.did(V.reciprocal(msk, msk))
                        if o is not None and j == offsets_at(v, s) + 1:
                            dve.wait_ge(offc_ready, tb + o + 1)
                            dve.wait_ge(off_kept, (tb + o) * 16 + 16)
                            if s is not None:
                                dve.wait_ge(diff_ready, (tb + s) * 2 + 2)
                            hold(dve)
                            V.transpose(offt[:, :], offc).then_inc(offt_ready, 1)
                        if s is not None and j == SOFTMAX_AT:
                            reduce_columns(UNITS - 1)
                            ch.after(reduced[UNITS - 1])
                            dve.wait_ge(hat_ready, tb + s + 1)
                            ch.link(V.tensor_tensor(rsum, rsum, hy, ALU.mult))
                            ch.link(V.tensor_reduce(lg, rsum.rearrange("p (n v) -> p n v", v=WR), AX.X, ALU.add))
                            ch.link(V.tensor_tensor(lg, lg, msk, ALU.mult))
                            ch.link(V.tensor_reduce(mx, view(lg[:, 0:1], [[3, PATCHES], [48, 3], [1, 3]]), AX.XY, ALU.max))
                            V.tensor_tensor(taps3(lg), taps3(lg), spread(mx), ALU.subtract).then_inc(lg_ready, 1)
                        if s is not None and j == SOFTMAX_AT + 1:
                            dve.wait_ge(p_ready, tb + s + 1)
                            ch.link(V.tensor_reduce(tot, view(lg[:, 0:1], [[3, PATCHES], [48, 3], [1, 3]]), AX.XY, ALU.add))
                            ch.link(V.reciprocal(inv, tot))
                            ch.link(V.tensor_tensor(lg, lg, msk, ALU.mult))
                            ch.link(V.tensor_tensor(taps3(lg), taps3(lg), spread(inv), ALU.mult))
                    if s is not None:
                        if v is not None:
                            dve.wait_ge(a_pool, (tb + v) * 8 + 8)
                        for ky in range(3):
                            ins = V.tensor_tensor(
                                view(gx[:, 18 * ky:18 * ky + 1], [[TAPS * WC, PATCHES], [WC, 3], [1, WC]]),
                                view(hx[:, 288 * ky:288 * ky + 1], [[3 * WC, PATCHES], [WC, 3], [1, WC]]),
                                reads(ky, WC), ALU.mult)
                        ins.then_inc(gx_ready, 1)
                        ch.close()
                    if o is not None:
                        co = Chain(dve, dve_o, tb + o, CHAIN_O)
                        dve.wait_ge(offt_ready, tb + o + 1)
                        offsets = offt[:, :].rearrange("p (s j) -> p s j", j=32)[:, :, 0:18]
                        co.did(V.tensor_reduce(offmax[:, 1:2], offsets, AX.XY, ALU.max))
                        co.link(V.tensor_reduce(offmax[:, 2:3], offsets, AX.XY, ALU.min))
                        co.link(V.scalar_tensor_tensor(offmax[:, 0:1], offmax[:, 2:3], -1.0, offmax[:, 0:1], ALU.mult, ALU.max))
                        co.did(V.tensor_tensor(offmax[:, 0:1], offmax[:, 0:1], offmax[:, 1:2], ALU.max))
                        co.close()

                pipeline(dve, dve_body)
                dve.drain().then_inc(done_b, 1)
                dve.wait_ge(done_b, b * 5 + 5)
                hold(dve)
                V.tensor_scalar(offmax[:, 0:1], offmax[:, 0:1], 2.0, None, ALU.min).then_inc(peak_ready, 1)
                dve.wait_ge(peak_row, b + 1)
                V.tensor_reduce(offmax[0:1, 3:4], P[0][0:1, 0:128], AX.X, ALU.max).then_inc(peak_ok, 1)
                V.memset(offmax[:, 0:1], 0.0)
                dve.wait_ge(peak_ok, b + 1)
                V.tensor_scalar(flag[0:1, 0:1], offmax[0:1, 3:4], ONE_PIXEL, None, ALU.is_gt).then_inc(flag_ready, 1)
                dve.wait_ge(flag_ready, b + 1)
                hold(dve)
                with dve.If(dve.value_load(flag[0:1, 0:1], min_val=0, max_val=1) != 0):
                    general_path(dve)
                dve.drain().then_inc(done_f, 1)
                dve.wait_ge(done_f, b * 5 + 5)
                hold(dve)

                V.memset(state[:, 0:129], 0.0)
                V.memset(view(vone[:, 128:129], [[129, 4], [1, 1]]), 1.0)
                dve.drain()
                q4 = lambda a, j: a[:, 128 * j:128 * j + 128]
                tiles = lambda a: a.rearrange("p (j n) -> p j n", j=4)
                row = lambda at, n: view(rows[:, at:at + 1], [[0, 4], [1, n]])
                le = lambda a: a.rearrange("p (j e) -> p j e", e=E)
                pair = lambda a: a.rearrange("p (j i k) -> p j i k", j=4, i=E)
                part = lambda p, j: P[p + j // 2][:, 256 * (j % 2):256 * (j % 2) + 129]

                def moments_of(k, ch, src):
                    for j in range(4):
                        ch.did(V.bn_stats(lstat[k][:, 6 * j:6 * j + 6], q4(src, j)))
                    ch.after(ch.n)
                    hold(dve)
                    for j in range(4):
                        ch.did(V.bn_aggr(lmom[k][:, 2 * j:2 * j + 2], lstat[k][:, 6 * j:6 * j + 6]))
                    ch.after(ch.n)
                    if k == 1:
                        V.tensor_scalar(lneg, view(lmom[k][:, 0:1], [[2, 4]]), -1.0, None, ALU.mult)
                    V.tensor_scalar(lrs[k][:, 0:4], view(lmom[k][:, 1:2], [[2, 4]]), 1e-5, None, ALU.add).then_inc(var_ready[k], 1)

                def dve_turn(c1, c2):
                    one, two = c1 is not None, c2 is not None
                    if one:
                        u1 = b * BANDS + c1
                        chain1 = Chain(dve, dve_c1, u1, CHAIN_C1)
                    if two:
                        u2 = b * BANDS + c2
                        chain2 = Chain(dve, dve_c2, u2, CHAIN_C2)

                    def weighted(j):
                        dve.wait_ge(ex_ready, u2 * 4 + j + 1)
                        for e in range(4):
                            src = P[4 + 2 * (j % 2)][:, 128 * e:128 * e + 128]
                            w = rw[:, E * j + e:E * j + e + 1]
                            dst = q4((acc, accb)[e % 2], j)
                            if e == 1:
                                ins = V.tensor_scalar(dst, src, w, None, ALU.mult)
                            else:
                                if e > 1:
                                    chain2.after(chain2.n - 1)
                                ins = V.scalar_tensor_tensor(dst, src, w, dst, ALU.mult, ALU.add)
                            if e < 3:
                                chain2.did(ins)
                        ins.then_inc(ex_used, 1)

                    if two:
                        dve.wait_ge(dve_c1, u2 * CHAIN_C1 + CHAIN_C1)
                        moments_of(1, chain2, t1)
                    if one:
                        dve.wait_ge(xr_in, u1 * 16 + 16)
                        V.tensor_tensor(tiles(x1), tiles(xin), row(0, C), ALU.add).then_inc(xr_used, 1)
                        dve.wait_ge(xr_used, u1 + 2)
                        dve.wait_ge(proj_ready, u1 + 2)
                        chain1.link(V.tensor_tensor(x1, x1, P[0][:, :], ALU.add))
                        moments_of(0, chain1, x1)
                        dve.wait_ge(std_ready[0], u1 + 1)
                        for j in range(4):
                            ins = V.tensor_scalar(q4(ln, j), q4(x1, j), lmom[0][:, 2 * j:2 * j + 1], lrs[0][:, j:j + 1],
                                                  ALU.subtract, ALU.mult)
                        ins.then_inc(ln_ready, 1)
                    if two:
                        dve.wait_ge(route_ready, u2 + 1)
                        chain2.link(V.tensor_tensor(le(rl), le(P[7][:, 0:4 * E]), row(2 * C, E), ALU.add))
                        chain2.link(V.tensor_reduce(rsm[:, 0:4], le(rl), AX.X, ALU.max))
                        V.tensor_tensor(le(rl), le(rl), view(rsm[:, 0:1], [[1, 4], [0, E]]), ALU.subtract).then_inc(logit_ready, 1)
                    if two:
                        dve.wait_ge(rexp_ready, u2 + 1)
                        other, own = view(re_[:, 0:1], [[E, 4], [0, E], [1, E]]), view(re_[:, 0:1], [[E, 4], [1, E], [0, E]])
                        chain2.did(V.tensor_tensor(pair(gt), other, own, ALU.is_gt))
                        chain2.link(V.tensor_tensor(pair(eq), other, own, ALU.is_equal))
                        chain2.link(V.tensor_tensor(pair(eq), pair(eq), view(before[:, 0:1], [[0, 4], [E, E], [1, E]]), ALU.mult))
                        chain2.link(V.tensor_tensor(gt, gt, eq, ALU.add))
                        chain2.link(V.tensor_reduce(rsel, gt.rearrange("p (n k) -> p n k", k=E), AX.X, ALU.add))
                        chain2.link(V.scalar_tensor_tensor(rsel, rsel, 2.0, re_, ALU.is_lt, ALU.mult))
                        chain2.link(V.tensor_reduce(rsm[:, 0:4], le(rsel), AX.X, ALU.add))
                        chain2.link(V.reciprocal(rsm[:, 4:8], rsm[:, 0:4]))
                        V.tensor_tensor(le(rw), le(rsel), view(rsm[:, 4:5], [[1, 4], [0, E]]), ALU.mult).then_inc(gate_ready, 1)
                    if one:
                        dve.wait_ge(qk_biased, u1 + 1)
                        V.tensor_scalar(qk_exp, qk_raw, 0.0, None, ALU.min).then_inc(clip_ready, 1)
                        dve.wait_ge(qkv_c, u1 * 3 + 3)
                        V.tensor_tensor(view(vone[:, 0:1], [[129, 4], [1, C]]), tiles(P[0][:, :]), row(C, C),
                                        ALU.add).then_inc(v_c, 1)
                    if one:
                        dve.wait_ge(exp_ready, u1 + 1)
                        V.scalar_tensor_tensor(qk, qk_raw, 0.0, qk_exp, ALU.max, ALU.add).then_inc(qk_ready, 1)
                    if two:
                        dve.wait_ge(gate_ready, u2 + 1)
                        dve.wait_ge(bias_c, u2 + 1)
                        dve.wait_ge(st_out, u2 * 16 + 16)
                        V.tensor_tensor(acc, t1, P[6][:, :], ALU.add).then_inc(acc_ready, 1)
                        dve.wait_ge(acc_ready, u2 + 1)
                        weighted(0)
                    if one:
                        if not two:
                            dve.wait_ge(causal_in, b * 16 + 16)
                        dve.wait_ge(st_ready, u1 + 1)
                        V.tensor_tensor(tiles(pmask), tiles(P[2][:, :]), view(causal[:, 0:1], [[0, 4], [1, 128]]),
                                        ALU.mult).then_inc(pm_ready, 1)
                        dve.wait_ge(delta_ready, u1 + 1)
                        for j in range(4):
                            ins = V.tensor_tensor(state[:, 129 * (j + 1):129 * (j + 2)], state[:, 129 * j:129 * (j + 1)],
                                                  part(0, j), ALU.add)
                            if j < 3:
                                chain1.link(ins)
                        ins.then_inc(state_ready, 1)
                    if two:
                        weighted(1)
                    if one:
                        dve.wait_ge(num_ready, u1 + 1)
                        for h in range(2):
                            chain1.did(V.tensor_scalar(den[:, 2 * h:2 * h + 2], view(P[2 + h][:, 128:129], [[256, 2]]),
                                                       1e-6, None, ALU.add))
                        chain1.did(V.tensor_copy(state[:, 0:129], state[:, 516:645]))
                        chain1.after(chain1.n)
                        chain1.link(V.reciprocal(den[:, :], den[:, :]))
                        for j in range(4):
                            chain1.did(V.scalar_tensor_tensor(q4(t1, j), part(2, j)[:, 0:C], den[:, j:j + 1], q4(x1, j),
                                                              ALU.mult, ALU.add))
                        chain1.close()
                    if two:
                        weighted(2)
                        weighted(3)
                        chain2.close()

                two_stages(dve, dve_turn)
                dve.drain().then_inc(done_c, 1)
                dve.wait_ge(done_c, b * 5 + 5)
                hold(dve)


_INS = ["x", "L0_conv_w_qkv", "L0_conv_b_qkv", "L0_conv_w_dw", "L0_conv_b_dw", "L0_conv_pconv_off_w", "L0_conv_w_off",
        "L0_conv_b_off", "L0_conv_pconv_mask_w", "L0_conv_w_mask", "L0_conv_b_mask", "L0_conv_w_proj",
        "L0_conv_b_proj", "L1_attn_W", "L1_attn_b", "L1_ffn_router_w", "L1_ffn_router_b", "L1_ffn_expert_w",
        "L1_ffn_expert_b"]


def _constants():
    import numpy as np
    p = np.arange(128)
    f32 = np.float32
    place_c, place_r = p % PCOLS, (p // PCOLS) % ROWS
    grid = np.concatenate([np.arange(WC)[None, :] - 1 - place_c[:, None],
                           np.arange(WR)[None, :] - 1 - place_r[:, None]], axis=1)
    e = np.arange(E)
    tap, group = np.arange(TAPS)[None, :], p // 32
    dilation = (2 * group + 1)[:, None]
    before = np.broadcast_to((e[None, :] < e[:, None]).reshape(1, E * E), (128, E * E))
    return [("ident", np.eye(128, dtype=f32)),
            ("gavg", ((p[:, None] // 4 == p[None, :] // 4) * 0.25).astype(f32)),
            ("causal", (p[:, None] <= p[None, :]).astype(f32)),
            ("grid", np.ascontiguousarray(grid.astype(f32))),
            ("before", np.ascontiguousarray(before.astype(f32))),
            ("place", np.ascontiguousarray(np.concatenate([
                place_r[:, None] + dilation * (tap // 3 - 1), place_c[:, None] + dilation * (tap % 3 - 1),
                group[:, None]], axis=1).astype(f32)))]


def kernel(**inputs):
    import numpy as _np
    import concourse.bacc as _bacc
    from concourse import mybir as _mybir
    from concourse.bass_utils import run_bass_kernel_spmd as _run

    nc = _bacc.Bacc("TRN2", target_bir_lowering=False, num_devices=1)
    arrays, args = {}, []
    for name, a in [(n, inputs[n]) for n in _INS] + _constants():
        a = _np.ascontiguousarray(a)
        arrays[f"in_{name}_dram"] = a
        args.append(nc.dram_tensor(f"in_{name}_dram", a.shape, _mybir.dt.from_np(a.dtype), kind="ExternalInput").ap())
    args.append(nc.dram_tensor("table_dram", (N * G, 2 * HC), FP32, kind="Internal").ap())
    args.append(nc.dram_tensor("offs_dram", (BANDS * 128, BPX), FP32, kind="Internal").ap())
    args.append(nc.dram_tensor("attn_dram", (128, N), FP32, kind="Internal").ap())
    args.append(nc.dram_tensor("out_0_dram", (B, H, W, C), FP32, kind="ExternalOutput").ap())
    hybrid_kernel(nc, *args)
    r = _run(nc, [arrays], core_ids=[0])
    return r.results[0]["out_0_dram"]
```
